# Optimizing a Trainium2 kernel written in Bass

```python
import numpy as np
import jax
import jax.numpy as jnp

def _softmax(x, axis=-1):
    return jax.nn.softmax(x, axis=axis)

def _gelu(x):
    return jax.nn.gelu(x, approximate=True)

def _silu(x):
    return jax.nn.silu(x)

def _sigmoid(x):
    return jax.nn.sigmoid(x)

def _layernorm(x, axis=-1, eps=1e-05):
    m = jnp.mean(x, axis=axis, keepdims=True)
    v = jnp.var(x, axis=axis, keepdims=True)
    return (x - m) / jnp.sqrt(v + eps)

def _scatter_add(tgt, idx, src, axis=0):
    return tgt.at[idx].add(src)

def _segment_sum(src, seg, n):
    return jax.ops.segment_sum(src, seg, n)
kernel_name = 'mk_metaformer_d1_conv_nhwc256_r4_1f0901'

def setup_inputs(seed: int=0):
    np.random.seed(seed)
    _w = jnp.asarray

    def _rec_inputs():
        import jax
        import jax.numpy as jnp
        _gk = jax.random.key(seed)
        x = -0.0003929 + 0.9999 * jax.random.normal(jax.random.fold_in(_gk, 1), (1, 128, 32, 64), jnp.float32)
        return x
    x = _rec_inputs()

    def _L0_conv_setup():
        import jax, jax.numpy as jnp
        import numpy as np
        E = 64
        C = 32
        B, NP, NC = (1, 128, 32)
        EPS = 1e-05

        def _ln(x, w, b):
            mu = jnp.mean(x, axis=-1, keepdims=True)
            var = jnp.var(x, axis=-1, keepdims=True)
            return (x - mu) * jax.lax.rsqrt(var + EPS) * w + b

        def _lin(x, W, b):
            return jnp.einsum('...i,oi->...o', x, W) + b
        key = jax.random.key(seed)
        ks = jax.random.split(key, 16)
        s = lambda fan_in: 1.0 / np.sqrt(fan_in)
        inp = {'z': jax.random.normal(ks[0], (B, NP, NC, E), jnp.float32), 'protein_pair': jax.random.normal(ks[1], (B, NP, NP, E), jnp.float32), 'compound_pair': jax.random.normal(ks[2], (B, NC, NC, E), jnp.float32), 'z_mask': jnp.ones((B, NP, NC, 1), jnp.float32), 'ln_w': jnp.ones((E,), jnp.float32), 'ln_b': jnp.zeros((E,), jnp.float32), 'lnc_w': jnp.ones((C,), jnp.float32), 'lnc_b': jnp.zeros((C,), jnp.float32), 'g1_w': jax.random.uniform(ks[3], (C, E), jnp.float32, -s(E), s(E)), 'g1_b': jnp.zeros((C,), jnp.float32), 'g2_w': jax.random.uniform(ks[4], (C, E), jnp.float32, -s(E), s(E)), 'g2_b': jnp.zeros((C,), jnp.float32), 'l1_w': jax.random.uniform(ks[5], (C, E), jnp.float32, -s(E), s(E)), 'l1_b': jnp.zeros((C,), jnp.float32), 'l2_w': jax.random.uniform(ks[6], (C, E), jnp.float32, -s(E), s(E)), 'l2_b': jnp.zeros((C,), jnp.float32), 'eg_w': jax.random.uniform(ks[7], (E, E), jnp.float32, -s(E), s(E)), 'eg_b': jnp.zeros((E,), jnp.float32), 'las_w': jax.random.uniform(ks[8], (E, C), jnp.float32, -s(C), s(C)), 'las_b': jnp.zeros((E,), jnp.float32)}
        return inp
    _L0_conv_all = _L0_conv_setup()
    _L0_conv_in = {k: v for k, v in _L0_conv_all.items() if k in ('protein_pair', 'compound_pair', 'z_mask', 'ln_w', 'ln_b', 'lnc_w', 'lnc_b', 'g1_w', 'g1_b', 'g2_w', 'g2_b', 'l1_w', 'l1_b', 'l2_w', 'l2_b', 'eg_w', 'eg_b', 'las_w', 'las_b')}
    del _L0_conv_all

    def _L0_ffn_setup():
        import jax, jax.numpy as jnp
        import numpy as np
        B, N, D = (16, 1024, 64)
        NUM_EXPERTS, TOP_K, HEADS = (4, 2, 4)
        N_EDGES = 262144
        LN_EPS = 1e-05

        def _layernorm(x, g, b):
            mu = x.mean(-1, keepdims=True)
            var = ((x - mu) ** 2).mean(-1, keepdims=True)
            return (x - mu) * jax.lax.rsqrt(var + LN_EPS) * g + b

        def _forward(x, edge_index, W_gat, att_src, att_dst, b_gat, ln_gamma, ln_beta, W1, b1, W2, b2):
            Bc, Nc, Dc = x.shape
            M = Bc * Nc
            x_flat = x.reshape(M, Dc)
            h = (x_flat @ W_gat).reshape(M, HEADS, NUM_EXPERTS)
            loops = jnp.arange(M, dtype=edge_index.dtype)
            src = jnp.concatenate([edge_index[0], loops])
            dst = jnp.concatenate([edge_index[1], loops])
            a_src = (h * att_src).sum(-1)
            a_dst = (h * att_dst).sum(-1)
            e = jax.nn.leaky_relu(a_src[src] + a_dst[dst], negative_slope=0.2)
            e_max = jax.ops.segment_max(e, dst, num_segments=M)
            ee = jnp.exp(e - e_max[dst])
            denom = jax.ops.segment_sum(ee, dst, num_segments=M)
            alpha = ee / (denom[dst] + 1e-16)
            msg = h[src] * alpha[:, :, None]
            agg = jax.ops.segment_sum(msg, dst, num_segments=M).reshape(M, HEADS * NUM_EXPERTS) + b_gat
            scores = _layernorm(agg, ln_gamma, ln_beta).reshape(M, HEADS, NUM_EXPERTS).mean(1)
            scores = scores.reshape(Bc, Nc, NUM_EXPERTS)
            topk_s, topk_i = jax.lax.top_k(scores, TOP_K)
            w = jax.nn.softmax(topk_s, axis=-1)
            out = jnp.zeros_like(x)
            for ei in range(NUM_EXPERTS):
                g = jnp.where(topk_i == ei, w, 0.0).sum(-1)
                hh = jax.nn.gelu(x @ W1[ei] + b1[ei], approximate=False)
                out = out + g[..., None] * (hh @ W2[ei] + b2[ei])
            return out
        key = jax.random.key(seed)
        ks = jax.random.split(key, 8)
        s = 0.05
        return {'x': jax.random.normal(ks[0], (B, N, D), jnp.float32), 'W_gat': jax.random.normal(ks[1], (D, HEADS * NUM_EXPERTS), jnp.float32) * s, 'att_src': jax.random.normal(ks[2], (HEADS, NUM_EXPERTS), jnp.float32) * s, 'att_dst': jax.random.normal(ks[3], (HEADS, NUM_EXPERTS), jnp.float32) * s, 'b_gat': jnp.zeros((HEADS * NUM_EXPERTS,), jnp.float32), 'ln_gamma': jnp.ones((HEADS * NUM_EXPERTS,), jnp.float32), 'ln_beta': jnp.zeros((HEADS * NUM_EXPERTS,), jnp.float32), 'W1': jax.random.normal(ks[4], (NUM_EXPERTS, D, 2 * D), jnp.float32) * s, 'b1': jnp.zeros((NUM_EXPERTS, 2 * D), jnp.float32), 'W2': jax.random.normal(ks[5], (NUM_EXPERTS, 2 * D, D), jnp.float32) * s, 'b2': jnp.zeros((NUM_EXPERTS, D), jnp.float32), 'edge_index': jax.random.randint(ks[6], (2, N_EDGES), 0, B * N, jnp.int32)}
    _L0_ffn_all = _L0_ffn_setup()
    _L0_ffn_in = {k: v for k, v in _L0_ffn_all.items() if k in ('W_gat', 'att_src', 'att_dst', 'b_gat', 'ln_gamma', 'ln_beta', 'W1', 'b1', 'W2', 'b2', 'edge_index')}
    del _L0_ffn_all
    return {'x': x, 'L0_conv_protein_pair': _L0_conv_in['protein_pair'], 'L0_conv_compound_pair': _L0_conv_in['compound_pair'], 'L0_conv_z_mask': _L0_conv_in['z_mask'], 'L0_conv_ln_w': _L0_conv_in['ln_w'], 'L0_conv_ln_b': _L0_conv_in['ln_b'], 'L0_conv_lnc_w': _L0_conv_in['lnc_w'], 'L0_conv_lnc_b': _L0_conv_in['lnc_b'], 'L0_conv_g1_w': _L0_conv_in['g1_w'], 'L0_conv_g1_b': _L0_conv_in['g1_b'], 'L0_conv_g2_w': _L0_conv_in['g2_w'], 'L0_conv_g2_b': _L0_conv_in['g2_b'], 'L0_conv_l1_w': _L0_conv_in['l1_w'], 'L0_conv_l1_b': _L0_conv_in['l1_b'], 'L0_conv_l2_w': _L0_conv_in['l2_w'], 'L0_conv_l2_b': _L0_conv_in['l2_b'], 'L0_conv_eg_w': _L0_conv_in['eg_w'], 'L0_conv_eg_b': _L0_conv_in['eg_b'], 'L0_conv_las_w': _L0_conv_in['las_w'], 'L0_conv_las_b': _L0_conv_in['las_b'], 'L0_ffn_W_gat': _L0_ffn_in['W_gat'], 'L0_ffn_att_src': _L0_ffn_in['att_src'], 'L0_ffn_att_dst': _L0_ffn_in['att_dst'], 'L0_ffn_b_gat': _L0_ffn_in['b_gat'], 'L0_ffn_ln_gamma': _L0_ffn_in['ln_gamma'], 'L0_ffn_ln_beta': _L0_ffn_in['ln_beta'], 'L0_ffn_W1': _L0_ffn_in['W1'], 'L0_ffn_b1': _L0_ffn_in['b1'], 'L0_ffn_W2': _L0_ffn_in['W2'], 'L0_ffn_b2': _L0_ffn_in['b2'], 'L0_ffn_edge_index': _L0_ffn_in['edge_index']}

def reference(x, L0_conv_protein_pair, L0_conv_compound_pair, L0_conv_z_mask, L0_conv_ln_w, L0_conv_ln_b, L0_conv_lnc_w, L0_conv_lnc_b, L0_conv_g1_w, L0_conv_g1_b, L0_conv_g2_w, L0_conv_g2_b, L0_conv_l1_w, L0_conv_l1_b, L0_conv_l2_w, L0_conv_l2_b, L0_conv_eg_w, L0_conv_eg_b, L0_conv_las_w, L0_conv_las_b, L0_ffn_W_gat, L0_ffn_att_src, L0_ffn_att_dst, L0_ffn_b_gat, L0_ffn_ln_gamma, L0_ffn_ln_beta, L0_ffn_W1, L0_ffn_b1, L0_ffn_W2, L0_ffn_b2, L0_ffn_edge_index):
    import jax
    import jax.numpy as jnp

    def _L0_conv_ref(z, protein_pair, compound_pair, z_mask, ln_w, ln_b, lnc_w, lnc_b, g1_w, g1_b, g2_w, g2_b, l1_w, l1_b, l2_w, l2_b, eg_w, eg_b, las_w, las_b):
        import jax, jax.numpy as jnp
        import numpy as np
        E = 64
        C = 32
        B, NP, NC = (1, 128, 32)
        EPS = 1e-05

        def _ln(x, w, b):
            mu = jnp.mean(x, axis=-1, keepdims=True)
            var = jnp.var(x, axis=-1, keepdims=True)
            return (x - mu) * jax.lax.rsqrt(var + EPS) * w + b

        def _lin(x, W, b):
            return jnp.einsum('...i,oi->...o', x, W) + b
        z_norm = _ln(z, ln_w, ln_b)
        protein_norm = _ln(protein_pair, ln_w, ln_b)
        compound_norm = _ln(compound_pair, ln_w, ln_b)
        ab1 = jax.nn.sigmoid(_lin(z_norm, g1_w, g1_b)) * _lin(z_norm, l1_w, l1_b) * z_mask
        ab2 = jax.nn.sigmoid(_lin(z_norm, g2_w, g2_b)) * _lin(z_norm, l2_w, l2_b) * z_mask
        protein_processed = jax.nn.sigmoid(_lin(protein_norm, g2_w, g2_b)) * _lin(protein_norm, l2_w, l2_b)
        compound_processed = jax.nn.sigmoid(_lin(compound_norm, g1_w, g1_b)) * _lin(compound_norm, l1_w, l1_b)
        block1 = jnp.einsum('bikc,bkjc->bijc', protein_processed, ab1)
        block2 = jnp.einsum('bikc,bjkc->bijc', ab2, compound_processed)
        g = jax.nn.sigmoid(_lin(z_norm, eg_w, eg_b))
        normalized = _ln(block1 + block2, lnc_w, lnc_b)
        return g * _lin(normalized, las_w, las_b) * z_mask

    def _L0_ffn_ref(x, W_gat, att_src, att_dst, b_gat, ln_gamma, ln_beta, W1, b1, W2, b2, edge_index):
        import jax, jax.numpy as jnp
        import numpy as np
        B, N, D = (16, 1024, 64)
        NUM_EXPERTS, TOP_K, HEADS = (4, 2, 4)
        N_EDGES = 262144
        LN_EPS = 1e-05

        def _layernorm(x, g, b):
            mu = x.mean(-1, keepdims=True)
            var = ((x - mu) ** 2).mean(-1, keepdims=True)
            return (x - mu) * jax.lax.rsqrt(var + LN_EPS) * g + b

        def _forward(x, edge_index, W_gat, att_src, att_dst, b_gat, ln_gamma, ln_beta, W1, b1, W2, b2):
            Bc, Nc, Dc = x.shape
            M = Bc * Nc
            x_flat = x.reshape(M, Dc)
            h = (x_flat @ W_gat).reshape(M, HEADS, NUM_EXPERTS)
            loops = jnp.arange(M, dtype=edge_index.dtype)
            src = jnp.concatenate([edge_index[0], loops])
            dst = jnp.concatenate([edge_index[1], loops])
            a_src = (h * att_src).sum(-1)
            a_dst = (h * att_dst).sum(-1)
            e = jax.nn.leaky_relu(a_src[src] + a_dst[dst], negative_slope=0.2)
            e_max = jax.ops.segment_max(e, dst, num_segments=M)
            ee = jnp.exp(e - e_max[dst])
            denom = jax.ops.segment_sum(ee, dst, num_segments=M)
            alpha = ee / (denom[dst] + 1e-16)
            msg = h[src] * alpha[:, :, None]
            agg = jax.ops.segment_sum(msg, dst, num_segments=M).reshape(M, HEADS * NUM_EXPERTS) + b_gat
            scores = _layernorm(agg, ln_gamma, ln_beta).reshape(M, HEADS, NUM_EXPERTS).mean(1)
            scores = scores.reshape(Bc, Nc, NUM_EXPERTS)
            topk_s, topk_i = jax.lax.top_k(scores, TOP_K)
            w = jax.nn.softmax(topk_s, axis=-1)
            out = jnp.zeros_like(x)
            for ei in range(NUM_EXPERTS):
                g = jnp.where(topk_i == ei, w, 0.0).sum(-1)
                hh = jax.nn.gelu(x @ W1[ei] + b1[ei], approximate=False)
                out = out + g[..., None] * (hh @ W2[ei] + b2[ei])
            return out
        return _forward(x, edge_index, W_gat, att_src, att_dst, b_gat, ln_gamma, ln_beta, W1, b1, W2, b2)

    def _gn(v, G=32, eps=1e-05):
        B_, H_, W_, C_ = v.shape
        g = v.reshape(B_, H_, W_, G, C_ // G)
        m = jnp.mean(g, axis=(1, 2, 4), keepdims=True)
        s = jnp.var(g, axis=(1, 2, 4), keepdims=True)
        return ((g - m) / jnp.sqrt(s + eps)).reshape(v.shape)

    def _ln_c(v, eps=1e-06):
        m = jnp.mean(v, axis=-1, keepdims=True)
        s = jnp.var(v, axis=-1, keepdims=True)
        return (v - m) / jnp.sqrt(s + eps)

    def _ln_t(v, eps=1e-05):
        m = jnp.mean(v, axis=-1, keepdims=True)
        s = jnp.var(v, axis=-1, keepdims=True)
        return (v - m) / jnp.sqrt(s + eps)

    def _to_tokens(v):
        B_, H_, W_, C_ = v.shape
        return v.reshape(B_, H_ * W_, C_)

    def _from_tokens(t, like):
        return t.reshape(like.shape)
    x = x + _L0_conv_ref(_ln_c(x), L0_conv_protein_pair, L0_conv_compound_pair, L0_conv_z_mask, L0_conv_ln_w, L0_conv_ln_b, L0_conv_lnc_w, L0_conv_lnc_b, L0_conv_g1_w, L0_conv_g1_b, L0_conv_g2_w, L0_conv_g2_b, L0_conv_l1_w, L0_conv_l1_b, L0_conv_l2_w, L0_conv_l2_b, L0_conv_eg_w, L0_conv_eg_b, L0_conv_las_w, L0_conv_las_b)
    t = _to_tokens(x)
    t = t + _L0_ffn_ref(_ln_t(t), L0_ffn_W_gat, L0_ffn_att_src, L0_ffn_att_dst, L0_ffn_b_gat, L0_ffn_ln_gamma, L0_ffn_ln_beta, L0_ffn_W1, L0_ffn_b1, L0_ffn_W2, L0_ffn_b2, L0_ffn_edge_index)
    x = _from_tokens(t, x)
    return x

_drawn_inputs = setup_inputs


def setup_inputs(seed=0):
    import zlib

    import numpy as np

    out = dict(_drawn_inputs(seed))
    spreads = {'L0_conv_ln_w': (1.0, 0.2),
     'L0_conv_ln_b': (0.0, 0.1),
     'L0_conv_lnc_w': (1.0, 0.2),
     'L0_conv_lnc_b': (0.0, 0.347),
     'L0_conv_g1_b': (0.0, 0.497),
     'L0_conv_g2_b': (0.0, 0.527),
     'L0_conv_l1_b': (0.0, 0.1),
     'L0_conv_l2_b': (0.0, 0.1),
     'L0_conv_eg_b': (0.0, 0.5),
     'L0_conv_las_b': (0.0, 0.1),
     'L0_ffn_b_gat': (0.0, 0.1),
     'L0_ffn_ln_gamma': (1.0, 0.6),
     'L0_ffn_ln_beta': (0.0, 0.704),
     'L0_ffn_b1': (0.0, 0.396),
     'L0_ffn_b2': (0.0, 0.1)}
    factors = {'L0_ffn_att_src': 24.218, 'L0_ffn_att_dst': 45.023}
    for name, (base, spread) in spreads.items():
        noise = np.random.default_rng([zlib.crc32(name.encode()), seed]).standard_normal(out[name].shape)
        drawn = base * np.exp(spread * noise) if base else spread * noise
        out[name] = jnp.asarray(drawn.astype(out[name].dtype))
    for name, factor in factors.items():
        out[name] = (out[name] * factor).astype(out[name].dtype)
    return out
```

```python
from contextlib import ExitStack

import concourse.bass as bass
from concourse import mybir
from concourse.alu_op_type import AluOpType as ALU

F32 = mybir.dt.float32
BF16 = mybir.dt.bfloat16
I32 = mybir.dt.int32
ACT = mybir.ActivationFunctionType
AX = mybir.AxisListType

P = 128
NC = 32
E = 64
C = 32
NODES = P * NC
LAST = NODES - 1
HEADS, EXPERTS = 4, 4
HF = HEADS * EXPERTS
ROW = HF + 2 * HEADS
HIDDEN = 2 * E
EDGES = 262144
EC = EDGES // P
OWNED = NC * NODES
NONE = -1.0e30

CH1, TAKE1 = 256, 40
NCH1 = EC // CH1
W1 = NCH1 * TAKE1
SLOTS = 176
CH2, TAKE2 = 128, 40
Y2 = P * 8
NCH2 = Y2 // CH2
W2 = NCH2 * TAKE2
RPG = 2
CH3, TAKE3 = 128, 48
NCH3 = EC // CH3
W3 = NCH3 * TAKE3
OHC = 128
OHB = W3 // OHC

XT, CT = NC, NC * NC // P
TILES = XT + CT + P
GT = 16


class Tally:

    def __init__(self, sem):
        self.sem, self.n = sem, 0

    def up(self):
        self.n += 1
        return 1


def build(nc, x, pp, comp, zmask, ln_w, ln_b, lnc_w, lnc_b, g1_w, g1_b, g2_w, g2_b, l1_w, l1_b, l2_w, l2_b,
          eg_w, eg_b, las_w, las_b, W_gat, att_src, att_dst, b_gat, gamma, beta, W1_, b1, W2_, b2, edges, out,
          force_general=False):
    ctx = ExitStack()

    def sb(name, shape, dt=F32):
        return ctx.enter_context(nc.sbuf_tensor(name, shape, dt))

    def sem(name):
        return ctx.enter_context(nc.semaphore(name))

    node_rows = nc.dram_tensor("node_rows", (NODES, ROW), F32, kind="Internal").ap()
    slot_rows = nc.dram_tensor("slot_rows", (P * SLOTS, ROW), F32, kind="Internal").ap()
    hist_dram = nc.dram_tensor("hist_dram", (64, 64), F32, kind="Internal").ap()
    state_rows = nc.dram_tensor("state_rows", (NODES, ROW), F32, kind="Internal").ap()

    stage_a = sb("stage_a", [P, 16384])
    stage_b = sb("stage_b", [P, EXPERTS * NC * E])
    stage_c = sb("stage_c", [P, 6400])

    def carve(region, dt=F32):
        at = [0]

        def take(*shape):
            n = 1
            for d in shape:
                n *= d
            words = n if dt == F32 or dt == I32 else n // 2
            ap = region[:, at[0]:at[0] + words]
            at[0] += words
            assert at[0] <= region.shape[1]
            if dt != F32:
                ap = ap.bitcast(dt)
            if len(shape) == 1:
                return ap
            names = "abcd"[:len(shape)]
            sizes = {c: d for c, d in zip(names, shape)}
            return ap.rearrange(f"p ({' '.join(names)}) -> p {' '.join(names)}", **sizes)
        return take

    a1 = carve(stage_a)
    tiles = a1(TILES, E)
    ppc = a1(C, P)
    squares_a = a1(GT * E)
    seg = carve(stage_a, BF16)(NC, SLOTS)
    segd = carve(stage_a[:, NC * SLOTS // 2:])(NC, SLOTS)
    onehot = carve(stage_a, BF16)(2, 2, 64, OHC)
    a3 = carve(stage_a)
    esc = a3(HEADS, SLOTS)
    rmax = a3(HEADS, SLOTS)
    carry = a3(HEADS, SLOTS)
    wgt = a3(HEADS, SLOTS)
    srow = a3(SLOTS, ROW)
    a4 = carve(stage_a, I32)
    gen_dst, gen_src = a4(EC), a4(EC)
    gen_keys, gen_plain = (stage_a[:, n * EC:(n + 1) * EC] for n in (2, 3))
    a5 = carve(stage_a[:, 4 * EC:16384])
    same = a5(P)
    earlier = a5(P)
    others = a5(HEADS, P)
    notsame, first_of = a5(P), a5(P)
    src_row, dst_row, old_row, new_row = a5(ROW), a5(ROW), a5(ROW), a5(ROW)
    payload = a5(HEADS + HF)
    escore, emax, expo = a5(HEADS), a5(HEADS), a5(2, HEADS)
    key1, valid1, dst1, rank1, write1 = (a5(1) for _ in range(5))
    gi = carve(stage_a[:, 16384 - 8:16384], I32)(8)

    yscratch = stage_a[:, TILES * E:TILES * E + EC]
    ktmp, plain_src, plain = (stage_b[:, n * EC:(n + 1) * EC] for n in (1, 2, 3))
    b1_ = carve(stage_b)
    sig = b1_(NC, 2 * E)
    ab = b1_(NC, E)
    abT = b1_(8, P)
    nb = b1_(NC, C)
    ab2 = nb.rearrange("p j c -> p (j c)").rearrange("p (c k) -> p c k", k=NC)
    yexp = carve(stage_b)(EXPERTS, NC, E)

    edst, esrc = stage_c[:, 0:EC].bitcast(I32), stage_c[:, EC:2 * EC].bitcast(I32)
    gath = carve(stage_c)(SLOTS, ROW)
    c1_ = carve(stage_c)
    bcast, owned = c1_(2, RPG * SLOTS), c1_(2, RPG * SLOTS)
    coll = c1_(Y2)
    clamped = carve(stage_c[:, SLOTS * ROW:6400])(EC)
    c3_ = carve(stage_c[:, SLOTS * ROW:6400])
    agg_in = c3_(NC, ROW)
    fin = c3_(8, NC, HEADS)

    ident = sb("ident", [P, P])
    digit_id = sb("digit_id", [P, 3, P], BF16)
    ones_col = sb("ones_col", [P, P])
    iota_j = sb("iota_j", [P, NC])
    iota_i = sb("iota_i", [P, NC], I32)
    own_i = sb("own_i", [P, 3], I32)
    own = sb("own", [P, 3])
    eps = sb("eps", [P, 2])
    pbias = sb("pbias", [1, E])
    cbias = sb("cbias", [1, E])
    before = sb("before", [P, EXPERTS, EXPERTS])

    w_nat = sb("w_nat", [P, 2 * E])
    eg_nat = sb("eg_nat", [E, 2 * E])
    las_nat = sb("las_nat", [E, 4 * C])
    affine = sb("affine", [P, 4])
    bias_in = sb("bias_in", [1, 4 * E])
    wT = sb("wT", [P, 3 * E])
    wTs = sb("wTs", [P, 3 * E])
    bdz = sb("bdz", [P, 2, 3 * E])
    bdp = sb("bdp", [P, 2, E])
    bdcp = sb("bdcp", [P, 2, E])
    bdlas = sb("bdlas", [P, 4, E])
    lasT = sb("lasT", [P, E])
    bias1 = sb("bias1", [1, 4 * E])
    wgat2 = sb("wgat2", [P, 2, HF])
    att = sb("att", [P, 2, HF])
    gat_aff = sb("gat_aff", [P, 3, HF])
    w1s = sb("w1s", [P, EXPERTS, HIDDEN])
    b1s = sb("b1s", [HIDDEN, EXPERTS])
    w2s = sb("w2s", [HIDDEN, EXPERTS, E])
    b2s = sb("b2s", [1, EXPERTS, E])
    mask = sb("mask", [P, NC])

    xin = sb("xin", [P, NC, E])
    tsum = sb("tsum", [P, TILES])
    tmean = sb("tmean", [P, TILES])
    tssq = sb("tssq", [P, TILES])
    tstd = sb("tstd", [P, TILES])
    trstd = sb("trstd", [P, TILES])
    xr = sb("xr", [P, 4, XT])
    tT = sb("tT", [P, 2, 4, P])
    psig = sb("psig", [P, 2, 8, C])
    cpk = sb("cpk", [C, NC, C])
    bdc = sb("bdc", [P, 8, 4, NC])
    nstat = sb("nstat", [P, 6, NC])
    xn = sb("xn", [P, NC, E])
    xnT = sb("xnT", [P, NC // 2, P])
    rows = sb("rows", [P, NC, ROW])
    last_row = sb("last_row", [P, ROW])

    work = xn[:, :, :].rearrange("p j e -> p (j e)")
    ccand, cidx = work[:, 0:W3], work[:, W3:2 * W3].bitcast(I32)
    cdigit = ccand.bitcast(I32)
    hi16, lo16 = work[:, 2 * W3:5 * W3 // 2].bitcast(BF16), work[:, W3:3 * W3 // 2].bitcast(BF16)
    cand1 = sb("cand1", [P, W1])
    sent = sb("sent", [P, SLOTS])
    senti = sb("senti", [P, 3, SLOTS], I32)
    digits = sb("digits", [P, 3, SLOTS], BF16)
    cand2 = cand1
    recv = sb("recv", [P, SLOTS])
    local = sb("local", [P, SLOTS])
    locali = senti
    tgt = sb("tgt", [P, SLOTS])
    counts = sb("counts", [P, 5])
    flag = sb("flag", [P, 1], I32)
    cum = sb("cum", [P, NC + 1])
    present = sb("present", [P, NC])
    tailf = sb("tailf", [P, NC])
    taili = sb("taili", [P, NC], I32)
    dslot = sb("dslot", [P, HEADS, SLOTS])
    head = sb("head", [P, SLOTS])
    reset = sb("reset", [P, SLOTS])
    histo = sb("histo", [64, 64])
    nclamp = sb("nclamp", [P, NC])

    hid = sb("hid", [P, 2, 4, P])
    squares = [squares_a, hid[:, :, :, :].rearrange("p b t n -> p (b t n)")]
    hatt = squares_a.rearrange("p (s j f) -> p s j f", s=2, j=NC)

    bank = [ctx.enter_context(nc.psum_tensor(f"bank{n}", [P, 512], F32)) for n in range(8)]

    vec, act_, pe_, pool_ = sem("vec"), sem("act"), sem("pe"), sem("pool")
    x_in, edges_in, comp_in, params_in = sem("x_in"), sem("edges_in"), sem("comp_in"), sem("params_in")
    pp_in = [sem(f"pp_in{n}") for n in range(P // GT)]
    consts = sem("consts")
    weights_turned, weights_copied, bias_made, bias_copied = sem("weights_turned"), sem("weights_copied"), \
        sem("bias_made"), sem("bias_copied")
    diagonals_zero = sem("diagonals_zero")
    summed, centered, squared, sumsq, normed = sem("summed"), sem("centered"), sem("squared"), sem("sumsq"), sem("normed")
    std_x, std_rest, rstd, var2_x, std2_x = sem("std_x"), sem("std_rest"), sem("rstd"), sem("var2_x"), sem("std2_x")
    turned, copied, projected, sigmoided, bank_read = sem("turned"), sem("copied"), sem("projected"), \
        sem("sigmoided"), sem("bank_read")
    scratch_free = sem("scratch_free")
    masked_ab, bdc_ready, blocks_done, nb_centered, nb_squared, nb_sumsq, nb_std, nb_ready = (
        sem(n) for n in ("masked_ab", "bdc_ready", "blocks_done", "nb_centered", "nb_squared", "nb_sumsq", "nb_std",
                         "nb_ready"))
    x1_ready, xn_centered, xn_squared, xn_sumsq, xn_std, xn_ready, gat_done, rows_ready, rows_stored, last_in = (
        sem(n) for n in ("x1_ready", "xn_centered", "xn_squared", "xn_sumsq", "xn_std", "xn_ready", "gat_done",
                         "rows_ready", "rows_stored", "last_in"))
    keys_ready, keys_counted, digits_ready, shown, shown_copied, owned_ready = (
        sem(n) for n in ("keys_ready", "keys_counted", "digits_ready", "shown", "shown_copied", "owned_ready"))
    missing_ready, missing_summed, flag_ready, idx_ready, tails_ready, masks_done = (
        sem(n) for n in ("missing_ready", "missing_summed", "flag_ready", "idx_ready", "tails_ready", "masks_done"))
    gathered, onehots_ready, hist_used, hist_copied, hist_stored, clamped_in = (
        sem(n) for n in ("gathered", "onehots_ready", "hist_used", "hist_copied", "hist_stored", "clamped_in"))
    exps_wanted, exps_done, slots_ready, slots_stored, tails_in = (
        sem(n) for n in ("exps_wanted", "exps_done", "slots_ready", "slots_stored", "tails_in"))
    hidden_done, gelued, y_done, y_copied = sem("hidden_done"), sem("gelued"), sem("y_done"), sem("y_copied")
    fin_wanted, fin_done, out_ready, out_stored = sem("fin_wanted"), sem("fin_done"), sem("out_ready"), sem("out_stored")

    groups = [(0, GT), (GT, GT), (XT, CT)] + [(XT + CT + GT * n, GT) for n in range(P // GT)]

    def v3(ap, inner):
        return ap.rearrange("p (a b) -> p a b", b=inner)

    def wide(ap, n):
        return ap.unsqueeze(2).to_broadcast([ap.shape[0], ap.shape[1], n])

    NX, NCP, NPR, NLAS = NC // 2, NC // 8, P // 8, NC // 8

    loads = [(w_nat[C * n:C * (n + 1), E * d:E * (d + 1)], w[:, :])
             for n, w in enumerate((l1_w, l2_w, g1_w, g2_w)) for d in range(2)]
    loads += [(eg_nat[:, E * d:E * (d + 1)], eg_w[:, :]) for d in range(2)]
    loads += [(las_nat[:, C * d:C * (d + 1)], las_w[:, :]) for d in range(4)]
    loads += [(affine[E * d:E * (d + 1), n:n + 1], w.unsqueeze(1)) for n, w in enumerate((ln_w, ln_b)) for d in range(2)]
    loads += [(affine[C * d:C * (d + 1), n + 2:n + 3], w.unsqueeze(1))
              for n, w in enumerate((lnc_w, lnc_b)) for d in range(4)]
    loads += [(bias_in[:, C * n:C * (n + 1)], w.unsqueeze(0)) for n, w in enumerate((l1_b, l2_b, g1_b, g2_b))]
    loads += [(bias_in[:, 2 * E:3 * E], eg_b.unsqueeze(0)), (bias_in[:, 3 * E:4 * E], las_b.unsqueeze(0))]
    loads += [(mask[:, :], zmask.rearrange("a i j b -> (a i) (j b)"))]
    late_loads = [(wgat2[E * q:E * (q + 1), q, :], W_gat[:, :]) for q in range(2)]
    late_loads += [(att[:, n, :], a.rearrange("h e -> (h e)").partition_broadcast(P)) for n, a in enumerate((att_src, att_dst))]
    late_loads += [(gat_aff[:, n, :], a.partition_broadcast(P)) for n, a in enumerate((b_gat, gamma, beta))]
    late_loads += [(w1s[E * q:E * (q + 1), :, :], W1_.rearrange("e i f -> i e f")) for q in range(2)]
    late_loads += [(w2s[:, :, :], W2_.rearrange("e f o -> f e o")), (b1s[:, :], b1.rearrange("e f -> f e")),
                   (b2s[:, :, :], b2.rearrange("e o -> (e o)").unsqueeze(0).rearrange("a (e o) -> a e o", e=EXPERTS))]
    late_in = sem("late_in")

    gen_blank, gen_state, gen_edges, gen_idx, gen_score, gen_others, gen_exp, gen_exped, gen_payload = (
        sem(f"gen_{n}") for n in ("blank", "state", "edges", "idx", "score", "others", "exp", "exped", "payload"))
    gen_tick = sem("gen_tick")
    gen_in = [sem(f"gen_in{n}") for n in range(3)]
    gen_same, gen_summed, gen_row, gen_written, gen_mask, gen_steps, gen_back, gen_zero = (
        sem(f"gen_{n}") for n in ("same", "summed", "row", "written", "mask", "steps", "back", "zero"))

    SHOWS = P // RPG

    def project_bank(n):
        return bank[2 + n % 4 if n < NX else 2 + n % 2]

    AT_TURN_AB, AT_BLOCKS, AT_SUM, AT_CENTER, AT_SUMSQ, AT_SCALE = 41, 43, 53, 55, 58, 61

    block = ctx.enter_context(nc.Block())

    @block.sync
    def _(sp):
        sp.dma_start(edst, edges[1].rearrange("(p c) -> p c", p=P)).then_inc(edges_in, 16)
        sp.dma_start(esrc, edges[0].rearrange("(p c) -> p c", p=P)).then_inc(edges_in, 16)
        sp.dma_start(xin[:, :, :], x.rearrange("a i j e -> (a i) j e")).then_inc(x_in, 16)
        sp.dma_start(tiles[:, XT:XT + CT, :],
                     comp.rearrange("a j k e -> (a j k) e").rearrange("(t p) e -> p t e", p=P)).then_inc(comp_in, 16)
        for n in range(P // GT):
            sp.dma_start(tiles[:, XT + CT + GT * n:XT + CT + GT * (n + 1), :],
                         pp[0, GT * n:GT * (n + 1), :, :].rearrange("i k e -> k i e")).then_inc(pp_in[n], 16)
        sp.wait_ge(rows_ready, 1)
        sp.dma_start(node_rows.rearrange("(p j) r -> p (j r)", p=P), rows[:, :, :].rearrange("p j r -> p (j r)")) \
            .then_inc(rows_stored, 16)
        sp.wait_ge(rows_stored, 16)
        sp.dma_start(last_row[:, :], node_rows[LAST, :].partition_broadcast(P)).then_inc(last_in, 16)
        sp.wait_ge(hist_copied, 1)
        sp.dma_start(hist_dram[:, :], histo[:, :]).then_inc(hist_stored, 16)
        sp.wait_ge(hist_stored, 16)
        sp.dma_start(nclamp[:, :], hist_dram.rearrange("a (b j) -> (a b) j", j=NC)).then_inc(clamped_in, 16)
        sp.wait_ge(slots_ready, 1)
        sp.dma_start(slot_rows.rearrange("(p l) r -> p (l r)", p=P), srow.rearrange("p l r -> p (l r)")) \
            .then_inc(slots_stored, 16)
        sp.wait_ge(flag_ready, 1)
        with sp.If(sp.value_load(flag[0:1, 0:1], min_val=0, max_val=1) > 0):
            sp.wait_ge(gen_blank, 1)
            sp.wait_ge(slots_stored, 16)
            sp.dma_start(gen_dst, edges[1].rearrange("(p c) -> p c", p=P)).then_inc(gen_edges, 16)
            sp.dma_start(gen_src, edges[0].rearrange("(p c) -> p c", p=P)).then_inc(gen_edges, 16)
            sp.dma_start(state_rows.rearrange("(p j) r -> p (j r)", p=P), agg_in.rearrange("p j r -> p (j r)")) \
                .then_inc(gen_state, 16)
            sp.wait_ge(gen_written, 16 * EC)
            sp.wait_ge(gen_state, 16)
            sp.dma_start(agg_in.rearrange("p j r -> p (j r)"), state_rows.rearrange("(p j) r -> p (j r)", p=P)) \
                .then_inc(gen_back, 16)
        for n in range(2):
            sp.wait_ge(out_ready, n + 1)
            sp.dma_start(out[0, :, 16 * n:16 * n + 16, :], xin[:, 16 * n:16 * n + 16, :]).then_inc(out_stored, 16)
        sp.wait_ge(out_stored, 32)

    @block.gpsimd
    def _(pool):
        g = nc.gpsimd
        t = Tally(pool_)
        g.memset(wgat2[:, :, :], 0.0).then_inc(pool_, t.up())
        pool.wait_ge(pool_, t.n)
        for dst, src in late_loads:
            g.dma_start(dst, src, allow_slow_non_contiguous=True).then_inc(late_in, 16)
        g.memset(ident[:, :], 0.0).then_inc(pool_, t.up())
        g.memset(ones_col[:, :], 1.0).then_inc(pool_, t.up())
        g.memset(eps[:, 0:1], 1e-6).then_inc(pool_, t.up())
        g.memset(eps[:, 1:2], 1e-5).then_inc(pool_, t.up())
        g.iota(iota_i[:, :], [[1, NC]], base=0, channel_multiplier=0).then_inc(pool_, t.up())
        g.iota(own_i[:, 0:1], [[0, 1]], base=1, channel_multiplier=OWNED).then_inc(pool_, t.up())
        g.iota(own_i[:, 1:2], [[0, 1]], base=OWNED, channel_multiplier=OWNED).then_inc(pool_, t.up())
        g.iota(own_i[:, 2:3], [[0, 1]], base=0, channel_multiplier=SLOTS).then_inc(pool_, t.up())
        g.memset(before[:, :, :], 0.0).then_inc(pool_, t.up())
        pool.wait_ge(pool_, t.n)
        g.affine_select(out=ident[:, :], in_=ident[:, :], compare_op=ALU.not_equal, fill=1.0, base=0,
                        pattern=[[-1, P]], channel_multiplier=1).then_inc(pool_, t.up())
        g.tensor_copy(iota_j[:, :], iota_i[:, :]).then_inc(pool_, t.up())
        g.tensor_copy(own[:, :], own_i[:, :]).then_inc(pool_, t.up())
        for e in range(1, EXPERTS):
            g.memset(before[:, e, 0:e], 1.0).then_inc(pool_, t.up())
        pool.wait_ge(pool_, t.n)
        for d in range(3):
            g.tensor_scalar(digit_id[:, d, :], ident[:, :], float(256 ** (2 - d)), None, ALU.mult).then_inc(pool_, t.up())
        pool.wait_ge(pool_, t.n)
        g.memset(cum[:, :], 0.0).then_inc(consts, 1)
        for z in (bdz[:, :, :], bdp[:, :, :], bdcp[:, :, :], bdlas[:, :, :], bdc[:, :, :, :]):
            g.memset(z, 0.0).then_inc(diagonals_zero, 1)
        for n, (a, m) in enumerate(groups):
            pool.wait_ge(summed, n + 1)
            part = tiles[:, a:a + m, :]
            g.tensor_scalar(tmean[:, a:a + m], tsum[:, a:a + m], 1.0 / E, None, ALU.mult).then_inc(pool_, t.up())
            pool.wait_ge(pool_, t.n)
            g.tensor_tensor(part, xin[:, a:a + m, :] if a < XT else part, wide(tmean[:, a:a + m], E), ALU.subtract) \
                .then_inc(centered, 1)
        for n, (a, m) in enumerate(groups):
            pool.wait_ge(rstd, 1 if a < XT else 2)
            pool.wait_ge(squared, n + 1)
            part = tiles[:, a:a + m, :]
            g.tensor_tensor(part, part, wide(trstd[:, a:a + m], E), ALU.mult).then_inc(normed, 1)
        pool.wait_ge(bank_read, NX)
        pool.wait_ge(params_in, 16 * len(loads))
        g.tensor_tensor(ab2, ab[:, :, C:E].rearrange("p k c -> p c k"), mask[:, :].unsqueeze(1).to_broadcast([P, C, NC]),
                        ALU.mult).then_inc(masked_ab, 1)
        g.tensor_tensor(ab[:, :, 0:C], ab[:, :, 0:C], wide(mask[:, :], C), ALU.mult).then_inc(masked_ab, 1)
        g.tensor_tensor(sig[:, :, E:2 * E], sig[:, :, E:2 * E], wide(mask[:, :], E), ALU.mult).then_inc(masked_ab, 1)
        pool.wait_ge(rows_stored, 16)
        pool.wait_ge(idx_ready, 1)
        for l in range(SLOTS):
            g.indirect_dma_start(out=gath[:, l, :], out_offset=None, in_=node_rows[:, :],
                                 in_offset=bass.IndirectOffsetOnAxis(ap=locali[:, 2, l:l + 1], axis=0)) \
                .then_inc(gathered, 16)
        pool.wait_ge(slots_stored, 16)
        pool.wait_ge(tails_ready, 1)
        for j in range(NC):
            g.indirect_dma_start(out=agg_in[:, j, :], out_offset=None, in_=slot_rows[:, :],
                                 in_offset=bass.IndirectOffsetOnAxis(ap=taili[:, j:j + 1], axis=0)) \
                .then_inc(tails_in, 16)
        pool.wait_ge(flag_ready, 1)
        with pool.If(pool.value_load(flag[0:1, 0:1], min_val=0, max_val=1) > 0):
            pool.wait_ge(slots_stored, 16)
            g.memset(earlier, 1.0).then_inc(gen_zero, 1)
            pool.wait_ge(gen_zero, 1)
            g.affine_select(out=earlier, in_=earlier, compare_op=ALU.is_gt, fill=0.0, base=0, pattern=[[-1, P]],
                            channel_multiplier=1).then_inc(gen_mask, 1)
            pool.wait_ge(gen_state, 16)
            with pool.Fori(0, EC) as step:
                pool.wait_ge(gen_idx, step + 1)
                pool.sem_inc(gen_tick)
                for n, (row, table, col) in enumerate(((src_row, node_rows, 1), (dst_row, node_rows, 2),
                                                       (old_row, state_rows, 2))):
                    g.indirect_dma_start(out=row, out_offset=None, in_=table[:, :],
                                         in_offset=bass.IndirectOffsetOnAxis(ap=gi[:, col:col + 1], axis=0)) \
                        .then_inc(gen_in[n], 16)
                pool.wait_ge(gen_row, step + 1)
                pool.sem_inc(gen_tick)
                g.indirect_dma_start(out=state_rows[:, :],
                                     out_offset=bass.IndirectOffsetOnAxis(ap=gi[:, 3:4], axis=0), in_=new_row,
                                     in_offset=None, bounds_check=NODES - 1, oob_is_err=False).then_inc(gen_written, 16)
                pool.wait_ge(gen_written, 16 * step + 16)
                pool.sem_inc(gen_tick)

    @block.scalar
    def _(act):
        a_ = nc.scalar
        t = Tally(act_)
        for dst, src in loads:
            act.dma_start(dst, src, allow_slow_non_contiguous=True).then_inc(params_in, 16)

        def square(n):
            a, m = groups[n]
            act.wait_ge(centered, n + 1)
            if n >= 2:
                act.wait_ge(sumsq, n - 1)
            a_.activation(v3(squares[n % 2][:, 0:m * E], E), tiles[:, a:a + m, :], ACT.Square).then_inc(squared, 1)

        def copy_turned(n, dst):
            act.wait_ge(turned, n + 1)
            a_.activation(dst, v3(bank[n % 2][:, :], P), ACT.Copy).then_inc(copied, 1)

        def copy_tile(n):
            if n >= 2:
                act.wait_ge(projected, 4 * (n - 1) if n - 2 < 4 else (NX + NCP if n - 2 == 4 else NX + NCP + n - 6))
            copy_turned(n, tT[:, n % 2])

        def sigmoid(n):
            act.wait_ge(projected, n + 1)
            ps = project_bank(n)
            if n < NX:
                a_.activation(sig[:, 2 * n:2 * n + 2, :], v3(ps[:, 0:6 * E], 3 * E)[:, :, E:3 * E], ACT.Sigmoid) \
                    .then_inc(sigmoided, 1)
            else:
                if n >= NX + 2:
                    act.wait_ge(bank_read, n - 1)
                p_ = C if n < NX + NCP else P
                a_.activation(psig[0:p_, n % 2], v3(ps[0:p_, :], E)[:, :, C:E], ACT.Sigmoid).then_inc(sigmoided, 1)

        square(0)
        square(1)
        act.wait_ge(keys_ready, 1)
        a_.activation(yscratch, work, ACT.Sign, accum_out=counts[:, 0:1]).then_inc(keys_counted, 1)
        act.wait_ge(scratch_free, 1)
        act.wait_ge(keys_counted, 1)
        a_.activation(yscratch, clamped, ACT.Sign, accum_out=counts[:, 3:4]).then_inc(keys_counted, 1)
        act.wait_ge(consts, 1)
        act.wait_ge(sumsq, 2)
        a_.activation(xr[:, 0], tssq[:, 0:XT], ACT.Sqrt, bias=eps[:, 0:1], scale=1.0 / E).then_inc(std_x, 1)
        act.wait_ge(var2_x, 1)
        a_.activation(xr[:, 3], xr[:, 2], ACT.Sqrt, bias=eps[:, 1:2]).then_inc(std2_x, 1)
        for n in range(2, len(groups)):
            square(n)
        act.wait_ge(sumsq, len(groups))
        a_.activation(tstd[:, XT:TILES], tssq[:, XT:TILES], ACT.Sqrt, bias=eps[:, 1:2], scale=1.0 / E) \
            .then_inc(std_rest, 1)
        act.wait_ge(scratch_free, 1)
        copy_tile(0)
        for n in range(4):
            copy_tile(n + 1)
            for m in range(4):
                sigmoid(4 * n + m)
        copy_tile(5)
        n = 5 + NPR
        for m in range(SHOWS):
            if m % 2 == 0 and m // 2 < NCP + NPR:
                k = m // 2
                sigmoid(NX + k)
                if NCP - 1 <= k < NCP + NPR - 2:
                    copy_tile(k + 3)
            elif m == AT_TURN_AB:
                for b in range(2):
                    copy_turned(n + b, abT[:, 4 * b:4 * b + 4, :])
            elif m == AT_CENTER + 2:
                act.wait_ge(nb_centered, 2)
                a_.activation(squares[0], nb.rearrange("p j c -> p (j c)"), ACT.Square).then_inc(nb_squared, 1)
            elif m == AT_SUMSQ + 2:
                act.wait_ge(nb_sumsq, 1)
                a_.activation(nstat[:, 2], nstat[:, 1], ACT.Sqrt, bias=eps[:, 1:2], scale=1.0 / C).then_inc(nb_std, 1)
            act.wait_ge(shown, m + 1)
            if m >= 2:
                act.wait_ge(owned_ready, m - 1)
            if m == 0:
                act.wait_ge(digits_ready, 1)
            a_.activation(bcast[:, m % 2], bank[4 + m % 2][:, 0:RPG * SLOTS], ACT.Copy).then_inc(shown_copied, 1)
        act.wait_ge(projected, NX + NCP + NPR)
        for b in range(2):
            copy_turned(n + 2 + b, tT[:, b])
        for b in range(2):
            act.wait_ge(xn_centered, 1)
            a_.activation(v3(squares[b], E), xn[:, 16 * b:16 * b + 16, :], ACT.Square).then_inc(xn_squared, 1)
        act.wait_ge(xn_sumsq, 1)
        a_.activation(nstat[:, 2], nstat[:, 1], ACT.Sqrt, bias=eps[:, 1:2], scale=1.0 / E).then_inc(xn_std, 1)
        for b in range(4):
            copy_turned(n + 4 + b, xnT[:, 4 * b:4 * b + 4, :])
        act.wait_ge(late_in, 16 * len(late_loads))
        act.wait_ge(xn_ready, 1)

        def gelu(f):
            act.wait_ge(hidden_done, f + 1)
            if f >= 2:
                act.wait_ge(y_done, f - 1)
            a_.activation(hid[:, f % 2].rearrange("p t n -> p (t n)"), bank[f % 2][:, :], ACT.Gelu,
                          bias=b1s[:, f // 8:f // 8 + 1]).then_inc(gelued, 1)

        def copy_y(f):
            e, q, b = f // 8, f // 4 % 2, f % 4
            act.wait_ge(y_done, f + 1)
            a_.activation(yexp[:, e, 8 * b + q:8 * b + 8:2, :], v3(bank[2 + f % 2][:, 0:4 * E], E), ACT.Copy) \
                .then_inc(y_copied, 1)

        for f in range(32):
            gelu(f)
            if f:
                copy_y(f - 1)
        copy_y(31)
        act.wait_ge(exps_wanted, 1)
        a_.activation(carry, carry, ACT.Exp).then_inc(exps_done, 1)
        a_.activation(wgt, wgt, ACT.Exp).then_inc(exps_done, 1)
        act.wait_ge(flag_ready, 1)
        with act.If(act.value_load(flag[0:1, 0:1], min_val=0, max_val=1) > 0):
            with act.Fori(0, EC) as step:
                act.wait_ge(gen_exp, step + 1)
                a_.activation(expo, expo, ACT.Exp).then_inc(gen_exped, 1)
        act.wait_ge(fin_wanted, 1)
        a_.activation(fin[:, 0:3], fin[:, 0:3], ACT.Exp).then_inc(fin_done, 1)
        act.wait_ge(fin_wanted, 2)
        a_.activation(nstat[:, 2], nstat[:, 1], ACT.Sqrt, bias=eps[:, 1:2], scale=1.0 / HF).then_inc(fin_done, 1)
        act.wait_ge(fin_wanted, 3)
        a_.activation(fin[:, 3], fin[:, 3], ACT.Exp).then_inc(fin_done, 1)

    @block.tensor
    def _(pe):
        p_ = nc.tensor
        t = Tally(pe_)
        pe.wait_ge(consts, 1)
        pe.wait_ge(params_in, 16 * len(loads))
        p_.transpose(bank[6][:, 0:P], w_nat[:, :], ident[:, :])
        p_.transpose(bank[6][:, P:P + E], eg_nat[:, :], ident[0:E, 0:E])
        p_.transpose(bank[6][:, P + E:P + 2 * E], las_nat[:, :], ident[0:E, 0:E]).then_inc(weights_turned, 1)
        pe.wait_ge(weights_copied, 2)
        p_.matmul(bank[7][0:1, 0:3 * E], affine[0:E, 1:2], wT[0:E, :], start=True, stop=True)
        p_.matmul(bank[7][0:1, 3 * E:4 * E], affine[0:C, 3:4], lasT[0:C, :], start=True, stop=True).then_inc(bias_made, 1)

        def turn(n, sources):
            if n >= 2:
                pe.wait_ge(copied, n - 1)
            for m, src in enumerate(sources):
                mm = p_.transpose(bank[n % 2][:, P * m:P * (m + 1)], src, ident[:, :])
            mm.then_inc(turned, 1)

        def turn_tiles(n):
            pe.wait_ge(normed, n // 2 + 1 if n < 4 else (3 if n == 4 else 4 + (n - 5) // 2))
            turn(n, [tiles[:, 8 * n + 2 * m:8 * n + 2 * m + 2, :].rearrange("p t e -> p (t e)") for m in range(4)])

        def project_x(n, b, m):
            if n >= 4:
                pe.wait_ge(bank_read, n - 3)
            ps = project_bank(n)
            p_.matmul(v3(ps[:, 0:6 * E], 3 * E), ones_col[0:1, :],
                      bias1[0:1, 0:3 * E].unsqueeze(1).to_broadcast([1, 2, 3 * E]), start=True, stop=False,
                      skip_group_check=True)
            p_.matmul(ps[:, 0:6 * E], tT[:, b, m, :], bdz[:, :, :].rearrange("p a b -> p (a b)"), start=False, stop=True,
                      skip_group_check=True).then_inc(projected, 1)

        def project_comp(n, b, m):
            pe.wait_ge(bank_read, n - 3 if n < NX + 2 else n - 1)
            ps = project_bank(n)
            p_.matmul(v3(ps[0:C, :], E), ones_col[0:1, 0:C], cbias[0:1, :].unsqueeze(1).to_broadcast([1, 8, E]),
                      start=True, stop=False, skip_group_check=True)
            for r in range(4):
                mm = p_.matmul(v3(ps[0:C, :], E)[:, r:8:4, :], tT[:, b, m, C * r:C * (r + 1)], bdcp[:, :, :],
                               start=False, stop=True, skip_group_check=True)
            mm.then_inc(projected, 1)

        def project_protein(n, b):
            pe.wait_ge(bank_read, n - 1)
            ps = bank[2 + n % 2]
            p_.matmul(v3(ps[:, :], E), ones_col[0:1, :], pbias[0:1, :].unsqueeze(1).to_broadcast([1, 8, E]),
                      start=True, stop=False, skip_group_check=True)
            for m in range(4):
                mm = p_.matmul(ps[:, 2 * E * m:2 * E * (m + 1)], tT[:, b, m, :], bdp[:, :, :].rearrange("p a b -> p (a b)"),
                               start=False, stop=True, skip_group_check=True)
            mm.then_inc(projected, 1)

        turn_tiles(0)
        turn_tiles(1)
        pe.wait_ge(bias_copied, 2)
        for n in range(4):
            pe.wait_ge(copied, n + 1)
            for m in range(4):
                project_x(4 * n + m, n % 2, m)
            turn_tiles(n + 2)
        n = 5 + NPR

        def blocks(g):
            ps = bank[6 + g // 4][:, P * (g % 4):P * (g % 4 + 1)]
            p_.matmul(ps, abT[:, g, :], bdc[:, g].rearrange("p c j -> p (c j)"), start=True, stop=False,
                      skip_group_check=True)
            for c in range(4):
                mm = p_.matmul(ps[:, NC * c:NC * (c + 1)], ppc[:, 4 * g + c, :], ab[:, :, 4 * g + c], start=False,
                               stop=True, skip_group_check=True)
            if g % 4 == 3:
                mm.then_inc(blocks_done, 1)

        for m in range(SHOWS):
            k = m // 2
            if m % 2 == 0 and k < NCP:
                if k == 0:
                    pe.wait_ge(copied, 5)
                project_comp(NX + k, 0, k)
                if k == NCP - 1:
                    turn_tiles(6)
            elif m % 2 == 0 and k < NCP + NPR:
                pe.wait_ge(copied, k + 2)
                project_protein(NX + k, (k + 1) % 2)
                if k + 3 < 5 + NPR:
                    turn_tiles(k + 3)
            elif m == AT_TURN_AB - 1:
                pe.wait_ge(masked_ab, 1)
                for b in range(2):
                    turn(n + b, [ab2[:, 4 * g:4 * g + 4, :].rearrange("p c k -> p (c k)")
                                 for g in range(4 * b, 4 * b + 4)])
            elif AT_BLOCKS <= m < AT_BLOCKS + 8:
                if m == AT_BLOCKS:
                    pe.wait_ge(bdc_ready, 1)
                    pe.wait_ge(masked_ab, 2)
                    pe.wait_ge(bank_read, NX + NCP + NPR)
                    pe.wait_ge(copied, n + 2)
                blocks(m - AT_BLOCKS)
            if m == 0:
                pe.wait_ge(digits_ready, 1)
            if m < 2:
                pe.wait_ge(bank_read, NX - 1 + m)
            else:
                pe.wait_ge(shown_copied, m - 1)
            for r in range(RPG):
                k = RPG * m + r
                for d in range(3):
                    mm = p_.matmul(bank[4 + m % 2][:, SLOTS * r:SLOTS * (r + 1)],
                                   digit_id[:, d, k:k + 1].to_broadcast([P, P]), digits[:, d, :], start=(d == 0),
                                   stop=(d == 2), skip_group_check=True)
            mm.then_inc(shown, 1)
        pe.wait_ge(nb_ready, 1)
        for b in range(2):
            turn(n + 2 + b, [nb[:, 4 * g:4 * g + 4, :].rearrange("p j c -> p (j c)") for g in range(4 * b, 4 * b + 4)])
        pe.wait_ge(copied, n + 4)
        for m in range(NLAS):
            k = NX + NCP + NPR + m
            pe.wait_ge(bank_read, k - 1)
            ps = bank[2 + k % 2]
            p_.matmul(v3(ps[:, :], E), ones_col[0:1, :], bias1[0:1, 3 * E:4 * E].unsqueeze(1).to_broadcast([1, 8, E]),
                      start=True, stop=False, skip_group_check=True)
            for h in range(2):
                g = 2 * m + h
                mm = p_.matmul(ps[:, 4 * E * h:4 * E * (h + 1)], tT[:, g // 4, g % 4, :],
                               bdlas[:, :, :].rearrange("p a b -> p (a b)"), start=False, stop=True, skip_group_check=True)
            mm.then_inc(projected, 1)
        pe.wait_ge(xn_ready, 1)
        for b in range(4):
            turn(n + 4 + b, [xn[:, 8 * b + 2 * m:8 * b + 2 * m + 2, :].rearrange("p j e -> p (j e)") for m in range(4)])
        pe.wait_ge(late_in, 16 * len(late_loads))
        pe.wait_ge(copied, n + 8)
        pe.wait_ge(nb_centered, 2)
        for u in range(NC // 2):
            mm = p_.matmul(bank[6][:, 2 * HF * u:2 * HF * (u + 1)], xnT[:, u, :], wgat2[:, :, :].rearrange("p q f -> p (q f)"),
                           start=True, stop=True, skip_group_check=True)
        mm.then_inc(gat_done, 1)
        def hidden(f):
            e, q, b = f // 8, f // 4 % 2, f % 4
            if f >= 2:
                pe.wait_ge(gelued, f - 1)
            p_.matmul(bank[f % 2][:, :], w1s[E * q:E * (q + 1), e, :],
                      xnT[E * q:E * (q + 1), 4 * b:4 * b + 4, :].rearrange("p t n -> p (t n)"), start=True, stop=True) \
                .then_inc(hidden_done, 1)

        def expert_out(f):
            e = f // 8
            if f >= 2:
                pe.wait_ge(y_copied, f - 1)
            pe.wait_ge(gelued, f + 1)
            ps = bank[2 + f % 2]
            p_.matmul(v3(ps[:, 0:4 * E], E), ones_col[0:1, :], b2s[:, e, :].unsqueeze(1).to_broadcast([1, 4, E]),
                      start=True, stop=False, skip_group_check=True)
            for m in range(4):
                mm = p_.matmul(ps[:, E * m:E * (m + 1)], hid[:, f % 2, m, :], w2s[:, e, :], start=False, stop=True,
                               skip_group_check=True)
            mm.then_inc(y_done, 1)

        def histogram(b):
            pe.wait_ge(onehots_ready, b + 1)
            for c in range(OHC):
                mm = p_.matmul(bank[4][0:64, 0:64], onehot[:, b % 2, 0, :, c], onehot[:, b % 2, 1, :, c],
                               start=(b == 0 and c == 0), stop=(b == OHB - 1 and c == OHC - 1))
            mm.then_inc(hist_used, 1)

        pe.wait_ge(bank_read, NX + NCP + NPR + NLAS)
        hidden(0)
        for f in range(32):
            if f < 31:
                hidden(f + 1)
            expert_out(f)
        pe.wait_ge(shown_copied, SHOWS)
        for b in range(OHB):
            histogram(b)
        pe.wait_ge(missing_ready, 1)
        p_.matmul(bank[5][:, 0:1], ones_col[:, :], counts[:, 2:3], start=True, stop=False)
        p_.matmul(bank[5][:, 0:1], ones_col[0:64, :], counts[0:64, 4:5], start=False, stop=True).then_inc(missing_summed, 1)
        pe.wait_ge(flag_ready, 1)
        with pe.If(pe.value_load(flag[0:1, 0:1], min_val=0, max_val=1) > 0):
            pe.wait_ge(y_copied, 32)
            with pe.Fori(0, EC) as step:
                pe.wait_ge(gen_idx, step + 1)
                p_.matmul(bank[0][:, 0:P], dst1.to_broadcast([P, P]), ident[:, :], start=True, stop=True).then_inc(gen_same, 1)
                pe.wait_ge(gen_score, step + 1)
                for h in range(HEADS):
                    mm = p_.matmul(bank[1][:, P * h:P * (h + 1)], escore[:, h:h + 1].to_broadcast([P, P]), ident[:, :],
                                   start=True, stop=True)
                mm.then_inc(gen_others, 1)
                pe.wait_ge(gen_payload, step + 1)
                p_.matmul(bank[2][:, 0:HEADS + HF], same, payload, start=True, stop=True).then_inc(gen_summed, 1)

    @block.vector
    def _(dve):
        v = nc.vector
        t = Tally(vec)

        def total(n):
            a, m = groups[n]
            if n == 0:
                dve.wait_ge(x_in, 16)
            elif n == 2:
                dve.wait_ge(comp_in, 16)
            elif n > 2:
                dve.wait_ge(pp_in[n - 3], 16)
            src = xin[:, a:a + m, :] if a < XT else tiles[:, a:a + m, :]
            v.tensor_reduce(tsum[:, a:a + m], src, AX.X, ALU.add).then_inc(summed, 1)

        def total_sq(n):
            a, m = groups[n]
            dve.wait_ge(squared, n + 1)
            v.tensor_reduce(tssq[:, a:a + m], v3(squares[n % 2][:, 0:m * E], E), AX.X, ALU.add).then_inc(sumsq, 1)

        def settle():
            dve.wait_ge(vec, t.n)

        dve.wait_ge(edges_in, 32)
        v.tensor_scalar(plain_src, esrc, float(LAST), None, ALU.is_lt).then_inc(vec, t.up())
        v.scalar_tensor_tensor(ktmp, edst, float(NODES), esrc, ALU.mult, ALU.add).then_inc(vec, t.up())
        dve.wait_ge(vec, t.n - 1)
        v.scalar_tensor_tensor(plain, edst, float(NODES), plain_src, ALU.is_lt, ALU.mult).then_inc(vec, t.up())
        settle()
        v.scalar_tensor_tensor(work, ktmp, 1.0, plain, ALU.add, ALU.mult).then_inc(keys_ready, 1)
        dve.wait_ge(keys_ready, 1)
        v.scalar_tensor_tensor(plain, edst, float(NODES), plain, ALU.is_lt, ALU.subtract).then_inc(vec, t.up())
        settle()
        v.scalar_tensor_tensor(clamped, edst, 1.0, plain, ALU.add, ALU.mult).then_inc(scratch_free, 1)
        total(0)
        total(1)

        def compact(source, dest, width, chunks, take, first=None, between=None):
            for r in range(take // 8):
                for c in range(chunks):
                    if r:
                        dve.wait_ge(vec, t.n - chunks + 1)
                    v.max(dest[:, take * c + 8 * r:take * c + 8 * r + 8], source[:, width * c:width * (c + 1)]) \
                        .then_inc(vec, t.up())
                if between is not None:
                    between(2 * r)
                if r == 0 and first is not None:
                    first()
                if r < take // 8 - 1:
                    for c in range(chunks):
                        dve.wait_ge(vec, t.n - chunks + 1)
                        part = source[:, width * c:width * (c + 1)]
                        v.match_replace(part, dest[:, take * c + 8 * r:take * c + 8 * r + 8], part, 0.0) \
                            .then_inc(vec, t.up())
                    if between is not None:
                        between(2 * r + 1)
            settle()

        dve.wait_ge(keys_ready, 1)
        compact(work, cand1[:, :], CH1, NCH1, TAKE1, first=lambda: dve.wait_ge(keys_counted, 1))
        total_sq(0)
        total_sq(1)
        dve.wait_ge(std_x, 1)
        v.reciprocal(xr[:, 1], xr[:, 0]).then_inc(vec, t.up())
        settle()
        v.scalar_tensor_tensor(xr[:, 2], tssq[:, 0:XT], 1.0 / E, xr[:, 1], ALU.mult, ALU.mult).then_inc(vec, t.up())
        settle()
        v.tensor_tensor(xr[:, 2], xr[:, 2], xr[:, 1], ALU.mult).then_inc(var2_x, 1)
        dve.wait_ge(std2_x, 1)
        v.reciprocal(xr[:, 3], xr[:, 3]).then_inc(vec, t.up())
        settle()
        v.tensor_tensor(trstd[:, 0:XT], xr[:, 1], xr[:, 3], ALU.mult).then_inc(rstd, 1)
        dve.wait_ge(weights_turned, 1)
        v.tensor_copy(wT[:, :], bank[6][:, 0:3 * E]).then_inc(weights_copied, 1)
        v.tensor_copy(lasT[:, :], bank[6][:, 3 * E:4 * E]).then_inc(weights_copied, 1)
        dve.wait_ge(weights_copied, 2)
        dve.wait_ge(diagonals_zero, 5)
        v.tensor_scalar(wTs[:, :], wT[:, :], affine[:, 0:1], None, ALU.mult).then_inc(vec, t.up())
        for q in range(4):
            rows_q = slice(C * q, C * (q + 1))
            v.tensor_scalar(bdlas[rows_q, q, :], lasT[rows_q, :], affine[rows_q, 2:3], None, ALU.mult) \
                .then_inc(vec, t.up())
        settle()
        for q in range(2):
            half = slice(E * q, E * (q + 1))
            v.tensor_copy(bdz[half, q, :], wTs[half, :]).then_inc(vec, t.up())
            v.tensor_copy(v3(bdp[half, q, :], C), v3(wTs[half, 0:2 * E], E)[:, :, C:E]).then_inc(vec, t.up())
            v.tensor_copy(v3(bdcp[half, q, :], C), v3(wTs[half, 0:2 * E], E)[:, :, 0:C]).then_inc(vec, t.up())
        dve.wait_ge(bias_made, 1)
        v.tensor_tensor(bias1[:, :], bank[7][0:1, 0:4 * E], bias_in[:, :], ALU.add).then_inc(vec, t.up())
        settle()
        v.tensor_copy(v3(cbias[0:1, :], C), v3(bias1[0:1, 0:2 * E], E)[:, :, 0:C]).then_inc(bias_copied, 1)
        v.tensor_copy(v3(pbias[0:1, :], C), v3(bias1[0:1, 0:2 * E], E)[:, :, C:E]).then_inc(bias_copied, 1)
        for n in range(2, len(groups)):
            total(n)
            if n > 3:
                total_sq(n - 2)
        total_sq(len(groups) - 2)
        total_sq(len(groups) - 1)
        dve.wait_ge(std_rest, 1)
        v.reciprocal(trstd[:, XT:TILES], tstd[:, XT:TILES]).then_inc(rstd, 1)

        def merge(source, dest, between):
            for r in range(SLOTS // 8):
                v.max(dest[:, 8 * r:8 * r + 8], source[:, :]).then_inc(vec, t.up())
                settle()
                if r < SLOTS // 8 - 1:
                    v.match_replace(source[:, :], dest[:, 8 * r:8 * r + 8], source[:, :], 0.0).then_inc(vec, t.up())
                between(r)
                settle()

        def read_bank(n):
            dve.wait_ge(sigmoided, n + 1)
            ps = project_bank(n)
            if n < NX:
                v.tensor_tensor(ab[:, 2 * n:2 * n + 2, :], v3(ps[:, 0:6 * E], 3 * E)[:, :, 0:E], sig[:, 2 * n:2 * n + 2, 0:E],
                                ALU.mult).then_inc(bank_read, 1)
            elif n < NX + NCP:
                m = n - NX
                v.tensor_tensor(cpk[:, 8 * m:8 * m + 8, :], v3(ps[0:C, :], E)[:, :, 0:C], psig[0:C, n % 2], ALU.mult) \
                    .then_inc(bank_read, 1)
            else:
                m = n - NX - NCP
                v.tensor_tensor(ppc[:, :, 8 * m:8 * m + 8].rearrange("p c i -> p i c"), v3(ps[:, :], E)[:, :, 0:C],
                                psig[:, n % 2], ALU.mult).then_inc(bank_read, 1)

        merge(cand1, sent, lambda r: read_bank(r - 4) if 4 <= r < 4 + NX else None)
        v.tensor_copy(senti[:, 0], sent[:, :]).then_inc(vec, t.up())
        settle()
        for d, (shift, op1) in enumerate(((16, None), (8, 255), (0, 255))):
            v.tensor_scalar(senti[:, 1 + d % 2], senti[:, 0], shift, op1, ALU.arith_shift_right,
                            ALU.bypass if op1 is None else ALU.bitwise_and).then_inc(vec, t.up())
            settle()
            ins = v.tensor_copy(digits[:, d, :], senti[:, 1 + d % 2])
            ins.then_inc(digits_ready if d == 2 else vec, 1)
            if d < 2:
                t.up()

        def compound_diagonals():
            dve.wait_ge(bank_read, NX + NCP)
            for c4 in range(4):
                ins = v.tensor_copy(bdc[C * c4:C * (c4 + 1), :, c4, :], cpk[:, :, c4:C:4].rearrange("k j g -> k g j"))
                ins.then_inc(bdc_ready if c4 == 3 else vec, 1)
                if c4 < 3:
                    t.up()

        chan = [bank[6 + b][:, :].rearrange("p (c j) -> p j c", j=NC) for b in range(2)]

        def channel_sums():
            for b in range(2):
                dve.wait_ge(blocks_done, b + 1)
                v.tensor_reduce(nstat[:, b], chan[b], AX.X, ALU.add).then_inc(vec, t.up())
            settle()
            v.tensor_tensor(nstat[:, 0], nstat[:, 0], nstat[:, 1], ALU.add).then_inc(vec, t.up())

        def channel_center():
            settle()
            for b in range(2):
                v.scalar_tensor_tensor(nb[:, :, 16 * b:16 * b + 16], wide(nstat[:, 0], 16), -1.0 / C, chan[b], ALU.mult,
                                       ALU.add).then_inc(nb_centered, 1)

        def channel_squares():
            dve.wait_ge(nb_squared, 1)
            v.tensor_reduce(nstat[:, 1], v3(squares[0], C), AX.X, ALU.add).then_inc(nb_sumsq, 1)

        def channel_scale():
            dve.wait_ge(nb_std, 1)
            v.reciprocal(nstat[:, 3], nstat[:, 2]).then_inc(vec, t.up())
            settle()
            dve.wait_ge(nb_centered, 2)
            v.tensor_tensor(nb, nb, wide(nstat[:, 3], C), ALU.mult).then_inc(nb_ready, 1)

        def update(m):
            if m == 0:
                dve.wait_ge(masked_ab, 3)
            n = NX + NCP + NPR + m
            dve.wait_ge(projected, n + 1)
            js = slice(8 * m, 8 * m + 8)
            v.tensor_tensor(sig[:, js, 0:E], v3(bank[2 + n % 2][:, :], E), sig[:, js, E:2 * E], ALU.mult) \
                .then_inc(bank_read, 1)
            dve.wait_ge(bank_read, n + 1)
            v.tensor_tensor(xin[:, js, :], xin[:, js, :], sig[:, js, 0:E], ALU.add).then_inc(vec, t.up())

        def token_center():
            settle()
            v.tensor_reduce(nstat[:, 0], xin[:, :, :], AX.X, ALU.add).then_inc(vec, t.up())
            settle()
            v.scalar_tensor_tensor(xn[:, :, :], wide(nstat[:, 0], E), -1.0 / E, xin[:, :, :], ALU.mult, ALU.add) \
                .then_inc(xn_centered, 1)

        def token_squares(b):
            dve.wait_ge(xn_squared, b + 1)
            ins = v.tensor_reduce(nstat[:, 1, 16 * b:16 * b + 16], v3(squares[b], E), AX.X, ALU.add)
            ins.then_inc(xn_sumsq if b else vec, 1)
            if not b:
                t.up()

        def token_scale():
            dve.wait_ge(xn_std, 1)
            v.reciprocal(nstat[:, 3], nstat[:, 2]).then_inc(vec, t.up())
            settle()
            dve.wait_ge(xn_centered, 1)
            v.tensor_tensor(xn[:, :, :], xn[:, :, :], wide(nstat[:, 3], E), ALU.mult).then_inc(xn_ready, 1)

        def node_row_parts():
            dve.wait_ge(gat_done, 1)
            v.tensor_copy(rows[:, :, 0:HF], v3(bank[6][:, :], HF)).then_inc(vec, t.up())
            settle()
            for n in range(2):
                v.tensor_tensor(hatt[:, n], rows[:, :, 0:HF], att[:, n, :].unsqueeze(1).to_broadcast([P, NC, HF]), ALU.mult) \
                    .then_inc(vec, t.up())
            settle()
            v.tensor_reduce(rows[:, :, HF:ROW].rearrange("p j (s h) -> p s j h", s=2),
                            hatt.rearrange("p s j (h e) -> p s j h e", h=HEADS), AX.X, ALU.add).then_inc(rows_ready, 1)

        def pick(m):
            dve.wait_ge(shown_copied, m + 1)
            if m >= 2:
                dve.wait_ge(vec, t.n)
            v.scalar_tensor_tensor(owned[:, m % 2], bcast[:, m % 2], own[:, 1:2], bcast[:, m % 2], ALU.is_le, ALU.mult) \
                .then_inc(owned_ready, 1)

        def largest(m):
            dve.wait_ge(owned_ready, m + 1)
            for r in range(RPG):
                k = RPG * m + r
                v.max(coll[:, 8 * k:8 * k + 8], owned[:, m % 2, SLOTS * r:SLOTS * (r + 1)]).then_inc(vec, t.up())

        pick(0)
        for m in range(SHOWS):
            if m + 1 < SHOWS:
                pick(m + 1)
            largest(m)
            k = m // 2
            if m % 2 == 0 and k < NCP + NPR:
                read_bank(NX + k)
            if m == 2 * NCP:
                compound_diagonals()
            elif m == AT_SUM:
                channel_sums()
            elif m == AT_CENTER:
                channel_center()
            elif m == AT_SUMSQ:
                channel_squares()
            elif m == AT_SCALE:
                channel_scale()
        settle()

        def between_rounds(r):
            if 2 <= r < 2 + NLAS:
                update(r - 2)
            elif r == 7:
                token_center()

        compact(coll, cand2[:, :], CH2, NCH2, TAKE2, between=between_rounds)

        def between_merges(r):
            if r < 2:
                token_squares(r)
            elif r == 3:
                token_scale()
            elif r == 14:
                node_row_parts()

        merge(cand2, recv, between_merges)
        v.tensor_scalar(locali[:, 0], recv[:, :], own[:, 0:1], -1.0, ALU.subtract, ALU.max).then_inc(vec, t.up())
        settle()
        v.tensor_single_scalar(locali[:, 2], locali[:, 0], NODES - 1, ALU.bitwise_and).then_inc(idx_ready, 1)
        v.tensor_single_scalar(locali[:, 1], locali[:, 0], 12, ALU.arith_shift_right).then_inc(vec, t.up())
        v.tensor_scalar(local[:, :], locali[:, 0], 0.0, None, ALU.is_ge).then_inc(vec, t.up())
        settle()
        v.tensor_copy(tgt[:, :], locali[:, 1]).then_inc(vec, t.up())
        v.tensor_reduce(counts[:, 1:2], local[:, :], AX.X, ALU.add).then_inc(vec, t.up())
        settle()
        v.tensor_tensor(counts[:, 2:3], counts[:, 0:1], counts[:, 1:2], ALU.subtract).then_inc(vec, t.up())
        dve.wait_ge(keys_counted, 2)
        settle()
        v.tensor_tensor(counts[:, 2:3], counts[:, 2:3], counts[:, 3:4], ALU.add).then_inc(vec, t.up())
        every_j = tgt[:, :].unsqueeze(1).to_broadcast([P, NC, SLOTS])
        v.tensor_tensor(seg, every_j, wide(iota_j[:, :], SLOTS), ALU.is_ge).then_inc(vec, t.up())
        settle()
        v.tensor_reduce(cum[:, 0:NC], seg, AX.X, ALU.add).then_inc(vec, t.up())
        settle()
        v.tensor_tensor(present[:, :], cum[:, 0:NC], cum[:, 1:NC + 1], ALU.is_gt).then_inc(vec, t.up())
        v.tensor_scalar(tailf[:, :], cum[:, 0:NC], -1.0, 0.0, ALU.add, ALU.max).then_inc(vec, t.up())
        v.tensor_tensor(seg, every_j, wide(iota_j[:, :], SLOTS), ALU.is_equal).then_inc(vec, t.up())
        settle()
        v.tensor_scalar(taili[:, :], tailf[:, :], own[:, 2:3], None, ALU.add).then_inc(tails_ready, 1)
        dve.wait_ge(rows_ready, 1)
        for h in range(HEADS):
            v.tensor_tensor(segd, seg, wide(rows[:, :, HF + HEADS + h], SLOTS), ALU.mult).then_inc(vec, t.up())
            settle()
            v.tensor_reduce(dslot[:, h], segd.rearrange("p j l -> p l j"), AX.X, ALU.add).then_inc(vec, t.up())
            settle()
        v.memset(head[:, 0:1], 1.0).then_inc(masks_done, 1)
        v.tensor_tensor(head[:, 1:SLOTS], tgt[:, 1:SLOTS], tgt[:, 0:SLOTS - 1], ALU.not_equal).then_inc(vec, t.up())
        settle()
        dve.wait_ge(masks_done, 1)
        v.tensor_scalar(reset[:, :], head[:, :], NONE, None, ALU.mult).then_inc(vec, t.up())
        settle()
        v.tensor_scalar(head[:, :], head[:, :], -1.0, 1.0, ALU.mult, ALU.add).then_inc(vec, t.up())
        compact(clamped, ccand, CH3, NCH3, TAKE3)
        v.tensor_scalar(cidx, ccand, -1.0, None, ALU.add).then_inc(vec, t.up())
        settle()
        for digit, (op, by) in ((hi16, (ALU.arith_shift_right, 6)), (lo16, (ALU.bitwise_and, 63))):
            v.tensor_single_scalar(cdigit, cidx, by, op).then_inc(vec, t.up())
            settle()
            v.tensor_copy(digit, cdigit).then_inc(vec, t.up())
            settle()
        for b in range(OHB):
            if b >= 2:
                dve.wait_ge(hist_used, b - 1)
            for h, val in enumerate((hi16, lo16)):
                for k in range(64):
                    ins = v.tensor_scalar(onehot[:, b % 2, h, k, :], val[:, OHC * b:OHC * (b + 1)], float(k), None,
                                          ALU.is_equal)
            ins.then_inc(onehots_ready, 1)
        dve.wait_ge(hist_used, OHB)
        v.tensor_copy(histo[:, :], bank[4][0:64, 0:64]).then_inc(hist_copied, 1)
        dve.wait_ge(hist_copied, 1)
        v.tensor_reduce(nstat[0:64, 0, 0:1], histo[:, :], AX.X, ALU.add).then_inc(vec, t.up())
        settle()
        v.tensor_scalar(counts[0:64, 4:5], nstat[0:64, 0, 0:1], -1.0, None, ALU.mult).then_inc(missing_ready, 1)
        dve.wait_ge(missing_summed, 1)
        v.tensor_scalar(flag[:, :], bank[5][:, 0:1], -1.0 if force_general else 0.5, None, ALU.is_gt).then_inc(flag_ready, 1)
        dve.wait_ge(gathered, 16 * SLOTS)
        v.tensor_tensor(esc, gath[:, :, HF:HF + HEADS].rearrange("p l h -> p h l"), dslot[:, :, :], ALU.add) \
            .then_inc(vec, t.up())
        settle()
        v.scalar_tensor_tensor(esc, esc, 0.2, esc, ALU.mult, ALU.max).then_inc(vec, t.up())
        settle()
        for h in range(HEADS):
            v.tensor_tensor_scan(rmax[:, h], reset[:, :], esc[:, h], NONE, ALU.add, ALU.max).then_inc(vec, t.up())
        v.memset(carry[:, :, 0:1], 0.0).then_inc(vec, t.up())
        settle()
        v.tensor_tensor(carry[:, :, 1:SLOTS], rmax[:, :, 0:SLOTS - 1], rmax[:, :, 1:SLOTS], ALU.subtract) \
            .then_inc(vec, t.up())
        v.tensor_tensor(wgt, esc, rmax, ALU.subtract).then_inc(vec, t.up())
        v.tensor_copy(srow[:, :, 0:HEADS].rearrange("p l h -> p h l"), rmax).then_inc(vec, t.up())
        settle()
        v.tensor_scalar(carry, carry, 0.0, None, ALU.min).then_inc(exps_wanted, 1)
        dve.wait_ge(exps_done, 2)
        v.tensor_tensor(carry, carry, head[:, :].unsqueeze(1).to_broadcast([P, HEADS, SLOTS]), ALU.mult) \
            .then_inc(vec, t.up())
        msg = gath[:, :, 0:HF].rearrange("p l (h e) -> p h l e", h=HEADS)
        for h in range(HEADS):
            v.tensor_tensor(msg[:, h], msg[:, h], wide(wgt[:, h], EXPERTS), ALU.mult).then_inc(vec, t.up())
        settle()
        for h in range(HEADS):
            v.tensor_tensor_scan(srow[:, :, HEADS + h], carry[:, h], wgt[:, h], 0.0, ALU.mult, ALU.add) \
                .then_inc(vec, t.up())
            for e in range(EXPERTS):
                f = EXPERTS * h + e
                v.tensor_tensor_scan(srow[:, :, 2 * HEADS + f], carry[:, h], gath[:, :, f], 0.0, ALU.mult, ALU.add) \
                    .then_inc(vec, t.up())
        settle()
        v.engine_nop().then_inc(slots_ready, 1)
        dve.wait_ge(tails_in, 16 * NC)
        with dve.If(dve.value_load(flag[0:1, 0:1], min_val=0, max_val=1) > 0):
            n0 = Tally(gen_steps)
            v.memset(agg_in[:, :, HEADS:ROW], 0.0).then_inc(gen_steps, n0.up())
            v.memset(present[:, :], 1.0).then_inc(gen_steps, n0.up())
            dve.wait_ge(gen_steps, n0.n)
            v.memset(agg_in[:, :, 0:HEADS], NONE).then_inc(gen_blank, 1)
            dve.wait_ge(gen_edges, 32)
            v.tensor_scalar(gen_plain, gen_src, float(LAST), None, ALU.min).then_inc(gen_steps, n0.up())
            dve.wait_ge(gen_steps, n0.n)
            v.scalar_tensor_tensor(gen_keys, gen_dst, float(NODES), gen_plain, ALU.mult, ALU.add) \
                .then_inc(gen_steps, n0.up())
            dve.wait_ge(gen_steps, n0.n)
            v.tensor_scalar(gen_plain, gen_dst, float(NODES), None, ALU.is_lt).then_inc(gen_steps, n0.up())
            dve.wait_ge(gen_steps, n0.n)
            dve.wait_ge(clamped_in, 16)
            v.memset(nclamp[:, :], 0.0).then_inc(gen_steps, n0.up())
            v.scalar_tensor_tensor(gen_keys, gen_keys, 1.0, gen_plain, ALU.add, ALU.mult).then_inc(gen_steps, n0.up())
            dve.wait_ge(gen_steps, n0.n)
            dve.wait_ge(gen_mask, 1)
            base, per_step = n0.n, 22
            with dve.Fori(0, EC) as step:
                k = Tally(gen_steps)

                def settled():
                    dve.wait_ge(gen_steps, step * per_step + (base + k.n))

                v.tensor_copy(key1, gen_keys[:, bass.ds(step, 1)]).then_inc(gen_steps, k.up())
                settled()
                v.tensor_scalar(gi[:, 0:1], key1, -1.0, None, ALU.add).then_inc(gen_steps, k.up())
                v.tensor_scalar(valid1, key1, 0.0, None, ALU.is_gt).then_inc(gen_steps, k.up())
                settled()
                v.tensor_single_scalar(gi[:, 1:2], gi[:, 0:1], NODES - 1, ALU.bitwise_and).then_inc(gen_steps, k.up())
                v.tensor_scalar(gi[:, 2:3], gi[:, 0:1], 12, NODES - 1, ALU.arith_shift_right, ALU.bitwise_and) \
                    .then_inc(gen_steps, k.up())
                settled()
                v.scalar_tensor_tensor(dst1, gi[:, 2:3], 1.0, valid1, ALU.add, ALU.mult).then_inc(gen_steps, k.up())
                settled()
                v.tensor_scalar(dst1, dst1, -1.0, None, ALU.add).then_inc(gen_idx, 1)
                for n in range(3):
                    dve.wait_ge(gen_in[n], 16 * step + 16)
                v.tensor_tensor(escore, src_row[:, HF:HF + HEADS], dst_row[:, HF + HEADS:ROW], ALU.add) \
                    .then_inc(gen_steps, k.up())
                settled()
                v.scalar_tensor_tensor(escore, escore, 0.2, escore, ALU.mult, ALU.max).then_inc(gen_score, 1)
                dve.wait_ge(gen_same, step + 1)
                v.tensor_scalar(same, bank[0][:, 0:P], dst1, None, ALU.is_equal).then_inc(gen_steps, k.up())
                settled()
                v.tensor_scalar(notsame, same, -1.0, -NONE, ALU.add, ALU.mult).then_inc(gen_steps, k.up())
                v.tensor_tensor(first_of, same, earlier, ALU.mult).then_inc(gen_steps, k.up())
                dve.wait_ge(gen_others, step + 1)
                v.tensor_tensor(others, v3(bank[1][:, :], P), same.unsqueeze(1).to_broadcast([P, HEADS, P]), ALU.mult) \
                    .then_inc(gen_steps, k.up())
                settled()
                v.tensor_tensor(others, others, notsame.unsqueeze(1).to_broadcast([P, HEADS, P]), ALU.add) \
                    .then_inc(gen_steps, k.up())
                v.tensor_reduce(rank1, first_of, AX.X, ALU.add).then_inc(gen_steps, k.up())
                settled()
                v.tensor_reduce(emax, others, AX.X, ALU.max).then_inc(gen_steps, k.up())
                settled()
                v.tensor_tensor(new_row[:, 0:HEADS], emax, old_row[:, 0:HEADS], ALU.max).then_inc(gen_steps, k.up())
                settled()
                v.tensor_tensor(expo[:, 0], escore, new_row[:, 0:HEADS], ALU.subtract).then_inc(gen_steps, k.up())
                v.tensor_tensor(expo[:, 1], old_row[:, 0:HEADS], new_row[:, 0:HEADS], ALU.subtract).then_inc(gen_exp, 1)
                v.scalar_tensor_tensor(write1, rank1, 0.5, valid1, ALU.is_lt, ALU.mult).then_inc(gen_steps, k.up())
                dve.wait_ge(gen_exped, step + 1)
                settled()
                v.tensor_scalar(payload[:, 0:HEADS], expo[:, 0], valid1, None, ALU.mult).then_inc(gen_steps, k.up())
                v.tensor_scalar(write1, write1, -2.0 * NODES, 2.0 * NODES, ALU.mult, ALU.add).then_inc(gen_steps, k.up())
                settled()
                v.tensor_tensor(payload[:, HEADS:].rearrange("p (h e) -> p h e", h=HEADS),
                                src_row[:, 0:HF].rearrange("p (h e) -> p h e", h=HEADS), wide(payload[:, 0:HEADS], EXPERTS),
                                ALU.mult).then_inc(gen_payload, 1)
                v.tensor_tensor(gi[:, 3:4], write1, gi[:, 2:3], ALU.add).then_inc(gen_steps, k.up())
                v.tensor_tensor(old_row[:, HEADS:2 * HEADS], old_row[:, HEADS:2 * HEADS], expo[:, 1], ALU.mult) \
                    .then_inc(gen_steps, k.up())
                old = old_row[:, 2 * HEADS:ROW].rearrange("p (h e) -> p h e", h=HEADS)
                v.tensor_tensor(old, old, wide(expo[:, 1], EXPERTS), ALU.mult).then_inc(gen_steps, k.up())
                settled()
                dve.wait_ge(gen_summed, step + 1)
                v.tensor_tensor(new_row[:, HEADS:ROW], old_row[:, HEADS:ROW], bank[2][:, 0:HEADS + HF], ALU.add) \
                    .then_inc(gen_row, 1)
                dve.wait_ge(gen_written, 16 * step + 16)
                assert k.n == per_step, k.n
            dve.wait_ge(gen_back, 16)
        dve.wait_ge(last_in, 16)
        dve.wait_ge(clamped_in, 16)
        a_dst = rows[:, :, HF + HEADS:ROW]
        v.tensor_tensor(fin[:, 1], rows[:, :, HF:HF + HEADS], a_dst, ALU.add).then_inc(vec, t.up())
        v.tensor_tensor(fin[:, 2], a_dst, last_row[:, HF:HF + HEADS].unsqueeze(1).to_broadcast([P, NC, HEADS]), ALU.add) \
            .then_inc(vec, t.up())
        v.tensor_scalar(nstat[:, 4], nclamp[:, :], 0.5, NONE, ALU.is_lt, ALU.mult).then_inc(vec, t.up())
        v.tensor_scalar(nstat[:, 5], present[:, :], -1.0, -NONE, ALU.add, ALU.mult).then_inc(vec, t.up())
        settle()
        v.scalar_tensor_tensor(fin[:, 1:3], fin[:, 1:3], 0.2, fin[:, 1:3], ALU.mult, ALU.max).then_inc(vec, t.up())
        settle()
        v.tensor_tensor(fin[:, 2], fin[:, 2], wide(nstat[:, 4], HEADS), ALU.add).then_inc(vec, t.up())
        dve.wait_ge(tails_in, 16 * NC)
        v.tensor_tensor(fin[:, 0], agg_in[:, :, 0:HEADS], wide(present[:, :], HEADS), ALU.mult).then_inc(vec, t.up())
        settle()
        v.tensor_tensor(fin[:, 0], fin[:, 0], wide(nstat[:, 5], HEADS), ALU.add).then_inc(vec, t.up())
        v.tensor_tensor(fin[:, 3], fin[:, 1], fin[:, 2], ALU.max).then_inc(vec, t.up())
        settle()
        v.tensor_tensor(fin[:, 3], fin[:, 3], fin[:, 0], ALU.max).then_inc(vec, t.up())
        settle()
        v.tensor_tensor(fin[:, 0:3], fin[:, 0:3], fin[:, 3].unsqueeze(1).to_broadcast([P, 3, NC, HEADS]), ALU.subtract) \
            .then_inc(fin_wanted, 1)
        dve.wait_ge(fin_done, 1)
        v.tensor_tensor(fin[:, 2], fin[:, 2], wide(nclamp[:, :], HEADS), ALU.mult).then_inc(vec, t.up())
        v.tensor_tensor(fin[:, 4], agg_in[:, :, HEADS:2 * HEADS], fin[:, 0], ALU.mult).then_inc(vec, t.up())
        settle()
        v.tensor_tensor(fin[:, 5], fin[:, 1], fin[:, 2], ALU.add).then_inc(vec, t.up())
        settle()
        v.scalar_tensor_tensor(fin[:, 5], fin[:, 5], 1e-16, fin[:, 4], ALU.add, ALU.add).then_inc(vec, t.up())
        settle()
        v.reciprocal(fin[:, 6], fin[:, 5]).then_inc(vec, t.up())
        settle()
        v.tensor_tensor(fin[:, 0:3], fin[:, 0:3], fin[:, 6].unsqueeze(1).to_broadcast([P, 3, NC, HEADS]), ALU.mult) \
            .then_inc(vec, t.up())
        settle()

        def heads(ap):
            return ap.rearrange("p j (h e) -> p j h e", h=HEADS)

        def per_head(n):
            return fin[:, n].unsqueeze(3).to_broadcast([P, NC, HEADS, EXPERTS])

        msg_in = agg_in[:, :, 2 * HEADS:ROW]
        v.tensor_tensor(heads(msg_in), heads(msg_in), per_head(0), ALU.mult).then_inc(vec, t.up())
        v.tensor_tensor(heads(hatt[:, 0]), heads(rows[:, :, 0:HF]), per_head(1), ALU.mult).then_inc(vec, t.up())
        v.tensor_tensor(heads(hatt[:, 1]), heads(last_row[:, 0:HF].unsqueeze(1).to_broadcast([P, NC, HF])), per_head(2),
                        ALU.mult).then_inc(vec, t.up())
        settle()
        agg = hatt[:, 0]

        def every_token(n):
            return gat_aff[:, n, :].unsqueeze(1).to_broadcast([P, NC, HF])

        for term in (msg_in, hatt[:, 1], every_token(0)):
            v.tensor_tensor(agg, agg, term, ALU.add).then_inc(vec, t.up())
            settle()
        v.tensor_reduce(nstat[:, 0], agg, AX.X, ALU.add).then_inc(vec, t.up())
        settle()
        v.scalar_tensor_tensor(agg, wide(nstat[:, 0], HF), -1.0 / HF, agg, ALU.mult, ALU.add).then_inc(vec, t.up())
        settle()
        v.tensor_tensor(hatt[:, 1], agg, agg, ALU.mult).then_inc(vec, t.up())
        settle()
        v.tensor_reduce(nstat[:, 1], hatt[:, 1], AX.X, ALU.add).then_inc(fin_wanted, 1)
        dve.wait_ge(fin_done, 2)
        v.reciprocal(nstat[:, 3], nstat[:, 2]).then_inc(vec, t.up())
        settle()
        v.tensor_tensor(agg, agg, wide(nstat[:, 3], HF), ALU.mult).then_inc(vec, t.up())
        settle()
        v.tensor_tensor(agg, agg, every_token(1), ALU.mult).then_inc(vec, t.up())
        settle()
        v.tensor_tensor(agg, agg, every_token(2), ALU.add).then_inc(vec, t.up())
        settle()
        score, top, gate, sel = fin[:, 2], nstat[:, 0], fin[:, 3], fin[:, 5]
        v.tensor_reduce(fin[:, 1], agg.rearrange("p j (h e) -> p j e h", h=HEADS), AX.X, ALU.add).then_inc(vec, t.up())
        settle()
        v.tensor_scalar(score, fin[:, 1], 1.0 / HEADS, None, ALU.mult).then_inc(vec, t.up())
        settle()
        mine = score.unsqueeze(3).to_broadcast([P, NC, EXPERTS, EXPERTS])
        other = score.unsqueeze(2).to_broadcast([P, NC, EXPERTS, EXPERTS])
        larger, equal = heads(hatt[:, 0]), heads(hatt[:, 1])
        v.tensor_tensor(larger, other, mine, ALU.is_gt).then_inc(vec, t.up())
        v.tensor_tensor(equal, other, mine, ALU.is_equal).then_inc(vec, t.up())
        v.tensor_reduce(top, score, AX.X, ALU.max).then_inc(vec, t.up())
        settle()
        v.tensor_tensor(equal, equal, before[:, :, :].unsqueeze(1).to_broadcast([P, NC, EXPERTS, EXPERTS]), ALU.mult) \
            .then_inc(vec, t.up())
        v.tensor_tensor(gate, score, wide(top, EXPERTS), ALU.subtract).then_inc(fin_wanted, 1)
        settle()
        v.tensor_tensor(larger, larger, equal, ALU.add).then_inc(vec, t.up())
        settle()
        v.tensor_reduce(fin[:, 4], larger, AX.X, ALU.add).then_inc(vec, t.up())
        settle()
        v.tensor_scalar(sel, fin[:, 4], 1.5, None, ALU.is_lt).then_inc(vec, t.up())
        settle()
        dve.wait_ge(fin_done, 3)
        v.tensor_tensor(gate, gate, sel, ALU.mult).then_inc(vec, t.up())
        settle()
        v.tensor_reduce(nstat[:, 1], gate, AX.X, ALU.add).then_inc(vec, t.up())
        settle()
        v.reciprocal(nstat[:, 3], nstat[:, 1]).then_inc(vec, t.up())
        settle()
        v.tensor_tensor(gate, gate, wide(nstat[:, 3], EXPERTS), ALU.mult).then_inc(vec, t.up())
        settle()
        dve.wait_ge(y_copied, 32)
        for n in range(2):
            js = slice(16 * n, 16 * n + 16)
            for e in range(EXPERTS):
                v.tensor_tensor(yexp[:, e, js, :], yexp[:, e, js, :], wide(gate[:, js, e], E), ALU.mult) \
                    .then_inc(vec, t.up())
            for e in range(EXPERTS):
                dve.wait_ge(vec, t.n - (3 if e == 0 else 0))
                v.tensor_tensor(xin[:, js, :], xin[:, js, :], yexp[:, e, js, :], ALU.add) \
                    .then_inc(*((out_ready, 1) if e == 3 else (vec, t.up())))

    ctx.close()


NAMES = ["x", "L0_conv_protein_pair", "L0_conv_compound_pair", "L0_conv_z_mask", "L0_conv_ln_w", "L0_conv_ln_b",
         "L0_conv_lnc_w", "L0_conv_lnc_b", "L0_conv_g1_w", "L0_conv_g1_b", "L0_conv_g2_w", "L0_conv_g2_b",
         "L0_conv_l1_w", "L0_conv_l1_b", "L0_conv_l2_w", "L0_conv_l2_b", "L0_conv_eg_w", "L0_conv_eg_b",
         "L0_conv_las_w", "L0_conv_las_b", "L0_ffn_W_gat", "L0_ffn_att_src", "L0_ffn_att_dst", "L0_ffn_b_gat",
         "L0_ffn_ln_gamma", "L0_ffn_ln_beta", "L0_ffn_W1", "L0_ffn_b1", "L0_ffn_W2", "L0_ffn_b2",
         "L0_ffn_edge_index"]


def program(nc, shapes, **options):
    args = [nc.dram_tensor(f"in_{n}", s, d, kind="ExternalInput").ap() for n, (s, d) in zip(NAMES, shapes)]
    out = nc.dram_tensor("out_0", (1, P, NC, E), F32, kind="ExternalOutput").ap()
    build(nc, *args, out, **options)


def kernel(**inputs):
    import concourse.bacc as bacc
    import numpy as np
    from concourse.bass_utils import run_bass_kernel_spmd

    nc = bacc.Bacc("TRN2", target_bir_lowering=False, num_devices=1)
    arrays = {f"in_{n}": np.ascontiguousarray(inputs[n]) for n in NAMES}
    program(nc, [(a.shape, mybir.dt.from_np(a.dtype)) for a in arrays.values()])
    r = run_bass_kernel_spmd(nc, [arrays], core_ids=[0])
    return r.results[0]["out_0"]
```

```python
from contextlib import ExitStack

import concourse.bass as bass
from concourse import mybir
from concourse.alu_op_type import AluOpType as ALU

F32 = mybir.dt.float32
BF16 = mybir.dt.bfloat16
I32 = mybir.dt.int32
ACT = mybir.ActivationFunctionType
AX = mybir.AxisListType

P = 128
NC = 32
E = 64
C = 32
NODES = P * NC
LAST = NODES - 1
HEADS, EXPERTS = 4, 4
HF = HEADS * EXPERTS
ROW = HF + 2 * HEADS
HIDDEN = 2 * E
EDGES = 262144
EC = EDGES // P
OWNED = NC * NODES
NONE = -1.0e30

CH1, TAKE1 = 256, 40
NCH1 = EC // CH1
W1 = NCH1 * TAKE1
SLOTS = 176
CH2, TAKE2 = 128, 40
Y2 = P * 8
NCH2 = Y2 // CH2
W2 = NCH2 * TAKE2
RPG = 2
CH3, TAKE3 = 128, 48
NCH3 = EC // CH3
W3 = NCH3 * TAKE3
OHC = 128
OHB = W3 // OHC
PARTS = (0, 80, 144, SLOTS)
OUT_PARTS = (0, 12, 22, NC)
SCAN_BEFORE = (1, 3, 4)

XT, CT = NC, NC * NC // P
TILES = XT + CT + P
GT = 16


class Tally:

    def __init__(self, sem):
        self.sem, self.n = sem, 0

    def up(self):
        self.n += 1
        return 1


def build(nc, x, pp, comp, zmask, ln_w, ln_b, lnc_w, lnc_b, g1_w, g1_b, g2_w, g2_b, l1_w, l1_b, l2_w, l2_b,
          eg_w, eg_b, las_w, las_b, W_gat, att_src, att_dst, b_gat, gamma, beta, W1_, b1, W2_, b2, edges, out,
          force_general=False):
    ctx = ExitStack()

    def sb(name, shape, dt=F32):
        return ctx.enter_context(nc.sbuf_tensor(name, shape, dt))

    def sem(name):
        return ctx.enter_context(nc.semaphore(name))

    node_rows = nc.dram_tensor("node_rows", (NODES, ROW), F32, kind="Internal").ap()
    slot_rows = nc.dram_tensor("slot_rows", (P * SLOTS, ROW), F32, kind="Internal").ap()
    hist_dram = nc.dram_tensor("hist_dram", (64, 64), F32, kind="Internal").ap()
    state_rows = nc.dram_tensor("state_rows", (NODES, ROW), F32, kind="Internal").ap()

    stage_a = sb("stage_a", [P, 16384])
    stage_b = sb("stage_b", [P, EXPERTS * NC * E])
    stage_c = sb("stage_c", [P, 6400])

    def carve(region, dt=F32):
        at = [0]

        def take(*shape):
            n = 1
            for d in shape:
                n *= d
            words = n if dt == F32 or dt == I32 else n // 2
            ap = region[:, at[0]:at[0] + words]
            at[0] += words
            assert at[0] <= region.shape[1]
            if dt != F32:
                ap = ap.bitcast(dt)
            if len(shape) == 1:
                return ap
            names = "abcd"[:len(shape)]
            sizes = {c: d for c, d in zip(names, shape)}
            return ap.rearrange(f"p ({' '.join(names)}) -> p {' '.join(names)}", **sizes)
        return take

    a1 = carve(stage_a)
    tiles = a1(TILES, E)
    ppc = a1(C, P)
    squares_a = a1(GT * E)
    seg = carve(stage_a, BF16)(NC, SLOTS)
    segd = carve(stage_a[:, NC * SLOTS // 2:])(NC, SLOTS)
    onehot = carve(stage_a, BF16)(2, 2, 64, OHC)
    a4 = carve(stage_a, I32)
    gen_dst, gen_src = a4(EC), a4(EC)
    gen_keys, gen_plain = (stage_a[:, n * EC:(n + 1) * EC] for n in (2, 3))
    a5 = carve(stage_a[:, 4 * EC:16384])
    same = a5(P)
    earlier = a5(P)
    others = a5(HEADS, P)
    notsame, first_of = a5(P), a5(P)
    src_row, dst_row, old_row, new_row = a5(ROW), a5(ROW), a5(ROW), a5(ROW)
    payload = a5(HEADS + HF)
    escore, emax, expo = a5(HEADS), a5(HEADS), a5(2, HEADS)
    key1, valid1, dst1, rank1, write1 = (a5(1) for _ in range(5))
    gi = carve(stage_a[:, 16384 - 8:16384], I32)(8)

    yscratch = stage_a[:, TILES * E:TILES * E + EC]
    ktmp, plain_src, plain = (stage_b[:, n * EC:(n + 1) * EC] for n in (1, 2, 3))
    b1_ = carve(stage_b)
    sig = b1_(NC, 2 * E)
    ab = b1_(NC, E)
    abT = b1_(8, P)
    nb = b1_(NC, C)
    ab2 = nb.rearrange("p j c -> p (j c)").rearrange("p (c k) -> p c k", k=NC)
    yexp = carve(stage_b)(EXPERTS, NC, E)

    edst, esrc = stage_c[:, 0:EC].bitcast(I32), stage_c[:, EC:2 * EC].bitcast(I32)
    gath = carve(stage_c)(SLOTS, ROW)
    c1_ = carve(stage_c)
    bcast, owned = c1_(4, RPG * SLOTS), c1_(2, RPG * SLOTS)
    coll = c1_(Y2)
    clamped = carve(stage_c[:, SLOTS * ROW:6400])(EC)
    c2_ = carve(stage_c[:, SLOTS * ROW:6400])
    wgt = c2_(HEADS, SLOTS)
    carry = c2_(HEADS, SLOTS)
    c3_ = carve(stage_c[:, SLOTS * ROW:6400])
    agg_in = c3_(NC, ROW)
    fin = c3_(8, NC, HEADS)

    ident = sb("ident", [P, P])
    digit_id = sb("digit_id", [P, 3, P], BF16)
    ones_col = sb("ones_col", [P, P])
    iota_j = sb("iota_j", [P, NC])
    iota_i = sb("iota_i", [P, NC], I32)
    own_i = sb("own_i", [P, 3], I32)
    own = sb("own", [P, 3])
    eps = sb("eps", [P, 2])
    zbias = sb("zbias", [3, 4 * E], BF16)
    pbias = sb("pbias", [3, E], BF16)
    cbias = sb("cbias", [3, E], BF16)
    parts = sb("parts", [3, 2, 4 * E], BF16)
    ones_row = sb("ones_row", [3, P], BF16)
    before = sb("before", [P, EXPERTS, EXPERTS])

    w_nat = sb("w_nat", [P, 2 * E])
    eg_nat = sb("eg_nat", [E, 2 * E])
    las_nat = sb("las_nat", [E, 4 * C])
    affine = sb("affine", [P, 4])
    bias_in = sb("bias_in", [3, 4 * E])
    wT = sb("wT", [P, 3 * E])
    wTs = sb("wTs", [P, 3 * E])
    bdz = sb("bdz", [P, 2, 3 * E])
    bdp = sb("bdp", [P, 2, E])
    bdcp = sb("bdcp", [P, 2, E])
    bdlas = sb("bdlas", [P, 4, E])
    lasT = sb("lasT", [P, E])
    bias1 = sb("bias1", [3, 4 * E])
    wgat2 = sb("wgat2", [P, 2, HF])
    att = sb("att", [P, 2, HF])
    gat_aff = sb("gat_aff", [P, 3, HF])
    beta_mean = sb("beta_mean", [P, EXPERTS])
    w1s = sb("w1s", [P, EXPERTS, HIDDEN])
    b1s = sb("b1s", [HIDDEN, EXPERTS])
    w2s = sb("w2s", [HIDDEN, EXPERTS, E])
    b2s = sb("b2s", [1, EXPERTS, E])
    mask = sb("mask", [P, NC])

    xin = sb("xin", [P, NC, E])
    tsum = sb("tsum", [P, TILES])
    tmean = sb("tmean", [P, TILES])
    tssq = sb("tssq", [P, TILES])
    tstd = sb("tstd", [P, TILES])
    trstd = sb("trstd", [P, TILES])
    xr = sb("xr", [P, 4, XT])
    tT = sb("tT", [P, 2, 4, P])
    psig = sb("psig", [P, 2, 8, C])
    cpk = sb("cpk", [C, NC, C])
    bdc = sb("bdc", [P, 8, 4, NC])
    nstat = sb("nstat", [P, 6, NC])
    xn = sb("xn", [P, NC, E])
    xnT = sb("xnT", [P, NC // 2, P])
    rows = sb("rows", [P, NC, ROW])
    last_row = sb("last_row", [P, ROW])

    work = xn[:, :, :].rearrange("p j e -> p (j e)")
    ccand, cidx = work[:, 0:W3], work[:, W3:2 * W3].bitcast(I32)
    cdigit = ccand.bitcast(I32)
    hi16, lo16 = work[:, 2 * W3:5 * W3 // 2].bitcast(BF16), work[:, W3:3 * W3 // 2].bitcast(BF16)
    cand1 = sb("cand1", [P, W1])
    sent = sb("sent", [P, SLOTS])
    senti = sb("senti", [P, 3, SLOTS], I32)
    digits = sb("digits", [P, 3, SLOTS], BF16)
    cand2 = cand1
    recv = sb("recv", [P, SLOTS])
    local = sb("local", [P, SLOTS])
    locali = senti
    tgt = sb("tgt", [P, SLOTS])
    counts = sb("counts", [P, 5])
    flag = sb("flag", [P, 1], I32)
    cum = sb("cum", [P, NC + 1])
    present = sb("present", [P, NC])
    tailf = sb("tailf", [P, NC])
    taili = sb("taili", [P, NC], I32)
    dslot = sb("dslot", [P, HEADS, SLOTS])
    head = sb("head", [P, SLOTS])
    reset = sb("reset", [P, SLOTS])
    histo = sb("histo", [64, 64])
    nclamp = sb("nclamp", [P, NC])

    hid = sb("hid", [P, 2, 4, P])
    squares = [squares_a, hid[:, :, :, :].rearrange("p b t n -> p (b t n)")]
    hatt = squares_a.rearrange("p (s j f) -> p s j f", s=2, j=NC)

    bank = [ctx.enter_context(nc.psum_tensor(f"bank{n}", [P, 512], F32)) for n in range(8)]

    vec, act_, pe_, pool_ = sem("vec"), sem("act"), sem("pe"), sem("pool")
    x_in, edges_in, comp_in, params_in = sem("x_in"), sem("edges_in"), sem("comp_in"), sem("params_in")
    pp_in = [sem(f"pp_in{n}") for n in range(P // GT)]
    consts = sem("consts")
    weights_turned, weights_copied, bias_made, bias_copied = sem("weights_turned"), sem("weights_copied"), \
        sem("bias_made"), sem("bias_copied")
    diagonals_zero = sem("diagonals_zero")
    summed, centered, squared, sumsq, normed = sem("summed"), sem("centered"), sem("squared"), sem("sumsq"), sem("normed")
    std_x, std_rest, rstd, var2_x, std2_x = sem("std_x"), sem("std_rest"), sem("rstd"), sem("var2_x"), sem("std2_x")
    turned, copied, projected, sigmoided, bank_read = sem("turned"), sem("copied"), sem("projected"), \
        sem("sigmoided"), sem("bank_read")
    scratch_free = sem("scratch_free")
    masked_ab, bdc_ready, blocks_done, nb_centered, nb_squared, nb_sumsq, nb_std, nb_ready = (
        sem(n) for n in ("masked_ab", "bdc_ready", "blocks_done", "nb_centered", "nb_squared", "nb_sumsq", "nb_std",
                         "nb_ready"))
    x1_ready, xn_centered, xn_squared, xn_sumsq, xn_std, xn_ready, gat_done, rows_ready, rows_stored, last_in = (
        sem(n) for n in ("x1_ready", "xn_centered", "xn_squared", "xn_sumsq", "xn_std", "xn_ready", "gat_done",
                         "rows_ready", "rows_stored", "last_in"))
    keys_ready, keys_counted, digits_ready, shown, shown_copied, owned_ready = (
        sem(n) for n in ("keys_ready", "keys_counted", "digits_ready", "shown", "shown_copied", "owned_ready"))
    missing_ready, missing_summed, flag_ready, idx_ready, tails_ready, masks_done = (
        sem(n) for n in ("missing_ready", "missing_summed", "flag_ready", "idx_ready", "tails_ready", "masks_done"))
    gathered = [sem(f"gathered{n}") for n in range(len(PARTS) - 1)]
    onehots_ready, hist_used, hist_copied, hist_stored, clamped_in = (
        sem(n) for n in ("onehots_ready", "hist_used", "hist_copied", "hist_stored", "clamped_in"))
    exps_wanted, exps_done, slots_ready, slots_stored, tails_in = (
        sem(n) for n in ("exps_wanted", "exps_done", "slots_ready", "slots_stored", "tails_in"))
    hidden_done, gelued, y_done, y_copied = sem("hidden_done"), sem("gelued"), sem("y_done"), sem("y_copied")
    gate_ready, out_last_ready = sem("gate_ready"), sem("out_last_ready")
    fin_wanted, fin_done, out_ready, out_stored = sem("fin_wanted"), sem("fin_done"), sem("out_ready"), sem("out_stored")

    groups = [(0, GT), (GT, GT), (XT, CT)] + [(XT + CT + GT * n, GT) for n in range(P // GT)]

    def v3(ap, inner):
        return ap.rearrange("p (a b) -> p a b", b=inner)

    def wide(ap, n):
        return ap.unsqueeze(2).to_broadcast([ap.shape[0], ap.shape[1], n])

    NX, NCP, NPR, NLAS = NC // 2, NC // 8, P // 8, NC // 8

    loads = [(w_nat[C * n:C * (n + 1), E * d:E * (d + 1)], w[:, :])
             for n, w in enumerate((l1_w, l2_w, g1_w, g2_w)) for d in range(2)]
    loads += [(eg_nat[:, E * d:E * (d + 1)], eg_w[:, :]) for d in range(2)]
    loads += [(las_nat[:, C * d:C * (d + 1)], las_w[:, :]) for d in range(4)]
    loads += [(affine[E * d:E * (d + 1), n:n + 1], w.unsqueeze(1)) for n, w in enumerate((ln_w, ln_b)) for d in range(2)]
    loads += [(affine[C * d:C * (d + 1), n + 2:n + 3], w.unsqueeze(1))
              for n, w in enumerate((lnc_w, lnc_b)) for d in range(4)]
    loads += [(bias_in[:, C * n:C * (n + 1)], w.partition_broadcast(3)) for n, w in enumerate((l1_b, l2_b, g1_b, g2_b))]
    loads += [(bias_in[:, 2 * E:3 * E], eg_b.partition_broadcast(3)), (bias_in[:, 3 * E:4 * E], las_b.partition_broadcast(3))]
    loads += [(mask[:, :], zmask.rearrange("a i j b -> (a i) (j b)"))]
    late_loads = [(wgat2[E * q:E * (q + 1), q, :], W_gat[:, :]) for q in range(2)]
    late_loads += [(att[:, n, :], a.rearrange("h e -> (h e)").partition_broadcast(P)) for n, a in enumerate((att_src, att_dst))]
    late_loads += [(gat_aff[:, n, :], a.partition_broadcast(P)) for n, a in enumerate((b_gat, gamma, beta))]
    late_loads += [(w1s[E * q:E * (q + 1), :, :], W1_.rearrange("e i f -> i e f")) for q in range(2)]
    late_loads += [(w2s[:, :, :], W2_.rearrange("e f o -> f e o")), (b1s[:, :], b1.rearrange("e f -> f e")),
                   (b2s[:, :, :], b2.rearrange("e o -> (e o)").unsqueeze(0).rearrange("a (e o) -> a e o", e=EXPERTS))]
    late_in = sem("late_in")

    gen_blank, gen_state, gen_edges, gen_idx, gen_score, gen_others, gen_exp, gen_exped, gen_payload = (
        sem(f"gen_{n}") for n in ("blank", "state", "edges", "idx", "score", "others", "exp", "exped", "payload"))
    gen_tick, gen_scores = sem("gen_tick"), sem("gen_scores")
    gen_in = [sem(f"gen_in{n}") for n in range(3)]
    gen_same, gen_summed, gen_row, gen_written, gen_mask, gen_steps, gen_back, gen_zero = (
        sem(f"gen_{n}") for n in ("same", "summed", "row", "written", "mask", "steps", "back", "zero"))

    SHOWS = P // RPG

    def project_bank(n):
        return bank[2 + n % 4 if n < NX else 2 + n % 2]

    EARLY = NX + NCP + 8
    AT_TURN_AB, AT_BLOCKS, AT_SUM, AT_CENTER, AT_SUMSQ, AT_SCALE, AT_TURN_NB = 23, 24, 47, 49, 52, 55, 58

    AT_LAS = (60, 62)
    AT_ROWS = 11

    block = ctx.enter_context(nc.Block())

    @block.sync
    def _(sp):
        sp.dma_start(edst, edges[1].rearrange("(p c) -> p c", p=P)).then_inc(edges_in, 16)
        sp.dma_start(esrc, edges[0].rearrange("(p c) -> p c", p=P)).then_inc(edges_in, 16)
        sp.dma_start(xin[:, :, :], x.rearrange("a i j e -> (a i) j e")).then_inc(x_in, 16)
        sp.dma_start(tiles[:, XT:XT + CT, :],
                     comp.rearrange("a j k e -> (a j k) e").rearrange("(t p) e -> p t e", p=P)).then_inc(comp_in, 16)
        for n in range(P // GT):
            sp.dma_start(tiles[:, XT + CT + GT * n:XT + CT + GT * (n + 1), :],
                         pp[0, GT * n:GT * (n + 1), :, :].rearrange("i k e -> k i e")).then_inc(pp_in[n], 16)
        sp.wait_ge(rows_ready, 1)
        sp.dma_start(node_rows.rearrange("(p j) r -> p (j r)", p=P), rows[:, :, :].rearrange("p j r -> p (j r)")) \
            .then_inc(rows_stored, 16)
        sp.wait_ge(rows_stored, 16)
        sp.dma_start(last_row[:, :], node_rows[LAST, :].partition_broadcast(P)).then_inc(last_in, 16)
        for n, (a, b) in enumerate(zip(PARTS, PARTS[1:])):
            sp.wait_ge(slots_ready, n + 1)
            sp.dma_start(slot_rows.rearrange("(p l) r -> p l r", p=P)[:, a:b, :], gath[:, a:b, :]).then_inc(slots_stored, 16)
        sp.wait_ge(hist_copied, 1)
        sp.dma_start(hist_dram[:, :], histo[:, :]).then_inc(hist_stored, 16)
        sp.wait_ge(hist_stored, 16)
        sp.dma_start(nclamp[:, :], hist_dram.rearrange("a (b j) -> (a b) j", j=NC)).then_inc(clamped_in, 16)
        sp.wait_ge(flag_ready, 1)
        with sp.If(sp.value_load(flag[0:1, 0:1], min_val=0, max_val=1) > 0):
            sp.wait_ge(gen_blank, 1)
            sp.dma_start(gen_dst, edges[1].rearrange("(p c) -> p c", p=P)).then_inc(gen_edges, 16)
            sp.dma_start(gen_src, edges[0].rearrange("(p c) -> p c", p=P)).then_inc(gen_edges, 16)
            sp.dma_start(state_rows.rearrange("(p j) r -> p (j r)", p=P), agg_in.rearrange("p j r -> p (j r)")) \
                .then_inc(gen_state, 16)
            sp.wait_ge(gen_written, 16 * EC)
            sp.wait_ge(gen_state, 16)
            sp.dma_start(agg_in.rearrange("p j r -> p (j r)"), state_rows.rearrange("(p j) r -> p (j r)", p=P)) \
                .then_inc(gen_back, 16)
        for n, (a, b) in enumerate(zip(OUT_PARTS, OUT_PARTS[1:])):
            if b < NC:
                sp.wait_ge(out_ready, n + 1)
            else:
                sp.wait_ge(out_last_ready, 1)
            sp.dma_start(out[0, :, a:b, :], xin[:, a:b, :]).then_inc(out_stored, 16)
        sp.wait_ge(out_stored, 16 * (len(OUT_PARTS) - 1))

    @block.gpsimd
    def _(pool):
        g = nc.gpsimd
        t = Tally(pool_)
        g.memset(wgat2[:, :, :], 0.0).then_inc(pool_, t.up())
        pool.wait_ge(pool_, t.n)
        for dst, src in late_loads:
            g.dma_start(dst, src, allow_slow_non_contiguous=True).then_inc(late_in, 16)
        g.memset(ident[:, :], 0.0).then_inc(pool_, t.up())
        g.memset(ones_col[:, :], 1.0).then_inc(pool_, t.up())
        g.memset(ones_row[:, :], 1.0).then_inc(pool_, t.up())
        g.memset(eps[:, 0:1], 1e-6).then_inc(pool_, t.up())
        g.memset(eps[:, 1:2], 1e-5).then_inc(pool_, t.up())
        g.iota(iota_i[:, :], [[1, NC]], base=0, channel_multiplier=0).then_inc(pool_, t.up())
        g.iota(own_i[:, 0:1], [[0, 1]], base=1, channel_multiplier=OWNED).then_inc(pool_, t.up())
        g.iota(own_i[:, 1:2], [[0, 1]], base=OWNED, channel_multiplier=OWNED).then_inc(pool_, t.up())
        g.iota(own_i[:, 2:3], [[0, 1]], base=0, channel_multiplier=SLOTS).then_inc(pool_, t.up())
        g.memset(before[:, :, :], 0.0).then_inc(pool_, t.up())
        pool.wait_ge(pool_, t.n)
        g.affine_select(out=ident[:, :], in_=ident[:, :], compare_op=ALU.not_equal, fill=1.0, base=0,
                        pattern=[[-1, P]], channel_multiplier=1).then_inc(pool_, t.up())
        g.tensor_copy(iota_j[:, :], iota_i[:, :]).then_inc(pool_, t.up())
        g.tensor_copy(own[:, :], own_i[:, :]).then_inc(pool_, t.up())
        for e in range(1, EXPERTS):
            g.memset(before[:, e, 0:e], 1.0).then_inc(pool_, t.up())
        pool.wait_ge(pool_, t.n)
        for d in range(3):
            g.tensor_scalar(digit_id[:, d, :], ident[:, :], float(256 ** (2 - d)), None, ALU.mult).then_inc(pool_, t.up())
        pool.wait_ge(pool_, t.n)
        g.memset(cum[:, :], 0.0).then_inc(consts, 1)
        for z in (bdz[:, :, :], bdp[:, :, :], bdcp[:, :, :], bdlas[:, :, :], bdc[:, :, :, :]):
            g.memset(z, 0.0).then_inc(diagonals_zero, 1)
        def center(n):
            a, m = groups[n]
            pool.wait_ge(summed, n + 1)
            part = tiles[:, a:a + m, :]
            g.tensor_scalar(tmean[:, a:a + m], tsum[:, a:a + m], 1.0 / E, None, ALU.mult).then_inc(pool_, t.up())
            pool.wait_ge(pool_, t.n)
            g.tensor_tensor(part, xin[:, a:a + m, :] if a < XT else part, wide(tmean[:, a:a + m], E), ALU.subtract) \
                .then_inc(centered, 1)

        def divide(n):
            a, m = groups[n]
            pool.wait_ge(rstd, 1 if a < XT else 2)
            pool.wait_ge(squared, n + 1)
            part = tiles[:, a:a + m, :]
            g.tensor_tensor(part, part, wide(trstd[:, a:a + m], E), ALU.mult).then_inc(normed, 1)

        for which in (range(2), range(2, len(groups))):
            for n in which:
                center(n)
            for n in which:
                divide(n)
        pool.wait_ge(bank_read, NX)
        pool.wait_ge(params_in, 16 * len(loads))
        g.tensor_tensor(ab2, ab[:, :, C:E].rearrange("p k c -> p c k"), mask[:, :].unsqueeze(1).to_broadcast([P, C, NC]),
                        ALU.mult).then_inc(masked_ab, 1)
        g.tensor_tensor(ab[:, :, 0:C], ab[:, :, 0:C], wide(mask[:, :], C), ALU.mult).then_inc(masked_ab, 1)
        g.tensor_tensor(sig[:, :, E:2 * E], sig[:, :, E:2 * E], wide(mask[:, :], E), ALU.mult).then_inc(masked_ab, 1)
        pool.wait_ge(rows_stored, 16)
        for n, (a, b) in enumerate(zip(PARTS, PARTS[1:])):
            pool.wait_ge(idx_ready, min(n, 1) + 1)
            for l in range(a, b):
                g.indirect_dma_start(out=gath[:, l, :], out_offset=None, in_=node_rows[:, :],
                                     in_offset=bass.IndirectOffsetOnAxis(ap=locali[:, 2, l:l + 1], axis=0)) \
                    .then_inc(gathered[n], 16)
        pool.wait_ge(slots_stored, 16 * (len(PARTS) - 1))
        pool.wait_ge(tails_ready, 1)
        for j in range(NC):
            g.indirect_dma_start(out=agg_in[:, j, :], out_offset=None, in_=slot_rows[:, :],
                                 in_offset=bass.IndirectOffsetOnAxis(ap=taili[:, j:j + 1], axis=0)) \
                .then_inc(tails_in, 16)
        pool.wait_ge(flag_ready, 1)
        with pool.If(pool.value_load(flag[0:1, 0:1], min_val=0, max_val=1) > 0):
            pool.wait_ge(hist_used, OHB)
            g.memset(earlier, 1.0).then_inc(gen_zero, 1)
            pool.wait_ge(gen_zero, 1)
            g.affine_select(out=earlier, in_=earlier, compare_op=ALU.is_gt, fill=0.0, base=0, pattern=[[-1, P]],
                            channel_multiplier=1).then_inc(gen_mask, 1)
            pool.wait_ge(gen_state, 16)
            with pool.Fori(0, EC) as step:
                pool.wait_ge(gen_idx, step + 1)
                pool.sem_inc(gen_tick)
                for n, (row, table, col) in enumerate(((src_row, node_rows, 1), (dst_row, node_rows, 2),
                                                       (old_row, state_rows, 2))):
                    g.indirect_dma_start(out=row, out_offset=None, in_=table[:, :],
                                         in_offset=bass.IndirectOffsetOnAxis(ap=gi[:, col:col + 1], axis=0)) \
                        .then_inc(gen_in[n], 16)
                pool.wait_ge(gen_row, step + 1)
                pool.sem_inc(gen_tick)
                g.indirect_dma_start(out=state_rows[:, :],
                                     out_offset=bass.IndirectOffsetOnAxis(ap=gi[:, 3:4], axis=0), in_=new_row,
                                     in_offset=None, bounds_check=NODES - 1, oob_is_err=False).then_inc(gen_written, 16)
                pool.wait_ge(gen_written, 16 * step + 16)
                pool.sem_inc(gen_tick)
        pool.wait_ge(gate_ready, 1)
        pool.wait_ge(y_copied, 32)
        js = slice(OUT_PARTS[-2], NC)
        for e in range(EXPERTS):
            g.tensor_tensor(yexp[:, e, js, :], yexp[:, e, js, :], wide(fin[:, 3, js, e], E), ALU.mult).then_inc(pool_, t.up())
        for e in range(EXPERTS):
            pool.wait_ge(pool_, t.n - (3 if e == 0 else 0))
            g.tensor_tensor(xin[:, js, :], xin[:, js, :], yexp[:, e, js, :], ALU.add) \
                .then_inc(*((out_last_ready, 1) if e == 3 else (pool_, t.up())))

    @block.scalar
    def _(act):
        a_ = nc.scalar
        t = Tally(act_)
        for dst, src in loads:
            act.dma_start(dst, src, allow_slow_non_contiguous=True).then_inc(params_in, 16)

        def square(n):
            a, m = groups[n]
            act.wait_ge(centered, n + 1)
            if n >= 2:
                act.wait_ge(sumsq, n - 1)
            a_.activation(v3(squares[n % 2][:, 0:m * E], E), tiles[:, a:a + m, :], ACT.Square).then_inc(squared, 1)

        def copy_turned(n, dst):
            act.wait_ge(turned, n + 1)
            a_.activation(dst, v3(bank[n % 2][:, :], P), ACT.Copy).then_inc(copied, 1)

        def copy_tile(n):
            if n >= 2:
                act.wait_ge(projected, 4 * (n - 1) if n - 2 < 4 else (NX + NCP if n - 2 == 4 else NX + NCP + n - 6))
            copy_turned(n, tT[:, n % 2])

        def sigmoid(n):
            act.wait_ge(projected, n + 1)
            ps = project_bank(n)
            if n < NX:
                a_.activation(sig[:, 2 * n:2 * n + 2, :], v3(ps[:, 0:6 * E], 3 * E)[:, :, E:3 * E], ACT.Sigmoid) \
                    .then_inc(sigmoided, 1)
            else:
                if n >= NX + 2:
                    act.wait_ge(bank_read, n - 1)
                p_ = C if n < NX + NCP else P
                a_.activation(psig[0:p_, n % 2], v3(ps[0:p_, :], E)[:, :, C:E], ACT.Sigmoid).then_inc(sigmoided, 1)

        square(0)
        square(1)
        act.wait_ge(keys_ready, 1)
        a_.activation(yscratch, work, ACT.Sign, accum_out=counts[:, 0:1]).then_inc(keys_counted, 1)
        act.wait_ge(scratch_free, 1)
        act.wait_ge(keys_counted, 1)
        a_.activation(yscratch, clamped, ACT.Sign, accum_out=counts[:, 3:4]).then_inc(keys_counted, 1)
        act.wait_ge(consts, 1)
        act.wait_ge(sumsq, 2)
        a_.activation(xr[:, 0], tssq[:, 0:XT], ACT.Sqrt, bias=eps[:, 0:1], scale=1.0 / E).then_inc(std_x, 1)
        act.wait_ge(var2_x, 1)
        a_.activation(xr[:, 3], xr[:, 2], ACT.Sqrt, bias=eps[:, 1:2]).then_inc(std2_x, 1)
        act.wait_ge(scratch_free, 1)
        for n in range(2, len(groups)):
            square(n)
            if n == 2:
                copy_tile(0)
                copy_tile(1)
            else:
                if n in (5, 7):
                    copy_tile((n - 1) // 2)
                for m in range(2):
                    sigmoid(2 * (n - 3) + m)
        act.wait_ge(sumsq, len(groups))
        a_.activation(tstd[:, XT:TILES], tssq[:, XT:TILES], ACT.Sqrt, bias=eps[:, 1:2], scale=1.0 / E) \
            .then_inc(std_rest, 1)
        copy_tile(4)
        copy_tile(5)

        def pair_bank(n):
            sigmoid(n)
            k = n - NX - NCP
            if -1 <= k < NPR - 2:
                copy_tile(k + 7)

        for n in range(NX, EARLY):
            pair_bank(n)
        n = 5 + NPR
        for m in range(SHOWS):
            act.wait_ge(shown, m + 1)
            if m >= 4:
                act.wait_ge(owned_ready, m - 3)
            if m == 0:
                act.wait_ge(digits_ready, 1)
            a_.activation(bcast[:, m % 4], bank[4 + m % 2][:, 0:RPG * SLOTS], ACT.Copy).then_inc(shown_copied, 1)
            if m % 3 == 0 and EARLY + m // 3 < NX + NCP + NPR:
                pair_bank(EARLY + m // 3)
            elif m == AT_TURN_AB:
                for b in range(2):
                    copy_turned(n + b, abT[:, 4 * b:4 * b + 4, :])
            elif m == AT_CENTER + 2:
                act.wait_ge(nb_centered, 2)
                a_.activation(squares[0], nb.rearrange("p j c -> p (j c)"), ACT.Square).then_inc(nb_squared, 1)
            elif m == AT_SUMSQ + 2:
                act.wait_ge(nb_sumsq, 1)
                a_.activation(nstat[:, 2], nstat[:, 1], ACT.Sqrt, bias=eps[:, 1:2], scale=1.0 / C).then_inc(nb_std, 1)
            elif m == AT_TURN_NB + 1:
                act.wait_ge(projected, NX + NCP + NPR)
                for b in range(2):
                    copy_turned(n + 2 + b, tT[:, b])
        for b in range(2):
            act.wait_ge(xn_centered, 1)
            a_.activation(v3(squares[b], E), xn[:, 16 * b:16 * b + 16, :], ACT.Square).then_inc(xn_squared, 1)
        act.wait_ge(xn_sumsq, 1)
        a_.activation(nstat[:, 2], nstat[:, 1], ACT.Sqrt, bias=eps[:, 1:2], scale=1.0 / E).then_inc(xn_std, 1)
        for b in range(4):
            copy_turned(n + 4 + b, xnT[:, 4 * b:4 * b + 4, :])
        act.wait_ge(late_in, 16 * len(late_loads))
        act.wait_ge(xn_ready, 1)

        def gelu(f):
            act.wait_ge(hidden_done, f + 1)
            if f >= 2:
                act.wait_ge(y_done, f - 1)
            a_.activation(hid[:, f % 2].rearrange("p t n -> p (t n)"), bank[f % 2][:, :], ACT.Gelu,
                          bias=b1s[:, f // 8:f // 8 + 1]).then_inc(gelued, 1)

        def copy_y(f):
            e, q, b = f // 8, f // 4 % 2, f % 4
            act.wait_ge(y_done, f + 1)
            a_.activation(yexp[:, e, 8 * b + q:8 * b + 8:2, :], v3(bank[2 + f % 2][:, 0:4 * E], E), ACT.Copy) \
                .then_inc(y_copied, 1)

        for f in range(32):
            gelu(f)
            if f:
                copy_y(f - 1)
        copy_y(31)
        for n, (a, b) in enumerate(zip(PARTS, PARTS[1:])):
            act.wait_ge(exps_wanted, n + 1)
            for what in (carry, wgt):
                a_.activation(what[:, :, a:b], what[:, :, a:b], ACT.Exp).then_inc(exps_done, 1)
        act.wait_ge(flag_ready, 1)
        with act.If(act.value_load(flag[0:1, 0:1], min_val=0, max_val=1) > 0):
            with act.Fori(0, EC) as step:
                act.wait_ge(gen_exp, step + 1)
                a_.activation(expo, expo, ACT.Exp).then_inc(gen_exped, 1)
        act.wait_ge(fin_wanted, 1)
        a_.activation(fin[:, 0:3], fin[:, 0:3], ACT.Exp).then_inc(fin_done, 1)
        act.wait_ge(fin_wanted, 2)
        a_.activation(nstat[:, 2], nstat[:, 1], ACT.Sqrt, bias=eps[:, 1:2], scale=1.0 / HF).then_inc(fin_done, 1)
        act.wait_ge(fin_wanted, 3)
        a_.activation(fin[:, 3], fin[:, 3], ACT.Exp).then_inc(fin_done, 1)

    @block.tensor
    def _(pe):
        p_ = nc.tensor
        t = Tally(pe_)
        pe.wait_ge(consts, 1)
        pe.wait_ge(params_in, 16 * len(loads))
        p_.transpose(bank[6][:, 0:P], w_nat[:, :], ident[:, :])
        p_.transpose(bank[6][:, P:P + E], eg_nat[:, :], ident[0:E, 0:E])
        p_.transpose(bank[6][:, P + E:P + 2 * E], las_nat[:, :], ident[0:E, 0:E]).then_inc(weights_turned, 1)
        pe.wait_ge(weights_copied, 2)
        p_.matmul(bank[7][0:3, 0:3 * E], affine[0:E, 1:2].to_broadcast([E, 3]), wT[0:E, :], start=True, stop=True)
        p_.matmul(bank[7][0:3, 3 * E:4 * E], affine[0:C, 3:4].to_broadcast([C, 3]), lasT[0:C, :], start=True, stop=True).then_inc(bias_made, 1)

        def turn(n, sources):
            if n >= 2:
                pe.wait_ge(copied, n - 1)
            for m, src in enumerate(sources):
                mm = p_.transpose(bank[n % 2][:, P * m:P * (m + 1)], src, ident[:, :])
            mm.then_inc(turned, 1)

        def turn_tiles(n):
            pe.wait_ge(normed, n // 2 + 1 if n < 4 else (3 if n == 4 else 4 + (n - 5) // 2))
            turn(n, [tiles[:, 8 * n + 2 * m:8 * n + 2 * m + 2, :].rearrange("p t e -> p (t e)") for m in range(4)])

        def project_x(n, b, m):
            if n >= 4:
                pe.wait_ge(bank_read, n - 3)
            ps = project_bank(n)
            p_.matmul(v3(ps[:, 0:6 * E], 3 * E), ones_row[:, :],
                      zbias[:, 0:3 * E].unsqueeze(1).to_broadcast([3, 2, 3 * E]), start=True, stop=False,
                      skip_group_check=True)
            p_.matmul(ps[:, 0:6 * E], tT[:, b, m, :], bdz[:, :, :].rearrange("p a b -> p (a b)"), start=False, stop=True,
                      skip_group_check=True).then_inc(projected, 1)

        def project_comp(n, b, m):
            pe.wait_ge(bank_read, n - 3 if n < NX + 2 else n - 1)
            ps = project_bank(n)
            p_.matmul(v3(ps[0:C, :], E), ones_row[:, 0:C], cbias[:, :].unsqueeze(1).to_broadcast([3, 8, E]),
                      start=True, stop=False, skip_group_check=True)
            for r in range(4):
                mm = p_.matmul(v3(ps[0:C, :], E)[:, r:8:4, :], tT[:, b, m, C * r:C * (r + 1)], bdcp[:, :, :],
                               start=False, stop=True, skip_group_check=True)
            mm.then_inc(projected, 1)

        def project_protein(n, b):
            pe.wait_ge(bank_read, n - 1)
            ps = bank[2 + n % 2]
            p_.matmul(v3(ps[:, :], E), ones_row[:, :], pbias[:, :].unsqueeze(1).to_broadcast([3, 8, E]),
                      start=True, stop=False, skip_group_check=True)
            for m in range(4):
                mm = p_.matmul(ps[:, 2 * E * m:2 * E * (m + 1)], tT[:, b, m, :], bdp[:, :, :].rearrange("p a b -> p (a b)"),
                               start=False, stop=True, skip_group_check=True)
            mm.then_inc(projected, 1)

        turn_tiles(0)
        turn_tiles(1)
        pe.wait_ge(bias_copied, 2)
        for n in range(4):
            pe.wait_ge(copied, n + 1)
            for m in range(4):
                project_x(4 * n + m, n % 2, m)
            if n < 2:
                turn_tiles(n + 2)
        turn_tiles(4)
        turn_tiles(5)
        pe.wait_ge(copied, 5)
        for k in range(NCP):
            project_comp(NX + k, 0, k)
        turn_tiles(6)

        def protein(n):
            k = n - NX - NCP
            pe.wait_ge(copied, k + 6)
            project_protein(n, (k + 1) % 2)
            if k + 7 < 5 + NPR:
                turn_tiles(k + 7)

        for n in range(NX + NCP, EARLY):
            protein(n)
        n = 5 + NPR

        def blocks(g):
            ps = bank[6 + g // 4][:, P * (g % 4):P * (g % 4 + 1)]
            p_.matmul(ps, abT[:, g, :], bdc[:, g].rearrange("p c j -> p (c j)"), start=True, stop=False,
                      skip_group_check=True)
            for c in range(4):
                mm = p_.matmul(ps[:, NC * c:NC * (c + 1)], ppc[:, 4 * g + c, :], ab[:, :, 4 * g + c], start=False,
                               stop=True, skip_group_check=True)
            if g % 4 == 3:
                mm.then_inc(blocks_done, 1)

        def project_last(m):
            if m == 0:
                pe.wait_ge(copied, n + 4)
            k = NX + NCP + NPR + m
            pe.wait_ge(bank_read, k - 1)
            ps = bank[2 + k % 2]
            p_.matmul(v3(ps[:, :], E), ones_row[:, :], zbias[:, 3 * E:4 * E].unsqueeze(1).to_broadcast([3, 8, E]),
                      start=True, stop=False, skip_group_check=True)
            for h in range(2):
                g = 2 * m + h
                mm = p_.matmul(ps[:, 4 * E * h:4 * E * (h + 1)], tT[:, g // 4, g % 4, :],
                               bdlas[:, :, :].rearrange("p a b -> p (a b)"), start=False, stop=True, skip_group_check=True)
            mm.then_inc(projected, 1)

        for m in range(SHOWS):
            if m == 0:
                pe.wait_ge(digits_ready, 1)
            if m < 2:
                pe.wait_ge(bank_read, NX - 1 + m)
            else:
                pe.wait_ge(shown_copied, m - 1)
            for r in range(RPG):
                row = RPG * m + r
                for d in range(3):
                    mm = p_.matmul(bank[4 + m % 2][:, SLOTS * r:SLOTS * (r + 1)],
                                   digit_id[:, d, row:row + 1].to_broadcast([P, P]), digits[:, d, :], start=(d == 0),
                                   stop=(d == 2), skip_group_check=True)
            mm.then_inc(shown, 1)
            if m % 3 == 0 and EARLY + m // 3 < NX + NCP + NPR:
                protein(EARLY + m // 3)
            elif m == AT_TURN_AB - 1:
                pe.wait_ge(masked_ab, 1)
                for b in range(2):
                    turn(n + b, [ab2[:, 4 * g:4 * g + 4, :].rearrange("p c k -> p (c k)")
                                 for g in range(4 * b, 4 * b + 4)])
            elif AT_BLOCKS <= m < AT_BLOCKS + 24 and (m - AT_BLOCKS) % 3 == 0:
                if m == AT_BLOCKS:
                    pe.wait_ge(bdc_ready, 1)
                    pe.wait_ge(masked_ab, 2)
                    pe.wait_ge(bank_read, NX + NCP + NPR)
                    pe.wait_ge(copied, n + 2)
                blocks((m - AT_BLOCKS) // 3)
            elif m == AT_TURN_NB:
                pe.wait_ge(nb_ready, 1)
                for b in range(2):
                    turn(n + 2 + b, [nb[:, 4 * g:4 * g + 4, :].rearrange("p j c -> p (j c)")
                                     for g in range(4 * b, 4 * b + 4)])
            elif m in AT_LAS:
                project_last(AT_LAS.index(m))
        for m in range(len(AT_LAS), NLAS):
            project_last(m)
        pe.wait_ge(xn_ready, 1)
        for b in range(4):
            turn(n + 4 + b, [xn[:, 8 * b + 2 * m:8 * b + 2 * m + 2, :].rearrange("p j e -> p (j e)") for m in range(4)])
        pe.wait_ge(late_in, 16 * len(late_loads))
        pe.wait_ge(copied, n + 8)
        pe.wait_ge(nb_centered, 2)
        for u in range(NC // 2):
            mm = p_.matmul(bank[6][:, 2 * HF * u:2 * HF * (u + 1)], xnT[:, u, :], wgat2[:, :, :].rearrange("p q f -> p (q f)"),
                           start=True, stop=True, skip_group_check=True)
        mm.then_inc(gat_done, 1)
        def hidden(f):
            e, q, b = f // 8, f // 4 % 2, f % 4
            if f >= 2:
                pe.wait_ge(gelued, f - 1)
            p_.matmul(bank[f % 2][:, :], w1s[E * q:E * (q + 1), e, :],
                      xnT[E * q:E * (q + 1), 4 * b:4 * b + 4, :].rearrange("p t n -> p (t n)"), start=True, stop=True) \
                .then_inc(hidden_done, 1)

        def expert_out(f):
            e = f // 8
            if f >= 2:
                pe.wait_ge(y_copied, f - 1)
            pe.wait_ge(gelued, f + 1)
            ps = bank[2 + f % 2]
            p_.matmul(v3(ps[:, 0:4 * E], E), ones_col[0:1, :], b2s[:, e, :].unsqueeze(1).to_broadcast([1, 4, E]),
                      start=True, stop=False, skip_group_check=True)
            for m in range(4):
                mm = p_.matmul(ps[:, E * m:E * (m + 1)], hid[:, f % 2, m, :], w2s[:, e, :], start=False, stop=True,
                               skip_group_check=True)
            mm.then_inc(y_done, 1)

        def histogram(b):
            pe.wait_ge(onehots_ready, b + 1)
            for c in range(OHC):
                mm = p_.matmul(bank[4][0:64, 0:64], onehot[:, b % 2, 0, :, c], onehot[:, b % 2, 1, :, c],
                               start=(b == 0 and c == 0), stop=(b == OHB - 1 and c == OHC - 1))
            mm.then_inc(hist_used, 1)

        pe.wait_ge(bank_read, NX + NCP + NPR + NLAS)
        hidden(0)
        for f in range(32):
            if f < 31:
                hidden(f + 1)
            expert_out(f)
        pe.wait_ge(shown_copied, SHOWS)
        for b in range(OHB):
            histogram(b)
        pe.wait_ge(missing_ready, 1)
        p_.matmul(bank[5][:, 0:1], ones_col[:, :], counts[:, 2:3], start=True, stop=False)
        p_.matmul(bank[5][:, 0:1], ones_col[0:64, :], counts[0:64, 4:5], start=False, stop=True).then_inc(missing_summed, 1)
        pe.wait_ge(flag_ready, 1)
        with pe.If(pe.value_load(flag[0:1, 0:1], min_val=0, max_val=1) > 0):
            pe.wait_ge(y_copied, 32)
            with pe.Fori(0, EC) as step:
                pe.wait_ge(gen_idx, step + 1)
                p_.matmul(bank[0][:, 0:P], dst1.to_broadcast([P, P]), ident[:, :], start=True, stop=True).then_inc(gen_same, 1)
                pe.wait_ge(gen_score, step + 1)
                for h in range(HEADS):
                    mm = p_.matmul(bank[1][:, P * h:P * (h + 1)], escore[:, h:h + 1].to_broadcast([P, P]), ident[:, :],
                                   start=True, stop=True)
                mm.then_inc(gen_others, 1)
                pe.wait_ge(gen_payload, step + 1)
                p_.matmul(bank[2][:, 0:HEADS + HF], same, payload, start=True, stop=True).then_inc(gen_summed, 1)

    @block.vector
    def _(dve):
        v = nc.vector
        t = Tally(vec)

        def total(n):
            a, m = groups[n]
            if n == 0:
                dve.wait_ge(x_in, 16)
            elif n == 2:
                dve.wait_ge(comp_in, 16)
            elif n > 2:
                dve.wait_ge(pp_in[n - 3], 16)
            src = xin[:, a:a + m, :] if a < XT else tiles[:, a:a + m, :]
            v.tensor_reduce(tsum[:, a:a + m], src, AX.X, ALU.add).then_inc(summed, 1)

        def total_sq(n):
            a, m = groups[n]
            dve.wait_ge(squared, n + 1)
            v.tensor_reduce(tssq[:, a:a + m], v3(squares[n % 2][:, 0:m * E], E), AX.X, ALU.add).then_inc(sumsq, 1)

        def settle():
            dve.wait_ge(vec, t.n)

        dve.wait_ge(edges_in, 32)
        v.tensor_scalar(plain_src, esrc, float(LAST), None, ALU.is_lt).then_inc(vec, t.up())
        v.scalar_tensor_tensor(ktmp, edst, float(NODES), esrc, ALU.mult, ALU.add).then_inc(vec, t.up())
        dve.wait_ge(vec, t.n - 1)
        v.scalar_tensor_tensor(plain, edst, float(NODES), plain_src, ALU.is_lt, ALU.mult).then_inc(vec, t.up())
        settle()
        v.scalar_tensor_tensor(work, ktmp, 1.0, plain, ALU.add, ALU.mult).then_inc(keys_ready, 1)
        dve.wait_ge(keys_ready, 1)
        v.scalar_tensor_tensor(plain, edst, float(NODES), plain, ALU.is_lt, ALU.subtract).then_inc(vec, t.up())
        settle()
        v.scalar_tensor_tensor(clamped, edst, 1.0, plain, ALU.add, ALU.mult).then_inc(scratch_free, 1)
        total(0)
        total(1)

        def compact(source, dest, width, chunks, take, first=None, between=None):
            for r in range(take // 8):
                for c in range(chunks):
                    if r:
                        dve.wait_ge(vec, t.n - chunks + 1)
                    v.max(dest[:, take * c + 8 * r:take * c + 8 * r + 8], source[:, width * c:width * (c + 1)]) \
                        .then_inc(vec, t.up())
                if between is not None:
                    between(2 * r)
                if r == 0 and first is not None:
                    first()
                if r < take // 8 - 1:
                    for c in range(chunks):
                        dve.wait_ge(vec, t.n - chunks + 1)
                        part = source[:, width * c:width * (c + 1)]
                        v.match_replace(part, dest[:, take * c + 8 * r:take * c + 8 * r + 8], part, 0.0) \
                            .then_inc(vec, t.up())
                    if between is not None:
                        between(2 * r + 1)
            settle()

        dve.wait_ge(keys_ready, 1)
        compact(work, cand1[:, :], CH1, NCH1, TAKE1, first=lambda: dve.wait_ge(keys_counted, 1))
        total_sq(0)
        total_sq(1)
        dve.wait_ge(std_x, 1)
        v.reciprocal(xr[:, 1], xr[:, 0]).then_inc(vec, t.up())
        settle()
        v.scalar_tensor_tensor(xr[:, 2], tssq[:, 0:XT], 1.0 / E, xr[:, 1], ALU.mult, ALU.mult).then_inc(vec, t.up())
        settle()
        v.tensor_tensor(xr[:, 2], xr[:, 2], xr[:, 1], ALU.mult).then_inc(var2_x, 1)
        dve.wait_ge(std2_x, 1)
        v.reciprocal(xr[:, 3], xr[:, 3]).then_inc(vec, t.up())
        settle()
        v.tensor_tensor(trstd[:, 0:XT], xr[:, 1], xr[:, 3], ALU.mult).then_inc(rstd, 1)
        dve.wait_ge(weights_turned, 1)
        v.tensor_copy(wT[:, :], bank[6][:, 0:3 * E]).then_inc(weights_copied, 1)
        v.tensor_copy(lasT[:, :], bank[6][:, 3 * E:4 * E]).then_inc(weights_copied, 1)
        dve.wait_ge(weights_copied, 2)
        dve.wait_ge(diagonals_zero, 5)
        v.tensor_scalar(wTs[:, :], wT[:, :], affine[:, 0:1], None, ALU.mult).then_inc(vec, t.up())
        for q in range(4):
            rows_q = slice(C * q, C * (q + 1))
            v.tensor_scalar(bdlas[rows_q, q, :], lasT[rows_q, :], affine[rows_q, 2:3], None, ALU.mult) \
                .then_inc(vec, t.up())
        settle()
        for q in range(2):
            half = slice(E * q, E * (q + 1))
            v.tensor_copy(bdz[half, q, :], wTs[half, :]).then_inc(vec, t.up())
            v.tensor_copy(v3(bdp[half, q, :], C), v3(wTs[half, 0:2 * E], E)[:, :, C:E]).then_inc(vec, t.up())
            v.tensor_copy(v3(bdcp[half, q, :], C), v3(wTs[half, 0:2 * E], E)[:, :, 0:C]).then_inc(vec, t.up())
        dve.wait_ge(bias_made, 1)
        v.tensor_tensor(bias1[:, :], bank[7][0:3, 0:4 * E], bias_in[:, :], ALU.add).then_inc(vec, t.up())
        settle()
        for k in range(3):
            part = parts[:, k % 2, :]
            v.tensor_copy(part, bias1[:, :]).then_inc(vec, t.up())
            settle()
            if k < 2:
                v.tensor_tensor(bias1[:, :], bias1[:, :], part, ALU.subtract).then_inc(vec, t.up())
            if k == 0:
                v.tensor_scalar(zbias[:, :], part, ident[0:3, 0:1], None, ALU.mult).then_inc(vec, t.up())
            else:
                v.scalar_tensor_tensor(zbias[:, :], part, ident[0:3, k:k + 1], zbias[:, :], ALU.mult, ALU.add) \
                    .then_inc(vec, t.up())
            settle()
        v.tensor_copy(v3(cbias[:, :], C), v3(zbias[:, 0:2 * E], E)[:, :, 0:C]).then_inc(bias_copied, 1)
        v.tensor_copy(v3(pbias[:, :], C), v3(zbias[:, 0:2 * E], E)[:, :, C:E]).then_inc(bias_copied, 1)
        def read_bank(n):
            dve.wait_ge(sigmoided, n + 1)
            ps = project_bank(n)
            if n < NX:
                v.tensor_tensor(ab[:, 2 * n:2 * n + 2, :], v3(ps[:, 0:6 * E], 3 * E)[:, :, 0:E], sig[:, 2 * n:2 * n + 2, 0:E],
                                ALU.mult).then_inc(bank_read, 1)
            elif n < NX + NCP:
                m = n - NX
                v.tensor_tensor(cpk[:, 8 * m:8 * m + 8, :], v3(ps[0:C, :], E)[:, :, 0:C], psig[0:C, n % 2], ALU.mult) \
                    .then_inc(bank_read, 1)
            else:
                m = n - NX - NCP
                v.tensor_tensor(ppc[:, :, 8 * m:8 * m + 8].rearrange("p c i -> p i c"), v3(ps[:, :], E)[:, :, 0:C],
                                psig[:, n % 2], ALU.mult).then_inc(bank_read, 1)

        for n in range(2, len(groups)):
            total(n)
            if n > 3:
                total_sq(n - 2)
            if n > 4:
                read_bank(2 * n - 10)
                read_bank(2 * n - 9)
        total_sq(len(groups) - 2)
        total_sq(len(groups) - 1)
        for n in range(NX - 4, NX):
            read_bank(n)
        dve.wait_ge(std_rest, 1)
        v.reciprocal(trstd[:, XT:TILES], tstd[:, XT:TILES]).then_inc(rstd, 1)

        def merge(source, dest, between):
            for r in range(SLOTS // 8):
                v.max(dest[:, 8 * r:8 * r + 8], source[:, :]).then_inc(vec, t.up())
                settle()
                if r < SLOTS // 8 - 1:
                    v.match_replace(source[:, :], dest[:, 8 * r:8 * r + 8], source[:, :], 0.0).then_inc(vec, t.up())
                between(r)
                settle()

        read_after = (5, 6, 7, 8, 10, 11, 13, 14, 16, 17, 19, 20)
        merge(cand1, sent, lambda r: read_bank(NX + read_after.index(r)) if r in read_after else None)
        v.tensor_copy(senti[:, 0], sent[:, :]).then_inc(vec, t.up())
        settle()
        for d, (shift, op1) in enumerate(((16, None), (8, 255), (0, 255))):
            v.tensor_scalar(senti[:, 1 + d % 2], senti[:, 0], shift, op1, ALU.arith_shift_right,
                            ALU.bypass if op1 is None else ALU.bitwise_and).then_inc(vec, t.up())
            settle()
            ins = v.tensor_copy(digits[:, d, :], senti[:, 1 + d % 2])
            ins.then_inc(digits_ready if d == 2 else vec, 1)
            if d < 2:
                t.up()

        def compound_diagonals():
            dve.wait_ge(bank_read, NX + NCP)
            for c4 in range(4):
                ins = v.tensor_copy(bdc[C * c4:C * (c4 + 1), :, c4, :], cpk[:, :, c4:C:4].rearrange("k j g -> k g j"))
                ins.then_inc(bdc_ready if c4 == 3 else vec, 1)
                if c4 < 3:
                    t.up()

        chan = [bank[6 + b][:, :].rearrange("p (c j) -> p j c", j=NC) for b in range(2)]

        def channel_sums():
            for b in range(2):
                dve.wait_ge(blocks_done, b + 1)
                v.tensor_reduce(nstat[:, b], chan[b], AX.X, ALU.add).then_inc(vec, t.up())
            settle()
            v.tensor_tensor(nstat[:, 0], nstat[:, 0], nstat[:, 1], ALU.add).then_inc(vec, t.up())

        def channel_center():
            settle()
            for b in range(2):
                v.scalar_tensor_tensor(nb[:, :, 16 * b:16 * b + 16], wide(nstat[:, 0], 16), -1.0 / C, chan[b], ALU.mult,
                                       ALU.add).then_inc(nb_centered, 1)

        def channel_squares():
            dve.wait_ge(nb_squared, 1)
            v.tensor_reduce(nstat[:, 1], v3(squares[0], C), AX.X, ALU.add).then_inc(nb_sumsq, 1)

        def channel_scale():
            dve.wait_ge(nb_std, 1)
            v.reciprocal(nstat[:, 3], nstat[:, 2]).then_inc(vec, t.up())
            settle()
            dve.wait_ge(nb_centered, 2)
            v.tensor_tensor(nb, nb, wide(nstat[:, 3], C), ALU.mult).then_inc(nb_ready, 1)

        def update(m):
            if m == 0:
                dve.wait_ge(masked_ab, 3)
            n = NX + NCP + NPR + m
            dve.wait_ge(projected, n + 1)
            js = slice(8 * m, 8 * m + 8)
            v.tensor_tensor(sig[:, js, 0:E], v3(bank[2 + n % 2][:, :], E), sig[:, js, E:2 * E], ALU.mult) \
                .then_inc(bank_read, 1)
            dve.wait_ge(bank_read, n + 1)
            v.tensor_tensor(xin[:, js, :], xin[:, js, :], sig[:, js, 0:E], ALU.add).then_inc(vec, t.up())

        def token_center():
            settle()
            v.tensor_reduce(nstat[:, 0], xin[:, :, :], AX.X, ALU.add).then_inc(vec, t.up())
            settle()
            v.scalar_tensor_tensor(xn[:, :, :], wide(nstat[:, 0], E), -1.0 / E, xin[:, :, :], ALU.mult, ALU.add) \
                .then_inc(xn_centered, 1)

        def token_squares(b):
            dve.wait_ge(xn_squared, b + 1)
            ins = v.tensor_reduce(nstat[:, 1, 16 * b:16 * b + 16], v3(squares[b], E), AX.X, ALU.add)
            ins.then_inc(xn_sumsq if b else vec, 1)
            if not b:
                t.up()

        def token_scale():
            dve.wait_ge(xn_std, 1)
            v.reciprocal(nstat[:, 3], nstat[:, 2]).then_inc(vec, t.up())
            settle()
            dve.wait_ge(xn_centered, 1)
            v.tensor_tensor(xn[:, :, :], xn[:, :, :], wide(nstat[:, 3], E), ALU.mult).then_inc(xn_ready, 1)

        def node_row_parts():
            dve.wait_ge(gat_done, 1)
            v.tensor_copy(rows[:, :, 0:HF], v3(bank[6][:, :], HF)).then_inc(vec, t.up())
            settle()
            for n in range(2):
                v.tensor_tensor(hatt[:, n], rows[:, :, 0:HF], att[:, n, :].unsqueeze(1).to_broadcast([P, NC, HF]), ALU.mult) \
                    .then_inc(vec, t.up())
            settle()
            v.tensor_reduce(rows[:, :, HF:ROW].rearrange("p j (s h) -> p s j h", s=2),
                            hatt.rearrange("p s j (h e) -> p s j h e", h=HEADS), AX.X, ALU.add).then_inc(rows_ready, 1)

        def pick(m):
            dve.wait_ge(shown_copied, m + 1)
            if m >= 2:
                dve.wait_ge(vec, t.n)
            v.scalar_tensor_tensor(owned[:, m % 2], bcast[:, m % 4], own[:, 1:2], bcast[:, m % 4], ALU.is_le, ALU.mult) \
                .then_inc(owned_ready, 1)

        def largest(m):
            dve.wait_ge(owned_ready, m + 1)
            for r in range(RPG):
                k = RPG * m + r
                v.max(coll[:, 8 * k:8 * k + 8], owned[:, m % 2, SLOTS * r:SLOTS * (r + 1)]).then_inc(vec, t.up())

        pick(0)
        for m in range(SHOWS):
            if m + 1 < SHOWS:
                pick(m + 1)
            largest(m)
            if m % 3 == 0 and EARLY + m // 3 < NX + NCP + NPR:
                read_bank(EARLY + m // 3)
            if m == 1:
                compound_diagonals()
            elif m == AT_SUM:
                channel_sums()
            elif m == AT_CENTER:
                channel_center()
            elif m == AT_SUMSQ:
                channel_squares()
            elif m == AT_SCALE:
                channel_scale()
        settle()

        def between_rounds(r):
            if r < NLAS:
                update(r)
            elif r == 4:
                token_center()
            elif r in (6, 7):
                token_squares(r - 6)

        compact(coll, cand2[:, :], CH2, NCH2, TAKE2, between=between_rounds)

        def local_index(a, b):
            settle()
            v.tensor_scalar(locali[:, 0, a:b], recv[:, a:b], own[:, 0:1], -1.0, ALU.subtract, ALU.max).then_inc(vec, t.up())
            settle()
            v.tensor_single_scalar(locali[:, 2, a:b], locali[:, 0, a:b], NODES - 1, ALU.bitwise_and).then_inc(idx_ready, 1)

        def between_merges(r):
            if r == 0:
                token_scale()
            elif r == PARTS[1] // 8:
                local_index(0, PARTS[1])
            elif r == AT_ROWS:
                node_row_parts()

        merge(cand2, recv, between_merges)
        local_index(PARTS[1], SLOTS)
        v.tensor_single_scalar(locali[:, 1], locali[:, 0], 12, ALU.arith_shift_right).then_inc(vec, t.up())
        v.tensor_scalar(local[:, :], locali[:, 0], 0.0, None, ALU.is_ge).then_inc(vec, t.up())
        settle()
        v.tensor_copy(tgt[:, :], locali[:, 1]).then_inc(vec, t.up())
        v.tensor_reduce(counts[:, 1:2], local[:, :], AX.X, ALU.add).then_inc(vec, t.up())
        settle()
        v.tensor_tensor(counts[:, 2:3], counts[:, 0:1], counts[:, 1:2], ALU.subtract).then_inc(vec, t.up())
        dve.wait_ge(keys_counted, 2)
        settle()
        v.tensor_tensor(counts[:, 2:3], counts[:, 2:3], counts[:, 3:4], ALU.add).then_inc(vec, t.up())
        every_j = tgt[:, :].unsqueeze(1).to_broadcast([P, NC, SLOTS])
        v.tensor_tensor(seg, every_j, wide(iota_j[:, :], SLOTS), ALU.is_ge).then_inc(vec, t.up())
        settle()
        v.tensor_reduce(cum[:, 0:NC], seg, AX.X, ALU.add).then_inc(vec, t.up())
        settle()
        v.tensor_tensor(present[:, :], cum[:, 0:NC], cum[:, 1:NC + 1], ALU.is_gt).then_inc(vec, t.up())
        v.tensor_scalar(tailf[:, :], cum[:, 0:NC], -1.0, 0.0, ALU.add, ALU.max).then_inc(vec, t.up())
        v.tensor_tensor(seg, every_j, wide(iota_j[:, :], SLOTS), ALU.is_equal).then_inc(vec, t.up())
        settle()
        v.tensor_scalar(taili[:, :], tailf[:, :], own[:, 2:3], None, ALU.add).then_inc(tails_ready, 1)
        dve.wait_ge(rows_ready, 1)
        for h in range(HEADS):
            v.tensor_tensor(segd, seg, wide(rows[:, :, HF + HEADS + h], SLOTS), ALU.mult).then_inc(vec, t.up())
            settle()
            v.tensor_reduce(dslot[:, h], segd.rearrange("p j l -> p l j"), AX.X, ALU.add).then_inc(vec, t.up())
            settle()
        v.memset(head[:, 0:1], 1.0).then_inc(masks_done, 1)
        v.tensor_tensor(head[:, 1:SLOTS], tgt[:, 1:SLOTS], tgt[:, 0:SLOTS - 1], ALU.not_equal).then_inc(vec, t.up())
        settle()
        dve.wait_ge(masks_done, 1)
        v.tensor_scalar(reset[:, :], head[:, :], NONE, None, ALU.mult).then_inc(vec, t.up())
        settle()
        v.tensor_scalar(head[:, :], head[:, :], -1.0, 1.0, ALU.mult, ALU.add).then_inc(vec, t.up())
        compact(clamped, ccand, CH3, NCH3, TAKE3)
        v.tensor_scalar(cidx, ccand, -1.0, None, ALU.add).then_inc(vec, t.up())
        settle()
        for digit, (op, by) in ((hi16, (ALU.arith_shift_right, 6)), (lo16, (ALU.bitwise_and, 63))):
            v.tensor_single_scalar(cdigit, cidx, by, op).then_inc(vec, t.up())
            settle()
            v.tensor_copy(digit, cdigit).then_inc(vec, t.up())
            settle()
        def onehots(b):
            if b >= 2:
                dve.wait_ge(hist_used, b - 1)
            for h, val in enumerate((hi16, lo16)):
                for k in range(64):
                    ins = v.tensor_scalar(onehot[:, b % 2, h, k, :], val[:, OHC * b:OHC * (b + 1)], float(k), None,
                                          ALU.is_equal)
            ins.then_inc(onehots_ready, 1)

        def scan_part(n):
            a, b = PARTS[n], PARTS[n + 1]
            length = b - a
            first = 1 if n == 0 else 0
            dve.wait_ge(gathered[n], 16 * length)
            e_, c_ = wgt[:, :, a:b], carry[:, :, a:b]
            rmax = gath[:, :, HF + HEADS:ROW].rearrange("p l h -> p h l")
            v.tensor_tensor(e_, gath[:, a:b, HF:HF + HEADS].rearrange("p l h -> p h l"), dslot[:, :, a:b], ALU.add) \
                .then_inc(vec, t.up())
            settle()
            v.scalar_tensor_tensor(e_, e_, 0.2, e_, ALU.mult, ALU.max).then_inc(vec, t.up())
            settle()
            for h in range(HEADS):
                v.tensor_tensor_scan(rmax[:, h, a:b], reset[:, a:b], e_[:, h], NONE if n == 0 else rmax[:, h, a - 1:a],
                                     ALU.add, ALU.max).then_inc(vec, t.up())
            if n == 0:
                v.memset(carry[:, :, 0:1], 0.0).then_inc(vec, t.up())
            settle()
            v.tensor_tensor(carry[:, :, a + first:b], rmax[:, :, a + first - 1:b - 1], rmax[:, :, a + first:b], ALU.subtract) \
                .then_inc(vec, t.up())
            v.tensor_tensor(e_, e_, rmax[:, :, a:b], ALU.subtract).then_inc(vec, t.up())
            settle()
            v.tensor_scalar(c_, c_, 0.0, None, ALU.min).then_inc(exps_wanted, 1)
            dve.wait_ge(exps_done, 2 * n + 2)
            v.tensor_tensor(c_, c_, head[:, a:b].unsqueeze(1).to_broadcast([P, HEADS, length]), ALU.mult) \
                .then_inc(vec, t.up())
            msg = gath[:, a:b, 0:HF].rearrange("p l (h e) -> p l h e", h=HEADS)
            v.tensor_tensor(msg, msg, e_.rearrange("p h l -> p l h").unsqueeze(3).to_broadcast([P, length, HEADS, EXPERTS]),
                            ALU.mult).then_inc(vec, t.up())
            settle()
            for f in range(HF + HEADS):
                h = f // EXPERTS if f < HF else f - HF
                terms = gath[:, a:b, f] if f < HF else e_[:, h]
                v.tensor_tensor_scan(gath[:, a:b, f], c_[:, h], terms, 0.0 if n == 0 else gath[:, a - 1:a, f],
                                           ALU.mult, ALU.add).then_inc(vec, t.up())
            settle()
            v.engine_nop().then_inc(slots_ready, 1)

        for b in range(OHB):
            if b in SCAN_BEFORE:
                scan_part(SCAN_BEFORE.index(b))
            onehots(b)
        dve.wait_ge(hist_used, OHB)
        v.tensor_copy(histo[:, :], bank[4][0:64, 0:64]).then_inc(hist_copied, 1)
        dve.wait_ge(hist_copied, 1)
        v.tensor_reduce(nstat[0:64, 0, 0:1], histo[:, :], AX.X, ALU.add).then_inc(vec, t.up())
        settle()
        v.tensor_scalar(counts[0:64, 4:5], nstat[0:64, 0, 0:1], -1.0, None, ALU.mult).then_inc(missing_ready, 1)
        dve.wait_ge(missing_summed, 1)
        v.tensor_scalar(flag[:, :], bank[5][:, 0:1], -1.0 if force_general else 0.5, None, ALU.is_gt).then_inc(flag_ready, 1)

        def own_scores(count):
            a_dst = rows[:, :, HF + HEADS:ROW]
            v.tensor_tensor(fin[:, 1], rows[:, :, HF:HF + HEADS], a_dst, ALU.add).then_inc(count.sem, count.up())
            v.tensor_tensor(fin[:, 2], a_dst, last_row[:, HF:HF + HEADS].unsqueeze(1).to_broadcast([P, NC, HEADS]), ALU.add) \
                .then_inc(count.sem, count.up())
            v.tensor_scalar(nstat[:, 4], nclamp[:, :], 0.5, NONE, ALU.is_lt, ALU.mult).then_inc(count.sem, count.up())
            v.tensor_scalar(nstat[:, 5], present[:, :], -1.0, -NONE, ALU.add, ALU.mult).then_inc(count.sem, count.up())
            dve.wait_ge(count.sem, count.n)
            v.scalar_tensor_tensor(fin[:, 1:3], fin[:, 1:3], 0.2, fin[:, 1:3], ALU.mult, ALU.max).then_inc(count.sem, count.up())
            dve.wait_ge(count.sem, count.n)
            v.tensor_tensor(fin[:, 2], fin[:, 2], wide(nstat[:, 4], HEADS), ALU.add).then_inc(count.sem, count.up())
            dve.wait_ge(count.sem, count.n)
            v.tensor_tensor(fin[:, 3], fin[:, 1], fin[:, 2], ALU.max).then_inc(count.sem, count.up())
            dve.wait_ge(count.sem, count.n)

        dve.wait_ge(late_in, 16 * len(late_loads))
        v.tensor_scalar(gat_aff[:, 1], gat_aff[:, 1], 1.0 / HEADS, None, ALU.mult).then_inc(vec, t.up())
        v.tensor_reduce(beta_mean[:, :], gat_aff[:, 2].rearrange("p (h e) -> p e h", h=HEADS), AX.X, ALU.add) \
            .then_inc(vec, t.up())
        settle()
        v.tensor_scalar(beta_mean[:, :], beta_mean[:, :], 1.0 / HEADS, None, ALU.mult).then_inc(vec, t.up())
        dve.wait_ge(last_in, 16)
        dve.wait_ge(clamped_in, 16)
        own_scores(t)
        dve.wait_ge(tails_in, 16 * NC)
        with dve.If(dve.value_load(flag[0:1, 0:1], min_val=0, max_val=1) > 0):
            n0 = Tally(gen_steps)
            v.memset(agg_in[:, :, 0:HF + HEADS], 0.0).then_inc(gen_steps, n0.up())
            v.memset(present[:, :], 1.0).then_inc(gen_steps, n0.up())
            dve.wait_ge(gen_steps, n0.n)
            v.memset(agg_in[:, :, HF + HEADS:ROW], NONE).then_inc(gen_blank, 1)
            dve.wait_ge(gen_edges, 32)
            v.tensor_scalar(gen_plain, gen_src, float(LAST), None, ALU.min).then_inc(gen_steps, n0.up())
            dve.wait_ge(gen_steps, n0.n)
            v.scalar_tensor_tensor(gen_keys, gen_dst, float(NODES), gen_plain, ALU.mult, ALU.add) \
                .then_inc(gen_steps, n0.up())
            dve.wait_ge(gen_steps, n0.n)
            v.tensor_scalar(gen_plain, gen_dst, float(NODES), None, ALU.is_lt).then_inc(gen_steps, n0.up())
            dve.wait_ge(gen_steps, n0.n)
            v.memset(nclamp[:, :], 0.0).then_inc(gen_steps, n0.up())
            v.scalar_tensor_tensor(gen_keys, gen_keys, 1.0, gen_plain, ALU.add, ALU.mult).then_inc(gen_steps, n0.up())
            dve.wait_ge(gen_steps, n0.n)
            dve.wait_ge(gen_mask, 1)
            base, per_step = n0.n, 22
            with dve.Fori(0, EC) as step:
                k = Tally(gen_steps)

                def settled():
                    dve.wait_ge(gen_steps, step * per_step + (base + k.n))

                v.tensor_copy(key1, gen_keys[:, bass.ds(step, 1)]).then_inc(gen_steps, k.up())
                settled()
                v.tensor_scalar(gi[:, 0:1], key1, -1.0, None, ALU.add).then_inc(gen_steps, k.up())
                v.tensor_scalar(valid1, key1, 0.0, None, ALU.is_gt).then_inc(gen_steps, k.up())
                settled()
                v.tensor_single_scalar(gi[:, 1:2], gi[:, 0:1], NODES - 1, ALU.bitwise_and).then_inc(gen_steps, k.up())
                v.tensor_scalar(gi[:, 2:3], gi[:, 0:1], 12, NODES - 1, ALU.arith_shift_right, ALU.bitwise_and) \
                    .then_inc(gen_steps, k.up())
                settled()
                v.scalar_tensor_tensor(dst1, gi[:, 2:3], 1.0, valid1, ALU.add, ALU.mult).then_inc(gen_steps, k.up())
                settled()
                v.tensor_scalar(dst1, dst1, -1.0, None, ALU.add).then_inc(gen_idx, 1)
                for n in range(3):
                    dve.wait_ge(gen_in[n], 16 * step + 16)
                v.tensor_tensor(escore, src_row[:, HF:HF + HEADS], dst_row[:, HF + HEADS:ROW], ALU.add) \
                    .then_inc(gen_steps, k.up())
                settled()
                v.scalar_tensor_tensor(escore, escore, 0.2, escore, ALU.mult, ALU.max).then_inc(gen_score, 1)
                dve.wait_ge(gen_same, step + 1)
                v.tensor_scalar(same, bank[0][:, 0:P], dst1, None, ALU.is_equal).then_inc(gen_steps, k.up())
                settled()
                v.tensor_scalar(notsame, same, -1.0, -NONE, ALU.add, ALU.mult).then_inc(gen_steps, k.up())
                v.tensor_tensor(first_of, same, earlier, ALU.mult).then_inc(gen_steps, k.up())
                dve.wait_ge(gen_others, step + 1)
                v.tensor_tensor(others, v3(bank[1][:, :], P), same.unsqueeze(1).to_broadcast([P, HEADS, P]), ALU.mult) \
                    .then_inc(gen_steps, k.up())
                settled()
                v.tensor_tensor(others, others, notsame.unsqueeze(1).to_broadcast([P, HEADS, P]), ALU.add) \
                    .then_inc(gen_steps, k.up())
                v.tensor_reduce(rank1, first_of, AX.X, ALU.add).then_inc(gen_steps, k.up())
                settled()
                v.tensor_reduce(emax, others, AX.X, ALU.max).then_inc(gen_steps, k.up())
                settled()
                v.tensor_tensor(new_row[:, HF + HEADS:ROW], emax, old_row[:, HF + HEADS:ROW], ALU.max).then_inc(gen_steps, k.up())
                settled()
                v.tensor_tensor(expo[:, 0], escore, new_row[:, HF + HEADS:ROW], ALU.subtract).then_inc(gen_steps, k.up())
                v.tensor_tensor(expo[:, 1], old_row[:, HF + HEADS:ROW], new_row[:, HF + HEADS:ROW], ALU.subtract) \
                    .then_inc(gen_exp, 1)
                v.scalar_tensor_tensor(write1, rank1, 0.5, valid1, ALU.is_lt, ALU.mult).then_inc(gen_steps, k.up())
                dve.wait_ge(gen_exped, step + 1)
                settled()
                v.tensor_scalar(payload[:, HF:], expo[:, 0], valid1, None, ALU.mult).then_inc(gen_steps, k.up())
                v.tensor_scalar(write1, write1, -2.0 * NODES, 2.0 * NODES, ALU.mult, ALU.add).then_inc(gen_steps, k.up())
                settled()
                v.tensor_tensor(payload[:, 0:HF].rearrange("p (h e) -> p h e", h=HEADS),
                                src_row[:, 0:HF].rearrange("p (h e) -> p h e", h=HEADS), wide(payload[:, HF:], EXPERTS),
                                ALU.mult).then_inc(gen_payload, 1)
                v.tensor_tensor(gi[:, 3:4], write1, gi[:, 2:3], ALU.add).then_inc(gen_steps, k.up())
                v.tensor_tensor(old_row[:, HF:HF + HEADS], old_row[:, HF:HF + HEADS], expo[:, 1], ALU.mult) \
                    .then_inc(gen_steps, k.up())
                old = old_row[:, 0:HF].rearrange("p (h e) -> p h e", h=HEADS)
                v.tensor_tensor(old, old, wide(expo[:, 1], EXPERTS), ALU.mult).then_inc(gen_steps, k.up())
                settled()
                dve.wait_ge(gen_summed, step + 1)
                v.tensor_tensor(new_row[:, 0:HF + HEADS], old_row[:, 0:HF + HEADS], bank[2][:, 0:HF + HEADS], ALU.add) \
                    .then_inc(gen_row, 1)
                dve.wait_ge(gen_written, 16 * step + 16)
                assert k.n == per_step, k.n
            dve.wait_ge(gen_back, 16)
            own_scores(Tally(gen_scores))
        v.tensor_tensor(fin[:, 0], agg_in[:, :, HF + HEADS:ROW], wide(present[:, :], HEADS), ALU.mult).then_inc(vec, t.up())
        settle()
        v.tensor_tensor(fin[:, 0], fin[:, 0], wide(nstat[:, 5], HEADS), ALU.add).then_inc(vec, t.up())
        settle()
        v.tensor_tensor(fin[:, 3], fin[:, 3], fin[:, 0], ALU.max).then_inc(vec, t.up())
        settle()
        v.tensor_tensor(fin[:, 0:3], fin[:, 0:3], fin[:, 3].unsqueeze(1).to_broadcast([P, 3, NC, HEADS]), ALU.subtract) \
            .then_inc(fin_wanted, 1)
        dve.wait_ge(fin_done, 1)
        v.tensor_tensor(fin[:, 2], fin[:, 2], wide(nclamp[:, :], HEADS), ALU.mult).then_inc(vec, t.up())
        v.tensor_tensor(fin[:, 4], agg_in[:, :, HF:HF + HEADS], fin[:, 0], ALU.mult).then_inc(vec, t.up())
        settle()
        v.tensor_tensor(fin[:, 5], fin[:, 1], fin[:, 2], ALU.add).then_inc(vec, t.up())
        settle()
        v.scalar_tensor_tensor(fin[:, 5], fin[:, 5], 1e-16, fin[:, 4], ALU.add, ALU.add).then_inc(vec, t.up())
        settle()
        v.reciprocal(fin[:, 6], fin[:, 5]).then_inc(vec, t.up())
        settle()
        v.tensor_tensor(fin[:, 0:3], fin[:, 0:3], fin[:, 6].unsqueeze(1).to_broadcast([P, 3, NC, HEADS]), ALU.mult) \
            .then_inc(vec, t.up())
        settle()

        def heads(ap):
            return ap.rearrange("p j (h e) -> p j h e", h=HEADS)

        def per_head(n):
            return fin[:, n].unsqueeze(3).to_broadcast([P, NC, HEADS, EXPERTS])

        msg_in = agg_in[:, :, 0:HF]
        v.tensor_tensor(heads(msg_in), heads(msg_in), per_head(0), ALU.mult).then_inc(vec, t.up())
        v.tensor_tensor(heads(hatt[:, 0]), heads(rows[:, :, 0:HF]), per_head(1), ALU.mult).then_inc(vec, t.up())
        v.tensor_tensor(heads(hatt[:, 1]), heads(last_row[:, 0:HF].unsqueeze(1).to_broadcast([P, NC, HF])), per_head(2),
                        ALU.mult).then_inc(vec, t.up())
        settle()
        agg = hatt[:, 0]

        def every_token(n):
            return gat_aff[:, n, :].unsqueeze(1).to_broadcast([P, NC, HF])

        for term in (msg_in, hatt[:, 1], every_token(0)):
            v.tensor_tensor(agg, agg, term, ALU.add).then_inc(vec, t.up())
            settle()
        v.tensor_reduce(nstat[:, 0], agg, AX.X, ALU.add).then_inc(vec, t.up())
        settle()
        v.scalar_tensor_tensor(agg, wide(nstat[:, 0], HF), -1.0 / HF, agg, ALU.mult, ALU.add).then_inc(vec, t.up())
        settle()
        v.tensor_tensor(hatt[:, 1], agg, agg, ALU.mult).then_inc(vec, t.up())
        settle()
        v.tensor_reduce(nstat[:, 1], hatt[:, 1], AX.X, ALU.add).then_inc(fin_wanted, 1)
        v.tensor_tensor(msg_in, agg, every_token(1), ALU.mult).then_inc(vec, t.up())
        settle()
        v.tensor_reduce(fin[:, 1], msg_in.rearrange("p j (h e) -> p j e h", h=HEADS), AX.X, ALU.add).then_inc(vec, t.up())
        dve.wait_ge(fin_done, 2)
        v.reciprocal(nstat[:, 3], nstat[:, 2]).then_inc(vec, t.up())
        settle()
        score, top, gate, sel = fin[:, 2], nstat[:, 0], fin[:, 3], fin[:, 5]
        v.tensor_tensor(score, fin[:, 1], wide(nstat[:, 3], EXPERTS), ALU.mult).then_inc(vec, t.up())
        settle()
        v.tensor_tensor(score, score, beta_mean[:, :].unsqueeze(1).to_broadcast([P, NC, EXPERTS]), ALU.add) \
            .then_inc(vec, t.up())
        settle()
        mine = score.unsqueeze(3).to_broadcast([P, NC, EXPERTS, EXPERTS])
        other = score.unsqueeze(2).to_broadcast([P, NC, EXPERTS, EXPERTS])
        larger, equal = heads(hatt[:, 0]), heads(hatt[:, 1])
        v.tensor_tensor(larger, other, mine, ALU.is_gt).then_inc(vec, t.up())
        v.tensor_tensor(equal, other, mine, ALU.is_equal).then_inc(vec, t.up())
        v.tensor_reduce(top, score, AX.X, ALU.max).then_inc(vec, t.up())
        settle()
        v.tensor_tensor(equal, equal, before[:, :, :].unsqueeze(1).to_broadcast([P, NC, EXPERTS, EXPERTS]), ALU.mult) \
            .then_inc(vec, t.up())
        v.tensor_tensor(gate, score, wide(top, EXPERTS), ALU.subtract).then_inc(fin_wanted, 1)
        settle()
        v.tensor_tensor(larger, larger, equal, ALU.add).then_inc(vec, t.up())
        settle()
        v.tensor_reduce(fin[:, 4], larger, AX.X, ALU.add).then_inc(vec, t.up())
        settle()
        v.tensor_scalar(sel, fin[:, 4], 1.5, None, ALU.is_lt).then_inc(vec, t.up())
        settle()
        dve.wait_ge(fin_done, 3)
        v.tensor_tensor(gate, gate, sel, ALU.mult).then_inc(vec, t.up())
        settle()
        v.tensor_reduce(nstat[:, 1], gate, AX.X, ALU.add).then_inc(vec, t.up())
        settle()
        v.reciprocal(nstat[:, 3], nstat[:, 1]).then_inc(vec, t.up())
        settle()
        v.tensor_tensor(gate, gate, wide(nstat[:, 3], EXPERTS), ALU.mult).then_inc(gate_ready, 1)
        dve.wait_ge(y_copied, 32)
        dve.wait_ge(gate_ready, 1)
        for a, b in zip(OUT_PARTS, OUT_PARTS[1:-1]):
            js = slice(a, b)
            for e in range(EXPERTS):
                v.tensor_tensor(yexp[:, e, js, :], yexp[:, e, js, :], wide(gate[:, js, e], E), ALU.mult) \
                    .then_inc(vec, t.up())
            for e in range(EXPERTS):
                dve.wait_ge(vec, t.n - (3 if e == 0 else 0))
                v.tensor_tensor(xin[:, js, :], xin[:, js, :], yexp[:, e, js, :], ALU.add) \
                    .then_inc(*((out_ready, 1) if e == 3 else (vec, t.up())))

    ctx.close()


NAMES = ["x", "L0_conv_protein_pair", "L0_conv_compound_pair", "L0_conv_z_mask", "L0_conv_ln_w", "L0_conv_ln_b",
         "L0_conv_lnc_w", "L0_conv_lnc_b", "L0_conv_g1_w", "L0_conv_g1_b", "L0_conv_g2_w", "L0_conv_g2_b",
         "L0_conv_l1_w", "L0_conv_l1_b", "L0_conv_l2_w", "L0_conv_l2_b", "L0_conv_eg_w", "L0_conv_eg_b",
         "L0_conv_las_w", "L0_conv_las_b", "L0_ffn_W_gat", "L0_ffn_att_src", "L0_ffn_att_dst", "L0_ffn_b_gat",
         "L0_ffn_ln_gamma", "L0_ffn_ln_beta", "L0_ffn_W1", "L0_ffn_b1", "L0_ffn_W2", "L0_ffn_b2",
         "L0_ffn_edge_index"]


def program(nc, shapes, **options):
    args = [nc.dram_tensor(f"in_{n}", s, d, kind="ExternalInput").ap() for n, (s, d) in zip(NAMES, shapes)]
    out = nc.dram_tensor("out_0", (1, P, NC, E), F32, kind="ExternalOutput").ap()
    build(nc, *args, out, **options)


def kernel(**inputs):
    import concourse.bacc as bacc
    import numpy as np
    from concourse.bass_utils import run_bass_kernel_spmd

    nc = bacc.Bacc("TRN2", target_bir_lowering=False, num_devices=1)
    arrays = {f"in_{n}": np.ascontiguousarray(inputs[n]) for n in NAMES}
    program(nc, [(a.shape, mybir.dt.from_np(a.dtype)) for a in arrays.values()])
    r = run_bass_kernel_spmd(nc, [arrays], core_ids=[0])
    return r.results[0]["out_0"]
```

```python
from contextlib import ExitStack

import concourse.bass as bass
from concourse import mybir
from concourse.alu_op_type import AluOpType as ALU

F32 = mybir.dt.float32
BF16 = mybir.dt.bfloat16
I32 = mybir.dt.int32
ACT = mybir.ActivationFunctionType
AX = mybir.AxisListType

P = 128
NC = 32
E = 64
C = 32
NODES = P * NC
LAST = NODES - 1
HEADS, EXPERTS = 4, 4
HF = HEADS * EXPERTS
ROW = HF + 2 * HEADS
HIDDEN = 2 * E
EDGES = 262144
EC = EDGES // P
OWNED = NC * NODES
NONE = -1.0e30

CH1, TAKE1 = 128, 24
NCH1 = EC // CH1
W1 = NCH1 * TAKE1
SLOTS = 176
CH2, TAKE2 = 128, 40
Y2 = P * 8
NCH2 = Y2 // CH2
W2 = NCH2 * TAKE2
RPG = 2
FEATS, OWNER = 8, 5
RPT = P // FEATS
PENALTY = 2.0 ** 18
CH3, TAKE3 = 128, 48
NCH3 = EC // CH3
W3 = NCH3 * TAKE3
OHC = 128
OHB = W3 // OHC
WEIGH_FROM, WEIGH_EACH = 10, 12
HIST_AFTER = (23, 27)
EXPS_BEFORE = 28
DSLOT_AT = (4, 7, 10, 20)
PARTS = (0, 112, 152, SLOTS)
SOMETIMES = (160, 168)
OUT_PARTS = (0, 11, 21, NC)
SCAN_BEFORE = (3, 4, 4)

XT, CT = NC, NC * NC // P
TILES = XT + CT + P
GT = 16


class Tally:

    def __init__(self, sem):
        self.sem, self.n = sem, 0

    def up(self):
        self.n += 1
        return 1


def build(nc, x, pp, comp, zmask, ln_w, ln_b, lnc_w, lnc_b, g1_w, g1_b, g2_w, g2_b, l1_w, l1_b, l2_w, l2_b,
          eg_w, eg_b, las_w, las_b, W_gat, att_src, att_dst, b_gat, gamma, beta, W1_, b1, W2_, b2, edges, out,
          force_general=False):
    ctx = ExitStack()

    def sb(name, shape, dt=F32):
        return ctx.enter_context(nc.sbuf_tensor(name, shape, dt))

    def sem(name):
        return ctx.enter_context(nc.semaphore(name))

    node_rows = nc.dram_tensor("node_rows", (NODES, ROW), F32, kind="Internal").ap()
    slot_rows = nc.dram_tensor("slot_rows", (P * SLOTS, ROW), F32, kind="Internal").ap()
    feat_dram = nc.dram_tensor("feat_dram", (P, FEATS * SLOTS), BF16, kind="Internal").ap()
    hist_dram = nc.dram_tensor("hist_dram", (64, 64), F32, kind="Internal").ap()
    state_rows = nc.dram_tensor("state_rows", (NODES, ROW), F32, kind="Internal").ap()

    stage_a = sb("stage_a", [P, 16384])
    stage_b = sb("stage_b", [P, EXPERTS * NC * E])
    stage_c = sb("stage_c", [P, 6400])

    def carve(region, dt=F32):
        at = [0]

        def take(*shape):
            n = 1
            for d in shape:
                n *= d
            words = n if dt == F32 or dt == I32 else n // 2
            ap = region[:, at[0]:at[0] + words]
            at[0] += words
            assert at[0] <= region.shape[1]
            if dt != F32:
                ap = ap.bitcast(dt)
            if len(shape) == 1:
                return ap
            names = "abcd"[:len(shape)]
            sizes = {c: d for c, d in zip(names, shape)}
            return ap.rearrange(f"p ({' '.join(names)}) -> p {' '.join(names)}", **sizes)
        return take

    a1 = carve(stage_a)
    tiles = a1(TILES, E)
    ppc = a1(C, P)
    squares_a = a1(GT * E)
    seg = carve(stage_a, BF16)(NC, SLOTS)
    segd = carve(stage_a[:, NC * SLOTS // 2:])(2, NC, SLOTS)
    onehot = carve(stage_a, BF16)(2, 2, 64, OHC)
    a4 = carve(stage_a, I32)
    gen_dst, gen_src = a4(EC), a4(EC)
    gen_keys, gen_plain = (stage_a[:, n * EC:(n + 1) * EC] for n in (2, 3))
    a5 = carve(stage_a[:, 4 * EC:16384])
    same = a5(P)
    earlier = a5(P)
    others = a5(HEADS, P)
    notsame, first_of = a5(P), a5(P)
    src_row, dst_row, old_row, new_row = a5(ROW), a5(ROW), a5(ROW), a5(ROW)
    payload = a5(HEADS + HF)
    escore, emax, expo = a5(HEADS), a5(HEADS), a5(2, HEADS)
    key1, valid1, dst1, rank1, write1 = (a5(1) for _ in range(5))
    gi = carve(stage_a[:, 16384 - 8:16384], I32)(8)

    yscratch = stage_a[:, TILES * E:TILES * E + EC]
    ktmp, plain_src, plain, dst_next = (stage_b[:, n * EC:(n + 1) * EC] for n in range(4))
    dst_ok = ktmp
    b1_ = carve(stage_b)
    sig = b1_(NC, 2 * E)
    ab = b1_(NC, E)
    abT = b1_(8, P)
    nb = b1_(NC, C)
    ab2 = nb.rearrange("p j c -> p (j c)").rearrange("p (c k) -> p c k", k=NC)
    yexp = carve(stage_b)(EXPERTS, NC, E)

    edst, esrc = stage_c[:, 0:EC].bitcast(I32), stage_c[:, EC:2 * EC].bitcast(I32)
    gath = carve(stage_c)(SLOTS, ROW)
    c1_ = carve(stage_c)
    bcast = c1_(4, RPG * SLOTS)
    coll = c1_(Y2)
    keyi = carve(coll, I32)(5, SLOTS)
    c1b_ = carve(stage_c[:, 4 * RPG * SLOTS + Y2:SLOTS * ROW], BF16)
    feats = c1b_(FEATS, SLOTS)
    turned_feats = c1b_(P // RPT, SLOTS)
    clamped = carve(stage_c[:, SLOTS * ROW:6400])(EC)
    c2_ = carve(stage_c[:, SLOTS * ROW:6400])
    wgt = c2_(HEADS, SLOTS)
    carry = c2_(HEADS, SLOTS)
    c3_ = carve(stage_c[:, SLOTS * ROW:6400])
    agg_in = c3_(NC, ROW)
    fin = c3_(8, NC, HEADS)

    ident = sb("ident", [P, P])
    owner_w = sb("owner_w", [P, RPT, P], BF16)
    digit_w = sb("digit_w", [P, RPT], BF16)
    row_w = sb("row_w", [P, P], BF16)
    row_block = sb("row_block", [P, RPT])
    coef = sb("coef", [P, 6])
    feat_i = sb("feat_i", [P, 2], I32)
    ones_col = sb("ones_col", [P, P])
    iota_j = sb("iota_j", [P, NC])
    iota_i = sb("iota_i", [P, NC], I32)
    own_i = sb("own_i", [P, 1], I32)
    own = sb("own", [P, 1])
    eps = sb("eps", [P, 2])
    limits = sb("limits", [P, 3])
    zbias = sb("zbias", [3, 4 * E], BF16)
    pbias = sb("pbias", [3, E], BF16)
    cbias = sb("cbias", [3, E], BF16)
    parts = sb("parts", [3, 2, 4 * E], BF16)
    ones_row = sb("ones_row", [3, P], BF16)
    before = sb("before", [P, EXPERTS, EXPERTS])

    w_nat = sb("w_nat", [P, 2 * E])
    eg_nat = sb("eg_nat", [E, 2 * E])
    las_nat = sb("las_nat", [E, 4 * C])
    affine = sb("affine", [P, 4])
    bias_in = sb("bias_in", [3, 4 * E])
    wT = sb("wT", [P, 3 * E])
    wTs = sb("wTs", [P, 3 * E])
    bdz = sb("bdz", [P, 2, 3 * E])
    bdp = sb("bdp", [P, 2, E])
    bdcp = sb("bdcp", [P, 2, E])
    bdlas = sb("bdlas", [P, 4, E])
    lasT = sb("lasT", [P, E])
    bias1 = sb("bias1", [3, 4 * E])
    wgat2 = sb("wgat2", [P, 2, HF])
    att = sb("att", [P, 2, HF])
    gat_aff = sb("gat_aff", [P, 3, HF])
    beta_mean = sb("beta_mean", [P, EXPERTS])
    w1s = sb("w1s", [P, EXPERTS, HIDDEN])
    b1s = sb("b1s", [HIDDEN, EXPERTS])
    w2s = sb("w2s", [HIDDEN, EXPERTS, E])
    b2s = sb("b2s", [1, EXPERTS, E])
    mask = sb("mask", [P, NC])

    xin = sb("xin", [P, NC, E])
    stats = sb("stats", [P, 5 * TILES])
    tsum, tmean, tssq, tstd, trstd = (stats[:, n * TILES:(n + 1) * TILES] for n in range(5))
    xr = sb("xr", [P, 4, XT])
    tT = sb("tT", [P, 2, 4, P])
    psig = sb("psig", [P, 2, 8, C])
    cpk = sb("cpk", [C, NC, C])
    bdc = sb("bdc", [P, 8, 4, NC])
    nstat = sb("nstat", [P, 6, NC])
    xn = sb("xn", [P, NC, E])
    xnT = sb("xnT", [P, NC // 2, P])
    rows = sb("rows", [P, NC, ROW])
    last_row = sb("last_row", [P, ROW])

    number_i, square_i, high_i, low_i = (xnT[:, n, :].bitcast(I32) for n in range(4))
    work = xn[:, :, :].rearrange("p j e -> p (j e)")
    ccand = stats[:, 0:W3]
    cidx = work[:, W3:2 * W3].bitcast(I32)
    cdigit = work[:, 0:W3].bitcast(I32)
    hi16, lo16 = work[:, 2 * W3:5 * W3 // 2].bitcast(BF16), work[:, W3:3 * W3 // 2].bitcast(BF16)
    cand1 = sb("cand1", [P, W1])
    sent = sb("sent", [P, SLOTS])
    senti = sb("senti", [P, 3, SLOTS], I32)
    cand2 = cand1
    assert W2 <= W1
    recv = sb("recv", [P, SLOTS])
    local = sb("local", [P, SLOTS])
    locali = senti
    tgt = sb("tgt", [P, SLOTS])
    counts = sb("counts", [P, 5])
    flag = sb("flag", [P, 1], I32)
    more = sb("more", [P, len(SOMETIMES)])
    more_i = sb("more_i", [P, len(SOMETIMES)], I32)
    cum = sb("cum", [P, NC + 1])
    present = sb("present", [P, NC])
    tailf = sb("tailf", [P, NC])
    taili = sb("taili", [P, NC], I32)
    dslot = sb("dslot", [P, HEADS, SLOTS])
    head = sb("head", [P, SLOTS])
    reset = sb("reset", [P, SLOTS])
    histo = sb("histo", [64, 64])
    nclamp = sb("nclamp", [P, NC])

    hid = sb("hid", [P, 2, 4, P])
    squares = [squares_a, hid[:, :, :, :].rearrange("p b t n -> p (b t n)")]
    hatt = squares_a.rearrange("p (s j f) -> p s j f", s=2, j=NC)

    bank = [ctx.enter_context(nc.psum_tensor(f"bank{n}", [P, 512], F32)) for n in range(8)]

    vec, act_, pe_, pool_ = sem("vec"), sem("act"), sem("pe"), sem("pool")
    x_in, edges_in, comp_in, params_in = sem("x_in"), sem("edges_in"), sem("comp_in"), sem("params_in")
    pp_in = [sem(f"pp_in{n}") for n in range(P // GT)]
    consts = sem("consts")
    weights_turned, weights_copied, bias_made, bias_copied = sem("weights_turned"), sem("weights_copied"), \
        sem("bias_made"), sem("bias_copied")
    diagonals_zero = sem("diagonals_zero")
    summed, centered, squared, sumsq, normed = sem("summed"), sem("centered"), sem("squared"), sem("sumsq"), sem("normed")
    std_x, std_rest, rstd, var2_x, std2_x = sem("std_x"), sem("std_rest"), sem("rstd"), sem("var2_x"), sem("std2_x")
    turned, copied, projected, sigmoided, bank_read = sem("turned"), sem("copied"), sem("projected"), \
        sem("sigmoided"), sem("bank_read")
    scratch_free = sem("scratch_free")
    masked_ab, bdc_ready, blocks_done, nb_centered, nb_squared, nb_sumsq, nb_std, nb_ready = (
        sem(n) for n in ("masked_ab", "bdc_ready", "blocks_done", "nb_centered", "nb_squared", "nb_sumsq", "nb_std",
                         "nb_ready"))
    x1_ready, xn_centered, xn_squared, xn_sumsq, xn_std, xn_ready, gat_done, rows_ready, rows_stored, last_in = (
        sem(n) for n in ("x1_ready", "xn_centered", "xn_squared", "xn_sumsq", "xn_std", "xn_ready", "gat_done",
                         "rows_ready", "rows_stored", "last_in"))
    keys_ready, keys_counted, feats_ready, feats_stored, feats_in, shown, shown_copied, keys_taken = (
        sem(n) for n in ("keys_ready", "keys_counted", "feats_ready", "feats_stored", "feats_in", "shown", "shown_copied",
                         "keys_taken"))
    seg_ready, weighted, dslot_done = sem("seg_ready"), sem("weighted"), sem("dslot_done")
    more_ready, more_summed, more_known, gathered_more, last_gathered = (
        sem(n) for n in ("more_ready", "more_summed", "more_known", "gathered_more", "last_gathered"))
    clamped_parts = sem("clamped_parts")
    numbers, row_weights = sem("numbers"), sem("row_weights")
    missing_ready, missing_summed, flag_ready, idx_ready, tails_ready, head_started = (
        sem(n) for n in ("missing_ready", "missing_summed", "flag_ready", "idx_ready", "tails_ready", "head_started"))
    gathered = [sem(f"gathered{n}") for n in range(len(PARTS) - 1)]
    onehots_ready, hist_used, hist_copied, hist_stored, clamped_in = (
        sem(n) for n in ("onehots_ready", "hist_used", "hist_copied", "hist_stored", "clamped_in"))
    exps_wanted, exps_done, slots_ready, slots_stored, tails_in = (
        sem(n) for n in ("exps_wanted", "exps_done", "slots_ready", "slots_stored", "tails_in"))
    hidden_done, gelued, y_done, y_copied = sem("hidden_done"), sem("gelued"), sem("y_done"), sem("y_copied")
    gate_ready, out_last_ready = sem("gate_ready"), sem("out_last_ready")
    fin_wanted, fin_done, out_ready, out_stored = sem("fin_wanted"), sem("fin_done"), sem("out_ready"), sem("out_stored")

    groups = [(0, GT), (GT, GT), (XT, CT)] + [(XT + CT + GT * n, GT) for n in range(P // GT)]

    def v3(ap, inner):
        return ap.rearrange("p (a b) -> p a b", b=inner)

    def wide(ap, n):
        return ap.unsqueeze(2).to_broadcast([ap.shape[0], ap.shape[1], n])

    NX, NCP, NPR, NLAS = NC // 2, NC // 8, P // 8, NC // 8

    loads = [(w_nat[C * n:C * (n + 1), E * d:E * (d + 1)], w[:, :])
             for n, w in enumerate((l1_w, l2_w, g1_w, g2_w)) for d in range(2)]
    loads += [(eg_nat[:, E * d:E * (d + 1)], eg_w[:, :]) for d in range(2)]
    loads += [(las_nat[:, C * d:C * (d + 1)], las_w[:, :]) for d in range(4)]
    loads += [(affine[E * d:E * (d + 1), n:n + 1], w.unsqueeze(1)) for n, w in enumerate((ln_w, ln_b)) for d in range(2)]
    loads += [(affine[C * d:C * (d + 1), n + 2:n + 3], w.unsqueeze(1))
              for n, w in enumerate((lnc_w, lnc_b)) for d in range(4)]
    loads += [(bias_in[:, C * n:C * (n + 1)], w.partition_broadcast(3)) for n, w in enumerate((l1_b, l2_b, g1_b, g2_b))]
    loads += [(bias_in[:, 2 * E:3 * E], eg_b.partition_broadcast(3)), (bias_in[:, 3 * E:4 * E], las_b.partition_broadcast(3))]
    loads += [(mask[:, :], zmask.rearrange("a i j b -> (a i) (j b)"))]
    late_loads = [(wgat2[E * q:E * (q + 1), q, :], W_gat[:, :]) for q in range(2)]
    late_loads += [(att[:, n, :], a.rearrange("h e -> (h e)").partition_broadcast(P)) for n, a in enumerate((att_src, att_dst))]
    late_loads += [(gat_aff[:, n, :], a.partition_broadcast(P)) for n, a in enumerate((b_gat, gamma, beta))]
    late_loads += [(w1s[E * q:E * (q + 1), :, :], W1_.rearrange("e i f -> i e f")) for q in range(2)]
    late_loads += [(w2s[:, :, :], W2_.rearrange("e f o -> f e o")), (b1s[:, :], b1.rearrange("e f -> f e")),
                   (b2s[:, :, :], b2.rearrange("e o -> (e o)").unsqueeze(0).rearrange("a (e o) -> a e o", e=EXPERTS))]
    late_in = sem("late_in")

    gen_blank, gen_state, gen_edges, gen_idx, gen_score, gen_others, gen_exp, gen_exped, gen_payload = (
        sem(f"gen_{n}") for n in ("blank", "state", "edges", "idx", "score", "others", "exp", "exped", "payload"))
    gen_tick, gen_scores = sem("gen_tick"), sem("gen_scores")
    gen_in = [sem(f"gen_in{n}") for n in range(3)]
    gen_same, gen_summed, gen_row, gen_written, gen_mask, gen_steps, gen_back, gen_zero = (
        sem(f"gen_{n}") for n in ("same", "summed", "row", "written", "mask", "steps", "back", "zero"))

    SHOWS = P // RPG

    def project_bank(n):
        return bank[2 + n % 4 if n < NX else 2 + n % 2]

    EARLY = NX + NCP + 8
    BANK_EVERY, BLOCK_EVERY = 2, 2
    AT_TURN_AB, AT_BLOCKS, AT_SUM, AT_CENTER, AT_SUMSQ, AT_SCALE, AT_TURN_NB = 16, 17, 34, 36, 40, 44, 46

    AT_LAS = (48, 50, 52, 54)
    AT_UPDATE = (50, 52, 54, 56)
    AT_TOKENS, AT_TOKEN_SQUARES = 58, (61, 62)
    AT_TOKEN_SCALE, AT_ROWS = 0, 8
    INDEX_FIRST = 32

    block = ctx.enter_context(nc.Block())

    @block.sync
    def _(sp):
        sp.dma_start(edst, edges[1].rearrange("(p c) -> p c", p=P)).then_inc(edges_in, 16)
        sp.dma_start(esrc, edges[0].rearrange("(p c) -> p c", p=P)).then_inc(edges_in, 16)
        sp.dma_start(xin[:, :, :], x.rearrange("a i j e -> (a i) j e")).then_inc(x_in, 16)
        sp.dma_start(tiles[:, XT:XT + CT, :],
                     comp.rearrange("a j k e -> (a j k) e").rearrange("(t p) e -> p t e", p=P)).then_inc(comp_in, 16)
        for n in range(P // GT):
            sp.dma_start(tiles[:, XT + CT + GT * n:XT + CT + GT * (n + 1), :],
                         pp[0, GT * n:GT * (n + 1), :, :].rearrange("i k e -> k i e")).then_inc(pp_in[n], 16)
        for dst, src in loads[len(loads) // 2 + 3:]:
            sp.dma_start(dst, src, allow_slow_non_contiguous=True).then_inc(params_in, 16)
        sp.wait_ge(feats_ready, 1)
        sp.dma_start(feat_dram[:, :], feats.rearrange("p f l -> p (f l)")).then_inc(feats_stored, 16)
        sp.wait_ge(feats_stored, 16)
        sp.dma_start(turned_feats, feat_dram.rearrange("(t r) (f l) -> (r f) t l", r=RPT, f=FEATS)).then_inc(feats_in, 16)
        sp.wait_ge(rows_ready, 1)
        sp.dma_start(node_rows.rearrange("(p j) r -> p (j r)", p=P), rows[:, :, :].rearrange("p j r -> p (j r)")) \
            .then_inc(rows_stored, 16)
        sp.wait_ge(rows_stored, 16)
        sp.dma_start(last_row[:, :], node_rows[LAST, :].partition_broadcast(P)).then_inc(last_in, 16)
        for n, (a, b) in enumerate(zip(PARTS, PARTS[1:])):
            sp.wait_ge(slots_ready, n + 1)
            sp.dma_start(slot_rows.rearrange("(p l) r -> p l r", p=P)[:, a:b, :], gath[:, a:b, :]).then_inc(slots_stored, 16)
        sp.wait_ge(hist_copied, 1)
        sp.dma_start(hist_dram[:, :], histo[:, :]).then_inc(hist_stored, 16)
        sp.wait_ge(hist_stored, 16)
        sp.dma_start(nclamp[:, :], hist_dram.rearrange("a (b j) -> (a b) j", j=NC)).then_inc(clamped_in, 16)
        sp.wait_ge(flag_ready, 1)
        with sp.If(sp.value_load(flag[0:1, 0:1], min_val=0, max_val=1) > 0):
            sp.wait_ge(gen_blank, 1)
            sp.dma_start(gen_dst, edges[1].rearrange("(p c) -> p c", p=P)).then_inc(gen_edges, 16)
            sp.dma_start(gen_src, edges[0].rearrange("(p c) -> p c", p=P)).then_inc(gen_edges, 16)
            sp.dma_start(state_rows.rearrange("(p j) r -> p (j r)", p=P), agg_in.rearrange("p j r -> p (j r)")) \
                .then_inc(gen_state, 16)
            sp.wait_ge(gen_written, 16 * EC)
            sp.wait_ge(gen_state, 16)
            sp.dma_start(agg_in.rearrange("p j r -> p (j r)"), state_rows.rearrange("(p j) r -> p (j r)", p=P)) \
                .then_inc(gen_back, 16)
        for n, (a, b) in enumerate(zip(OUT_PARTS, OUT_PARTS[1:])):
            if b < NC:
                sp.wait_ge(out_ready, n + 1)
            else:
                sp.wait_ge(out_last_ready, 1)
            sp.dma_start(out[0, :, a:b, :], xin[:, a:b, :]).then_inc(out_stored, 16)
        sp.wait_ge(out_stored, 16 * (len(OUT_PARTS) - 1))

    @block.gpsimd
    def _(pool):
        g = nc.gpsimd
        t = Tally(pool_)
        g.iota(number_i, [[1, P]], base=0, channel_multiplier=0).then_inc(numbers, 1)
        g.iota(feat_i[:, 0:1], [[0, 1]], base=0, channel_multiplier=1).then_inc(numbers, 1)
        g.memset(wgat2[:, :, :], 0.0).then_inc(pool_, t.up())
        pool.wait_ge(pool_, t.n)
        for dst, src in late_loads:
            g.dma_start(dst, src, allow_slow_non_contiguous=True).then_inc(late_in, 16)
        g.memset(ident[:, :], 0.0).then_inc(pool_, t.up())
        g.memset(ones_col[:, :], 1.0).then_inc(pool_, t.up())
        g.memset(ones_row[:, :], 1.0).then_inc(pool_, t.up())
        g.memset(eps[:, 0:1], 1e-6).then_inc(pool_, t.up())
        g.memset(eps[:, 1:2], 1e-5).then_inc(pool_, t.up())
        for n, value in enumerate((1.0, 0.5 - LAST, NODES - 0.5)):
            g.memset(limits[:, n:n + 1], value).then_inc(pool_, t.up())
        g.iota(iota_i[:, :], [[1, NC]], base=0, channel_multiplier=0).then_inc(pool_, t.up())
        g.iota(own_i[:, :], [[0, 1]], base=0, channel_multiplier=SLOTS).then_inc(pool_, t.up())
        g.memset(row_block[:, :], 1.0).then_inc(pool_, t.up())
        g.memset(before[:, :, :], 0.0).then_inc(pool_, t.up())
        pool.wait_ge(pool_, t.n)
        g.affine_select(out=ident[:, :], in_=ident[:, :], compare_op=ALU.not_equal, fill=1.0, base=0,
                        pattern=[[-1, P]], channel_multiplier=1).then_inc(pool_, t.up())
        g.tensor_copy(iota_j[:, :], iota_i[:, :]).then_inc(pool_, t.up())
        g.tensor_copy(own[:, :], own_i[:, :]).then_inc(pool_, t.up())
        for e in range(1, EXPERTS):
            g.memset(before[:, e, 0:e], 1.0).then_inc(pool_, t.up())
        pool.wait_ge(pool_, t.n)
        for sign, base in ((1, 0), (-1, FEATS - 1)):
            g.affine_select(out=row_block[:, :], in_=row_block[:, :], compare_op=ALU.is_ge, fill=0.0, base=base,
                            pattern=[[-sign * FEATS, RPT]], channel_multiplier=sign).then_inc(pool_, t.up())
            pool.wait_ge(pool_, t.n)
        pool.wait_ge(row_weights, 1)
        g.tensor_tensor(digit_w[:, :], row_block[:, :], coef[:, 5:6].to_broadcast([P, RPT]), ALU.mult).then_inc(pool_, t.up())
        g.tensor_tensor(owner_w[:, :, :], row_w[:, :].unsqueeze(1).to_broadcast([P, RPT, P]), wide(row_block[:, :], P),
                        ALU.mult).then_inc(pool_, t.up())
        pool.wait_ge(pool_, t.n)
        g.memset(cum[:, :], 0.0).then_inc(consts, 1)
        for z in (bdz[:, :, :], bdp[:, :, :], bdcp[:, :, :], bdlas[:, :, :], bdc[:, :, :, :]):
            g.memset(z, 0.0).then_inc(diagonals_zero, 1)
        def clamped_keys():
            pool.wait_ge(clamped_parts, 1)
            g.tensor_tensor(clamped, clamped, dst_ok, ALU.mult).then_inc(pool_, t.up())
            pool.wait_ge(pool_, t.n)
            g.tensor_tensor(clamped, clamped, dst_next, ALU.mult).then_inc(scratch_free, 1)

        def center(n):
            a, m = groups[n]
            pool.wait_ge(summed, n + 1)
            part = tiles[:, a:a + m, :]
            g.tensor_scalar(tmean[:, a:a + m], tsum[:, a:a + m], 1.0 / E, None, ALU.mult).then_inc(pool_, t.up())
            pool.wait_ge(pool_, t.n)
            g.tensor_tensor(part, xin[:, a:a + m, :] if a < XT else part, wide(tmean[:, a:a + m], E), ALU.subtract) \
                .then_inc(centered, 1)

        def divide(n):
            a, m = groups[n]
            pool.wait_ge(rstd, 1 if a < XT else 2)
            pool.wait_ge(squared, n + 1)
            part = tiles[:, a:a + m, :]
            g.tensor_tensor(part, part, wide(trstd[:, a:a + m], E), ALU.mult).then_inc(normed, 1)

        for which in (range(2), range(2, len(groups))):
            for n in which:
                center(n)
            if which[0] == 0:
                clamped_keys()
            for n in which:
                divide(n)
        pool.wait_ge(bank_read, NX)
        pool.wait_ge(params_in, 16 * len(loads))
        g.tensor_tensor(ab2, ab[:, :, C:E].rearrange("p k c -> p c k"), mask[:, :].unsqueeze(1).to_broadcast([P, C, NC]),
                        ALU.mult).then_inc(masked_ab, 1)
        g.tensor_tensor(ab[:, :, 0:C], ab[:, :, 0:C], wide(mask[:, :], C), ALU.mult).then_inc(masked_ab, 1)
        g.tensor_tensor(sig[:, :, E:2 * E], sig[:, :, E:2 * E], wide(mask[:, :], E), ALU.mult).then_inc(masked_ab, 1)
        pool.wait_ge(scratch_free, 1)
        g.memset(gath[:, SOMETIMES[0]:SLOTS, :], 0.0).then_inc(pool_, t.up())
        pool.wait_ge(pool_, t.n)
        pool.wait_ge(rows_stored, 16)
        for n, (a, b) in enumerate(zip(PARTS, PARTS[1:])):
            for l in range(a, min(b, SOMETIMES[0])):
                if l in (0, INDEX_FIRST):
                    pool.wait_ge(idx_ready, 1 if l == 0 else 2)
                g.indirect_dma_start(out=gath[:, l, :], out_offset=None, in_=node_rows[:, :],
                                     in_offset=bass.IndirectOffsetOnAxis(ap=locali[:, 2, l:l + 1], axis=0)) \
                    .then_inc(gathered[n], 16)
        pool.wait_ge(more_known, 1)
        for n, (a, b) in enumerate(zip(SOMETIMES, SOMETIMES[1:] + (SLOTS,))):
            with pool.If(pool.value_load(more_i[0:1, n:n + 1], min_val=0, max_val=1) > 0):
                for l in range(a, b):
                    g.indirect_dma_start(out=gath[:, l, :], out_offset=None, in_=node_rows[:, :],
                                         in_offset=bass.IndirectOffsetOnAxis(ap=locali[:, 2, l:l + 1], axis=0)) \
                        .then_inc(gathered_more, 16)
                pool.wait_ge(gathered_more, 16 * (b - SOMETIMES[0]))
        pool.sem_inc(last_gathered)
        pool.wait_ge(slots_stored, 16 * (len(PARTS) - 1))
        pool.wait_ge(tails_ready, 1)
        for j in range(NC):
            g.indirect_dma_start(out=agg_in[:, j, :], out_offset=None, in_=slot_rows[:, :],
                                 in_offset=bass.IndirectOffsetOnAxis(ap=taili[:, j:j + 1], axis=0)) \
                .then_inc(tails_in, 16)
        pool.wait_ge(flag_ready, 1)
        with pool.If(pool.value_load(flag[0:1, 0:1], min_val=0, max_val=1) > 0):
            pool.wait_ge(hist_used, OHB)
            g.memset(earlier, 1.0).then_inc(gen_zero, 1)
            pool.wait_ge(gen_zero, 1)
            g.affine_select(out=earlier, in_=earlier, compare_op=ALU.is_gt, fill=0.0, base=0, pattern=[[-1, P]],
                            channel_multiplier=1).then_inc(gen_mask, 1)
            pool.wait_ge(gen_state, 16)
            with pool.Fori(0, EC) as step:
                pool.wait_ge(gen_idx, step + 1)
                pool.sem_inc(gen_tick)
                for n, (row, table, col) in enumerate(((src_row, node_rows, 1), (dst_row, node_rows, 2),
                                                       (old_row, state_rows, 2))):
                    g.indirect_dma_start(out=row, out_offset=None, in_=table[:, :],
                                         in_offset=bass.IndirectOffsetOnAxis(ap=gi[:, col:col + 1], axis=0)) \
                        .then_inc(gen_in[n], 16)
                pool.wait_ge(gen_row, step + 1)
                pool.sem_inc(gen_tick)
                g.indirect_dma_start(out=state_rows[:, :],
                                     out_offset=bass.IndirectOffsetOnAxis(ap=gi[:, 3:4], axis=0), in_=new_row,
                                     in_offset=None, bounds_check=NODES - 1, oob_is_err=False).then_inc(gen_written, 16)
                pool.wait_ge(gen_written, 16 * step + 16)
                pool.sem_inc(gen_tick)
        pool.wait_ge(gate_ready, 1)
        pool.wait_ge(y_copied, 32)
        js = slice(OUT_PARTS[-2], NC)
        for e in range(EXPERTS):
            g.tensor_tensor(yexp[:, e, js, :], yexp[:, e, js, :], wide(fin[:, 3, js, e], E), ALU.mult).then_inc(pool_, t.up())
        for e in range(EXPERTS):
            pool.wait_ge(pool_, t.n - (3 if e == 0 else 0))
            g.tensor_tensor(xin[:, js, :], xin[:, js, :], yexp[:, e, js, :], ALU.add) \
                .then_inc(*((out_last_ready, 1) if e == 3 else (pool_, t.up())))

    @block.scalar
    def _(act):
        a_ = nc.scalar
        t = Tally(act_)
        for dst, src in loads[:len(loads) // 2 + 3]:
            act.dma_start(dst, src, allow_slow_non_contiguous=True).then_inc(params_in, 16)

        def square(n):
            a, m = groups[n]
            act.wait_ge(centered, n + 1)
            if n >= 2:
                act.wait_ge(sumsq, n - 1)
            a_.activation(v3(squares[n % 2][:, 0:m * E], E), tiles[:, a:a + m, :], ACT.Square).then_inc(squared, 1)

        def copy_turned(n, dst):
            act.wait_ge(turned, n + 1)
            a_.activation(dst, v3(bank[n % 2][:, :], P), ACT.Copy).then_inc(copied, 1)

        def copy_tile(n):
            if n >= 2:
                act.wait_ge(projected, 4 * (n - 1) if n - 2 < 4 else (NX + NCP if n - 2 == 4 else NX + NCP + n - 6))
            copy_turned(n, tT[:, n % 2])

        def sigmoid(n):
            act.wait_ge(projected, n + 1)
            ps = project_bank(n)
            if n < NX:
                a_.activation(sig[:, 2 * n:2 * n + 2, :], v3(ps[:, 0:6 * E], 3 * E)[:, :, E:3 * E], ACT.Sigmoid) \
                    .then_inc(sigmoided, 1)
            else:
                if n >= NX + 2:
                    act.wait_ge(bank_read, n - 1)
                p_ = C if n < NX + NCP else P
                a_.activation(psig[0:p_, n % 2], v3(ps[0:p_, :], E)[:, :, C:E], ACT.Sigmoid).then_inc(sigmoided, 1)

        act.wait_ge(keys_ready, 1)
        a_.activation(yscratch, work, ACT.Sign, accum_out=counts[:, 0:1]).then_inc(keys_counted, 1)
        act.wait_ge(consts, 1)
        act.wait_ge(edges_in, 32)
        a_.activation(dst_next, edst, ACT.Identity, bias=limits[:, 0:1])
        a_.activation(clamped, esrc, ACT.Sign, bias=limits[:, 1:2]).then_inc(act_, t.up())
        a_.activation(dst_ok, edst, ACT.Sign, bias=limits[:, 2:3], scale=-1.0).then_inc(act_, t.up())
        act.wait_ge(act_, t.n)
        a_.activation(clamped, clamped, ACT.Relu)
        a_.activation(dst_ok, dst_ok, ACT.Relu).then_inc(clamped_parts, 1)
        square(0)
        square(1)
        act.wait_ge(sumsq, 2)
        a_.activation(xr[:, 0], tssq[:, 0:XT], ACT.Sqrt, bias=eps[:, 0:1], scale=1.0 / E).then_inc(std_x, 1)
        act.wait_ge(var2_x, 1)
        a_.activation(xr[:, 3], xr[:, 2], ACT.Sqrt, bias=eps[:, 1:2]).then_inc(std2_x, 1)
        act.wait_ge(scratch_free, 1)
        act.wait_ge(keys_counted, 1)
        a_.activation(yscratch, clamped, ACT.Sign, accum_out=counts[:, 3:4]).then_inc(keys_counted, 1)
        for n in range(2, len(groups)):
            square(n)
            if n == 2:
                copy_tile(0)
                copy_tile(1)
            else:
                if n in (5, 7):
                    copy_tile((n - 1) // 2)
                for m in range(2):
                    sigmoid(2 * (n - 3) + m)
        act.wait_ge(sumsq, len(groups))
        a_.activation(tstd[:, XT:TILES], tssq[:, XT:TILES], ACT.Sqrt, bias=eps[:, 1:2], scale=1.0 / E) \
            .then_inc(std_rest, 1)
        copy_tile(4)
        copy_tile(5)

        def pair_bank(n):
            sigmoid(n)
            k = n - NX - NCP
            if -1 <= k < NPR - 2:
                copy_tile(k + 7)

        for n in range(NX, EARLY):
            pair_bank(n)
        n = 5 + NPR
        for m in range(SHOWS):
            act.wait_ge(shown, m + 1)
            if m >= 4:
                act.wait_ge(keys_taken, m - 3)
            a_.activation(bcast[:, m % 4], bank[4 + m % 2][:, 0:RPG * SLOTS], ACT.Relu).then_inc(shown_copied, 1)
            if m % BANK_EVERY == 0 and EARLY + m // BANK_EVERY < NX + NCP + NPR:
                pair_bank(EARLY + m // BANK_EVERY)
            elif m == AT_TURN_AB:
                for b in range(2):
                    copy_turned(n + b, abT[:, 4 * b:4 * b + 4, :])
            elif m == AT_CENTER + 2:
                act.wait_ge(nb_centered, 2)
                a_.activation(squares[0], nb.rearrange("p j c -> p (j c)"), ACT.Square).then_inc(nb_squared, 1)
            elif m == AT_SUMSQ + 2:
                act.wait_ge(nb_sumsq, 1)
                a_.activation(nstat[:, 2], nstat[:, 1], ACT.Sqrt, bias=eps[:, 1:2], scale=1.0 / C).then_inc(nb_std, 1)
            elif m in (AT_TOKENS + 2, AT_TOKENS + 3):
                act.wait_ge(xn_centered, 1)
                b = m - AT_TOKENS - 2
                a_.activation(v3(squares[b], E), xn[:, 16 * b:16 * b + 16, :], ACT.Square).then_inc(xn_squared, 1)
            elif m == AT_TURN_NB + 1:
                act.wait_ge(projected, NX + NCP + NPR)
                for b in range(2):
                    copy_turned(n + 2 + b, tT[:, b])
        act.wait_ge(xn_sumsq, 1)
        a_.activation(nstat[:, 2], nstat[:, 1], ACT.Sqrt, bias=eps[:, 1:2], scale=1.0 / E).then_inc(xn_std, 1)
        for b in range(4):
            copy_turned(n + 4 + b, xnT[:, 4 * b:4 * b + 4, :])
        act.wait_ge(late_in, 16 * len(late_loads))
        act.wait_ge(xn_ready, 1)

        def gelu(f):
            act.wait_ge(hidden_done, f + 1)
            if f >= 2:
                act.wait_ge(y_done, f - 1)
            a_.activation(hid[:, f % 2].rearrange("p t n -> p (t n)"), bank[f % 2][:, :], ACT.Gelu,
                          bias=b1s[:, f // 8:f // 8 + 1]).then_inc(gelued, 1)

        def copy_y(f):
            e, q, b = f // 8, f // 4 % 2, f % 4
            act.wait_ge(y_done, f + 1)
            a_.activation(yexp[:, e, 8 * b + q:8 * b + 8:2, :], v3(bank[2 + f % 2][:, 0:4 * E], E), ACT.Copy) \
                .then_inc(y_copied, 1)

        def weigh(h, j):
            if j == 0:
                act.wait_ge(seg_ready, 1)
                if h >= 2:
                    act.wait_ge(dslot_done, h - 1)
            ins = a_.activation(segd[:, h % 2, j, :], seg[:, j, :], ACT.Copy, scale=rows[:, j, HF + HEADS + h:HF + HEADS + h + 1])
            if j == NC - 1:
                ins.then_inc(weighted, 1)

        def exponentials(n):
            a, b = PARTS[n], PARTS[n + 1]
            act.wait_ge(exps_wanted, n + 1)
            for what in (carry, wgt):
                a_.activation(what[:, :, a:b], what[:, :, a:b], ACT.Exp).then_inc(exps_done, 1)

        act.wait_ge(rows_ready, 1)
        for f in range(32):
            if f == EXPS_BEFORE:
                exponentials(0)
            gelu(f)
            if f:
                copy_y(f - 1)
            for k in range((f - WEIGH_FROM) * WEIGH_EACH, (f - WEIGH_FROM + 1) * WEIGH_EACH):
                if 0 <= k < HEADS * NC:
                    weigh(k // NC, k % NC)
        copy_y(31)
        for n in range(1, len(PARTS) - 1):
            exponentials(n)
        act.wait_ge(flag_ready, 1)
        with act.If(act.value_load(flag[0:1, 0:1], min_val=0, max_val=1) > 0):
            with act.Fori(0, EC) as step:
                act.wait_ge(gen_exp, step + 1)
                a_.activation(expo, expo, ACT.Exp).then_inc(gen_exped, 1)
        act.wait_ge(fin_wanted, 1)
        a_.activation(fin[:, 0:3], fin[:, 0:3], ACT.Exp).then_inc(fin_done, 1)
        act.wait_ge(fin_wanted, 2)
        a_.activation(nstat[:, 2], nstat[:, 1], ACT.Sqrt, bias=eps[:, 1:2], scale=1.0 / HF).then_inc(fin_done, 1)
        act.wait_ge(fin_wanted, 3)
        a_.activation(fin[:, 3], fin[:, 3], ACT.Exp).then_inc(fin_done, 1)

    @block.tensor
    def _(pe):
        p_ = nc.tensor
        t = Tally(pe_)
        pe.wait_ge(consts, 1)
        pe.wait_ge(params_in, 16 * len(loads))
        p_.transpose(bank[6][:, 0:P], w_nat[:, :], ident[:, :])
        p_.transpose(bank[6][:, P:P + E], eg_nat[:, :], ident[0:E, 0:E])
        p_.transpose(bank[6][:, P + E:P + 2 * E], las_nat[:, :], ident[0:E, 0:E]).then_inc(weights_turned, 1)
        pe.wait_ge(weights_copied, 2)
        p_.matmul(bank[7][0:3, 0:3 * E], affine[0:E, 1:2].to_broadcast([E, 3]), wT[0:E, :], start=True, stop=True)
        p_.matmul(bank[7][0:3, 3 * E:4 * E], affine[0:C, 3:4].to_broadcast([C, 3]), lasT[0:C, :], start=True, stop=True).then_inc(bias_made, 1)

        def turn(n, sources):
            if n >= 2:
                pe.wait_ge(copied, n - 1)
            for m, src in enumerate(sources):
                mm = p_.transpose(bank[n % 2][:, P * m:P * (m + 1)], src, ident[:, :])
            mm.then_inc(turned, 1)

        def turn_tiles(n):
            pe.wait_ge(normed, n // 2 + 1 if n < 4 else (3 if n == 4 else 4 + (n - 5) // 2))
            turn(n, [tiles[:, 8 * n + 2 * m:8 * n + 2 * m + 2, :].rearrange("p t e -> p (t e)") for m in range(4)])

        def project_x(n, b, m):
            if n >= 4:
                pe.wait_ge(bank_read, n - 3)
            ps = project_bank(n)
            p_.matmul(v3(ps[:, 0:6 * E], 3 * E), ones_row[:, :],
                      zbias[:, 0:3 * E].unsqueeze(1).to_broadcast([3, 2, 3 * E]), start=True, stop=False,
                      skip_group_check=True)
            p_.matmul(ps[:, 0:6 * E], tT[:, b, m, :], bdz[:, :, :].rearrange("p a b -> p (a b)"), start=False, stop=True,
                      skip_group_check=True).then_inc(projected, 1)

        def project_comp(n, b, m):
            pe.wait_ge(bank_read, n - 3 if n < NX + 2 else n - 1)
            ps = project_bank(n)
            p_.matmul(v3(ps[0:C, :], E), ones_row[:, 0:C], cbias[:, :].unsqueeze(1).to_broadcast([3, 8, E]),
                      start=True, stop=False, skip_group_check=True)
            for r in range(4):
                mm = p_.matmul(v3(ps[0:C, :], E)[:, r:8:4, :], tT[:, b, m, C * r:C * (r + 1)], bdcp[:, :, :],
                               start=False, stop=True, skip_group_check=True)
            mm.then_inc(projected, 1)

        def project_protein(n, b):
            pe.wait_ge(bank_read, n - 1)
            ps = bank[2 + n % 2]
            p_.matmul(v3(ps[:, :], E), ones_row[:, :], pbias[:, :].unsqueeze(1).to_broadcast([3, 8, E]),
                      start=True, stop=False, skip_group_check=True)
            for m in range(4):
                mm = p_.matmul(ps[:, 2 * E * m:2 * E * (m + 1)], tT[:, b, m, :], bdp[:, :, :].rearrange("p a b -> p (a b)"),
                               start=False, stop=True, skip_group_check=True)
            mm.then_inc(projected, 1)

        turn_tiles(0)
        turn_tiles(1)
        pe.wait_ge(bias_copied, 2)
        for n in range(4):
            pe.wait_ge(copied, n + 1)
            for m in range(4):
                project_x(4 * n + m, n % 2, m)
            if n < 2:
                turn_tiles(n + 2)
        turn_tiles(4)
        turn_tiles(5)
        pe.wait_ge(copied, 5)
        for k in range(NCP):
            project_comp(NX + k, 0, k)
        turn_tiles(6)

        def protein(n):
            k = n - NX - NCP
            pe.wait_ge(copied, k + 6)
            project_protein(n, (k + 1) % 2)
            if k + 7 < 5 + NPR:
                turn_tiles(k + 7)

        for n in range(NX + NCP, EARLY):
            protein(n)
        n = 5 + NPR

        def blocks(g):
            ps = bank[6 + g // 4][:, P * (g % 4):P * (g % 4 + 1)]
            p_.matmul(ps, abT[:, g, :], bdc[:, g].rearrange("p c j -> p (c j)"), start=True, stop=False,
                      skip_group_check=True)
            for c in range(4):
                mm = p_.matmul(ps[:, NC * c:NC * (c + 1)], ppc[:, 4 * g + c, :], ab[:, :, 4 * g + c], start=False,
                               stop=True, skip_group_check=True)
            if g % 4 == 3:
                mm.then_inc(blocks_done, 1)

        def project_last(m):
            if m == 0:
                pe.wait_ge(copied, n + 4)
            k = NX + NCP + NPR + m
            pe.wait_ge(bank_read, k - 1)
            ps = bank[2 + k % 2]
            p_.matmul(v3(ps[:, :], E), ones_row[:, :], zbias[:, 3 * E:4 * E].unsqueeze(1).to_broadcast([3, 8, E]),
                      start=True, stop=False, skip_group_check=True)
            for h in range(2):
                g = 2 * m + h
                mm = p_.matmul(ps[:, 4 * E * h:4 * E * (h + 1)], tT[:, g // 4, g % 4, :],
                               bdlas[:, :, :].rearrange("p a b -> p (a b)"), start=False, stop=True, skip_group_check=True)
            mm.then_inc(projected, 1)

        for m in range(SHOWS):
            if m == 0:
                pe.wait_ge(feats_in, 16)
            if m < 2:
                pe.wait_ge(bank_read, NX - 1 + m)
            else:
                pe.wait_ge(shown_copied, m - 1)
            for r in range(RPG):
                row = RPG * m + r
                ps, keys = bank[4 + m % 2][:, SLOTS * r:SLOTS * (r + 1)], turned_feats[:, row // RPT, :]
                p_.matmul(ps, owner_w[:, row % RPT, :], keys, start=True, stop=False, skip_group_check=True)
                mm = p_.matmul(ps, digit_w[:, row % RPT:row % RPT + 1].to_broadcast([P, P]), keys, start=False,
                               stop=True, skip_group_check=True)
            mm.then_inc(shown, 1)
            if m % BANK_EVERY == 0 and EARLY + m // BANK_EVERY < NX + NCP + NPR:
                protein(EARLY + m // BANK_EVERY)
            elif m == AT_TURN_AB - 1:
                pe.wait_ge(masked_ab, 1)
                for b in range(2):
                    turn(n + b, [ab2[:, 4 * g:4 * g + 4, :].rearrange("p c k -> p (c k)")
                                 for g in range(4 * b, 4 * b + 4)])
            elif AT_BLOCKS <= m < AT_BLOCKS + 8 * BLOCK_EVERY and (m - AT_BLOCKS) % BLOCK_EVERY == 0:
                if m == AT_BLOCKS:
                    pe.wait_ge(bdc_ready, 1)
                    pe.wait_ge(masked_ab, 2)
                    pe.wait_ge(bank_read, NX + NCP + NPR)
                    pe.wait_ge(copied, n + 2)
                blocks((m - AT_BLOCKS) // BLOCK_EVERY)
            elif m == AT_TURN_NB:
                pe.wait_ge(nb_ready, 1)
                for b in range(2):
                    turn(n + 2 + b, [nb[:, 4 * g:4 * g + 4, :].rearrange("p j c -> p (j c)")
                                     for g in range(4 * b, 4 * b + 4)])
            elif m in AT_LAS:
                project_last(AT_LAS.index(m))
        for m in range(len(AT_LAS), NLAS):
            project_last(m)
        pe.wait_ge(xn_ready, 1)
        for b in range(4):
            turn(n + 4 + b, [xn[:, 8 * b + 2 * m:8 * b + 2 * m + 2, :].rearrange("p j e -> p (j e)") for m in range(4)])
        pe.wait_ge(late_in, 16 * len(late_loads))
        pe.wait_ge(copied, n + 8)
        pe.wait_ge(nb_centered, 2)
        for u in range(NC // 2):
            mm = p_.matmul(bank[6][:, 2 * HF * u:2 * HF * (u + 1)], xnT[:, u, :], wgat2[:, :, :].rearrange("p q f -> p (q f)"),
                           start=True, stop=True, skip_group_check=True)
        mm.then_inc(gat_done, 1)
        def hidden(f):
            e, q, b = f // 8, f // 4 % 2, f % 4
            if f >= 2:
                pe.wait_ge(gelued, f - 1)
            p_.matmul(bank[f % 2][:, :], w1s[E * q:E * (q + 1), e, :],
                      xnT[E * q:E * (q + 1), 4 * b:4 * b + 4, :].rearrange("p t n -> p (t n)"), start=True, stop=True) \
                .then_inc(hidden_done, 1)

        def expert_out(f):
            e = f // 8
            if f >= 2:
                pe.wait_ge(y_copied, f - 1)
            pe.wait_ge(gelued, f + 1)
            ps = bank[2 + f % 2]
            p_.matmul(v3(ps[:, 0:4 * E], E), ones_col[0:1, :], b2s[:, e, :].unsqueeze(1).to_broadcast([1, 4, E]),
                      start=True, stop=False, skip_group_check=True)
            for m in range(4):
                mm = p_.matmul(ps[:, E * m:E * (m + 1)], hid[:, f % 2, m, :], w2s[:, e, :], start=False, stop=True,
                               skip_group_check=True)
            mm.then_inc(y_done, 1)

        def histogram(b):
            pe.wait_ge(onehots_ready, b + 1)
            for c in range(OHC):
                mm = p_.matmul(bank[4][0:64, 0:64], onehot[:, b % 2, 0, :, c], onehot[:, b % 2, 1, :, c],
                               start=(b == 0 and c == 0), stop=(b == OHB - 1 and c == OHC - 1))
            mm.then_inc(hist_used, 1)

        pe.wait_ge(bank_read, NX + NCP + NPR + NLAS)
        hidden(0)
        for f in range(32):
            if f == 6:
                pe.wait_ge(more_ready, 1)
                pe.wait_ge(shown_copied, SHOWS)
                p_.matmul(bank[5][:, 0:len(SOMETIMES)], ones_col[:, :], more[:, :], start=True, stop=True) \
                    .then_inc(more_summed, 1)
            if f < 31:
                hidden(f + 1)
            expert_out(f)
            if f in HIST_AFTER:
                histogram(HIST_AFTER.index(f))
        for b in range(len(HIST_AFTER), OHB):
            histogram(b)
        pe.wait_ge(missing_ready, 1)
        pe.wait_ge(more_known, 1)
        p_.matmul(bank[5][:, 0:1], ones_col[:, :], counts[:, 2:3], start=True, stop=False)
        p_.matmul(bank[5][:, 0:1], ones_col[0:64, :], counts[0:64, 4:5], start=False, stop=True).then_inc(missing_summed, 1)
        pe.wait_ge(flag_ready, 1)
        with pe.If(pe.value_load(flag[0:1, 0:1], min_val=0, max_val=1) > 0):
            pe.wait_ge(y_copied, 32)
            with pe.Fori(0, EC) as step:
                pe.wait_ge(gen_idx, step + 1)
                p_.matmul(bank[0][:, 0:P], dst1.to_broadcast([P, P]), ident[:, :], start=True, stop=True).then_inc(gen_same, 1)
                pe.wait_ge(gen_score, step + 1)
                for h in range(HEADS):
                    mm = p_.matmul(bank[1][:, P * h:P * (h + 1)], escore[:, h:h + 1].to_broadcast([P, P]), ident[:, :],
                                   start=True, stop=True)
                mm.then_inc(gen_others, 1)
                pe.wait_ge(gen_payload, step + 1)
                p_.matmul(bank[2][:, 0:HEADS + HF], same, payload, start=True, stop=True).then_inc(gen_summed, 1)

    @block.vector
    def _(dve):
        v = nc.vector
        t = Tally(vec)

        def total(n):
            a, m = groups[n]
            if n == 0:
                dve.wait_ge(x_in, 16)
            elif n == 2:
                dve.wait_ge(comp_in, 16)
            elif n > 2:
                dve.wait_ge(pp_in[n - 3], 16)
            src = xin[:, a:a + m, :] if a < XT else tiles[:, a:a + m, :]
            v.tensor_reduce(tsum[:, a:a + m], src, AX.X, ALU.add).then_inc(summed, 1)

        def total_sq(n):
            a, m = groups[n]
            dve.wait_ge(squared, n + 1)
            v.tensor_reduce(tssq[:, a:a + m], v3(squares[n % 2][:, 0:m * E], E), AX.X, ALU.add).then_inc(sumsq, 1)

        def settle():
            dve.wait_ge(vec, t.n)

        dve.wait_ge(numbers, 2)
        v.tensor_single_scalar(feat_i[:, 1:2], feat_i[:, 0:1], FEATS - 1, ALU.bitwise_and).then_inc(vec, t.up())
        v.tensor_tensor(square_i, number_i, number_i, ALU.mult).then_inc(vec, t.up())
        settle()
        v.tensor_copy(coef[:, 0:1], feat_i[:, 1:2]).then_inc(vec, t.up())
        v.tensor_single_scalar(high_i, square_i, 0xFF00, ALU.bitwise_and).then_inc(vec, t.up())
        v.tensor_single_scalar(low_i, square_i, 0xFF, ALU.bitwise_and).then_inc(vec, t.up())
        settle()
        for n, (number, op, factor) in enumerate(((1.5, ALU.is_le, -1.0), (2.0, ALU.is_equal, 2.0), (3.0, ALU.is_equal, -1.0),
                                                  (4.0, ALU.is_equal, -1.0), (4.5, ALU.is_ge, 1.0))):
            v.tensor_scalar(coef[:, n + 1:n + 2], coef[:, 0:1], number, factor, op, ALU.mult).then_inc(vec, t.up())
        settle()
        pf = xnT[:, 4, :]
        v.tensor_scalar(pf, high_i, coef[:, 3:4], None, ALU.mult).then_inc(vec, t.up())
        settle()
        v.scalar_tensor_tensor(pf, low_i, coef[:, 4:5], pf, ALU.mult, ALU.add).then_inc(vec, t.up())
        settle()
        v.scalar_tensor_tensor(pf, number_i, coef[:, 2:3], pf, ALU.mult, ALU.add).then_inc(vec, t.up())
        settle()
        v.tensor_scalar(row_w[:, :], pf, coef[:, 1:2], None, ALU.add).then_inc(row_weights, 1)
        dve.wait_ge(edges_in, 32)
        v.tensor_scalar(plain_src, esrc, float(LAST), None, ALU.is_lt).then_inc(vec, t.up())
        v.scalar_tensor_tensor(ktmp, edst, float(NODES), esrc, ALU.mult, ALU.add).then_inc(vec, t.up())
        dve.wait_ge(vec, t.n - 1)
        v.scalar_tensor_tensor(plain, edst, float(NODES), plain_src, ALU.is_lt, ALU.mult).then_inc(vec, t.up())
        settle()
        v.scalar_tensor_tensor(work, ktmp, 1.0, plain, ALU.add, ALU.mult).then_inc(keys_ready, 1)
        total(0)
        total(1)

        def compact(source, dest, width, chunks, take, first=None, between=None, rounds=None):
            for r in rounds or range(take // 8):
                for c in range(chunks):
                    if r:
                        dve.wait_ge(vec, t.n - chunks + 1)
                    v.max(dest[:, take * c + 8 * r:take * c + 8 * r + 8], source[:, width * c:width * (c + 1)]) \
                        .then_inc(vec, t.up())
                if between is not None:
                    between(2 * r)
                if r == 0 and first is not None:
                    first()
                if r < take // 8 - 1:
                    for c in range(chunks):
                        dve.wait_ge(vec, t.n - chunks + 1)
                        part = source[:, width * c:width * (c + 1)]
                        v.match_replace(part, dest[:, take * c + 8 * r:take * c + 8 * r + 8], part, 0.0) \
                            .then_inc(vec, t.up())
                    if between is not None:
                        between(2 * r + 1)
            settle()

        dve.wait_ge(keys_ready, 1)
        compact(work, cand1[:, :], CH1, NCH1, TAKE1, first=lambda: dve.wait_ge(keys_counted, 1))
        total_sq(0)
        total_sq(1)
        dve.wait_ge(std_x, 1)
        v.reciprocal(xr[:, 1], xr[:, 0]).then_inc(vec, t.up())
        settle()
        v.scalar_tensor_tensor(xr[:, 2], tssq[:, 0:XT], 1.0 / E, xr[:, 1], ALU.mult, ALU.mult).then_inc(vec, t.up())
        settle()
        v.tensor_tensor(xr[:, 2], xr[:, 2], xr[:, 1], ALU.mult).then_inc(var2_x, 1)
        dve.wait_ge(std2_x, 1)
        v.reciprocal(xr[:, 3], xr[:, 3]).then_inc(vec, t.up())
        settle()
        v.tensor_tensor(trstd[:, 0:XT], xr[:, 1], xr[:, 3], ALU.mult).then_inc(rstd, 1)
        dve.wait_ge(weights_turned, 1)
        v.tensor_copy(wT[:, :], bank[6][:, 0:3 * E]).then_inc(weights_copied, 1)
        v.tensor_copy(lasT[:, :], bank[6][:, 3 * E:4 * E]).then_inc(weights_copied, 1)
        dve.wait_ge(weights_copied, 2)
        dve.wait_ge(diagonals_zero, 5)
        v.tensor_scalar(wTs[:, :], wT[:, :], affine[:, 0:1], None, ALU.mult).then_inc(vec, t.up())
        for q in range(4):
            rows_q = slice(C * q, C * (q + 1))
            v.tensor_scalar(bdlas[rows_q, q, :], lasT[rows_q, :], affine[rows_q, 2:3], None, ALU.mult) \
                .then_inc(vec, t.up())
        settle()
        for q in range(2):
            half = slice(E * q, E * (q + 1))
            v.tensor_copy(bdz[half, q, :], wTs[half, :]).then_inc(vec, t.up())
            v.tensor_copy(v3(bdp[half, q, :], C), v3(wTs[half, 0:2 * E], E)[:, :, C:E]).then_inc(vec, t.up())
            v.tensor_copy(v3(bdcp[half, q, :], C), v3(wTs[half, 0:2 * E], E)[:, :, 0:C]).then_inc(vec, t.up())
        dve.wait_ge(bias_made, 1)
        v.tensor_tensor(bias1[:, :], bank[7][0:3, 0:4 * E], bias_in[:, :], ALU.add).then_inc(vec, t.up())
        settle()
        for k in range(3):
            part = parts[:, k % 2, :]
            v.tensor_copy(part, bias1[:, :]).then_inc(vec, t.up())
            settle()
            if k < 2:
                v.tensor_tensor(bias1[:, :], bias1[:, :], part, ALU.subtract).then_inc(vec, t.up())
            if k == 0:
                v.tensor_scalar(zbias[:, :], part, ident[0:3, 0:1], None, ALU.mult).then_inc(vec, t.up())
            else:
                v.scalar_tensor_tensor(zbias[:, :], part, ident[0:3, k:k + 1], zbias[:, :], ALU.mult, ALU.add) \
                    .then_inc(vec, t.up())
            settle()
        v.tensor_copy(v3(cbias[:, :], C), v3(zbias[:, 0:2 * E], E)[:, :, 0:C]).then_inc(bias_copied, 1)
        v.tensor_copy(v3(pbias[:, :], C), v3(zbias[:, 0:2 * E], E)[:, :, C:E]).then_inc(bias_copied, 1)
        def read_bank(n):
            dve.wait_ge(sigmoided, n + 1)
            ps = project_bank(n)
            if n < NX:
                v.tensor_tensor(ab[:, 2 * n:2 * n + 2, :], v3(ps[:, 0:6 * E], 3 * E)[:, :, 0:E], sig[:, 2 * n:2 * n + 2, 0:E],
                                ALU.mult).then_inc(bank_read, 1)
            elif n < NX + NCP:
                m = n - NX
                v.tensor_tensor(cpk[:, 8 * m:8 * m + 8, :], v3(ps[0:C, :], E)[:, :, 0:C], psig[0:C, n % 2], ALU.mult) \
                    .then_inc(bank_read, 1)
            else:
                m = n - NX - NCP
                v.tensor_tensor(ppc[:, :, 8 * m:8 * m + 8].rearrange("p c i -> p i c"), v3(ps[:, :], E)[:, :, 0:C],
                                psig[:, n % 2], ALU.mult).then_inc(bank_read, 1)

        for n in range(2, len(groups)):
            total(n)
            if n > 3:
                total_sq(n - 2)
            if n > 4:
                read_bank(2 * n - 10)
                read_bank(2 * n - 9)
        total_sq(len(groups) - 2)
        total_sq(len(groups) - 1)
        for n in range(NX - 4, NX):
            read_bank(n)
        dve.wait_ge(std_rest, 1)
        v.reciprocal(trstd[:, XT:TILES], tstd[:, XT:TILES]).then_inc(rstd, 1)

        def merge(source, dest, between):
            for r in range(SLOTS // 8):
                v.max(dest[:, 8 * r:8 * r + 8], source[:, :]).then_inc(vec, t.up())
                settle()
                if r < SLOTS // 8 - 1:
                    v.match_replace(source[:, :], dest[:, 8 * r:8 * r + 8], source[:, :], 0.0).then_inc(vec, t.up())
                between(r)
                settle()

        read_after = (5, 6, 7, 8, 10, 11, 13, 14, 16, 17, 19, 20)
        merge(cand1, sent, lambda r: read_bank(NX + read_after.index(r)) if r in read_after else None)
        owner_i, top_i, mid_i, bottom_i = (keyi[:, n] for n in range(1, 5))
        v.tensor_scalar(keyi[:, 0], sent[:, :], -1.0, None, ALU.add).then_inc(vec, t.up())
        v.memset(feats[:, 3:5, :], PENALTY).then_inc(vec, t.up())
        settle()
        v.tensor_single_scalar(owner_i, keyi[:, 0], 17, ALU.arith_shift_right).then_inc(vec, t.up())
        for part, bits in ((top_i, 0x10000), (mid_i, 0xFF00), (bottom_i, 0xFF)):
            v.tensor_single_scalar(part, keyi[:, 0], bits, ALU.bitwise_and).then_inc(vec, t.up())
        settle()
        v.tensor_tensor(senti[:, 0], owner_i, owner_i, ALU.mult).then_inc(vec, t.up())
        v.tensor_scalar(feats[:, 2], owner_i, PENALTY, None, ALU.mult).then_inc(vec, t.up())
        v.tensor_copy(feats[:, 5], top_i).then_inc(vec, t.up())
        v.tensor_copy(feats[:, 6], mid_i).then_inc(vec, t.up())
        v.tensor_scalar(feats[:, 7], bottom_i, 1.0, None, ALU.add).then_inc(vec, t.up())
        settle()
        v.tensor_single_scalar(senti[:, 1], senti[:, 0], 0xFF00, ALU.bitwise_and).then_inc(vec, t.up())
        v.tensor_single_scalar(senti[:, 2], senti[:, 0], 0xFF, ALU.bitwise_and).then_inc(vec, t.up())
        settle()
        v.tensor_scalar(feats[:, 0], senti[:, 1], PENALTY, None, ALU.mult).then_inc(vec, t.up())
        v.tensor_scalar(feats[:, 1], senti[:, 2], PENALTY, None, ALU.mult).then_inc(vec, t.up())
        settle()
        v.engine_nop().then_inc(feats_ready, 1)
        dve.wait_ge(keys_counted, 2)
        dve.wait_ge(normed, len(groups))
        compact(clamped, ccand, CH3, NCH3, TAKE3, rounds=range(1))

        def compound_diagonals():
            dve.wait_ge(bank_read, NX + NCP)
            for c4 in range(4):
                ins = v.tensor_copy(bdc[C * c4:C * (c4 + 1), :, c4, :], cpk[:, :, c4:C:4].rearrange("k j g -> k g j"))
                ins.then_inc(bdc_ready if c4 == 3 else vec, 1)
                if c4 < 3:
                    t.up()

        chan = [bank[6 + b][:, :].rearrange("p (c j) -> p j c", j=NC) for b in range(2)]

        def channel_sums():
            for b in range(2):
                dve.wait_ge(blocks_done, b + 1)
                v.tensor_reduce(nstat[:, b], chan[b], AX.X, ALU.add).then_inc(vec, t.up())
            settle()
            v.tensor_tensor(nstat[:, 0], nstat[:, 0], nstat[:, 1], ALU.add).then_inc(vec, t.up())

        def channel_center():
            settle()
            for b in range(2):
                v.scalar_tensor_tensor(nb[:, :, 16 * b:16 * b + 16], wide(nstat[:, 0], 16), -1.0 / C, chan[b], ALU.mult,
                                       ALU.add).then_inc(nb_centered, 1)

        def channel_squares():
            dve.wait_ge(nb_squared, 1)
            v.tensor_reduce(nstat[:, 1], v3(squares[0], C), AX.X, ALU.add).then_inc(nb_sumsq, 1)

        def channel_scale():
            dve.wait_ge(nb_std, 1)
            v.reciprocal(nstat[:, 3], nstat[:, 2]).then_inc(vec, t.up())
            settle()
            dve.wait_ge(nb_centered, 2)
            v.tensor_tensor(nb, nb, wide(nstat[:, 3], C), ALU.mult).then_inc(nb_ready, 1)

        def update(m):
            if m == 0:
                dve.wait_ge(masked_ab, 3)
            n = NX + NCP + NPR + m
            dve.wait_ge(projected, n + 1)
            js = slice(8 * m, 8 * m + 8)
            v.tensor_tensor(sig[:, js, 0:E], v3(bank[2 + n % 2][:, :], E), sig[:, js, E:2 * E], ALU.mult) \
                .then_inc(bank_read, 1)
            dve.wait_ge(bank_read, n + 1)
            v.tensor_tensor(xin[:, js, :], xin[:, js, :], sig[:, js, 0:E], ALU.add).then_inc(vec, t.up())

        def token_center():
            settle()
            v.tensor_reduce(nstat[:, 0], xin[:, :, :], AX.X, ALU.add).then_inc(vec, t.up())
            settle()
            v.scalar_tensor_tensor(xn[:, :, :], wide(nstat[:, 0], E), -1.0 / E, xin[:, :, :], ALU.mult, ALU.add) \
                .then_inc(xn_centered, 1)

        def token_squares(b):
            dve.wait_ge(xn_squared, b + 1)
            ins = v.tensor_reduce(nstat[:, 1, 16 * b:16 * b + 16], v3(squares[b], E), AX.X, ALU.add)
            ins.then_inc(xn_sumsq if b else vec, 1)
            if not b:
                t.up()

        def token_scale():
            dve.wait_ge(xn_std, 1)
            v.reciprocal(nstat[:, 3], nstat[:, 2]).then_inc(vec, t.up())
            settle()
            dve.wait_ge(xn_centered, 1)
            v.tensor_tensor(xn[:, :, :], xn[:, :, :], wide(nstat[:, 3], E), ALU.mult).then_inc(xn_ready, 1)

        def node_row_parts():
            dve.wait_ge(gat_done, 1)
            v.tensor_copy(rows[:, :, 0:HF], v3(bank[6][:, :], HF)).then_inc(vec, t.up())
            settle()
            for n in range(2):
                v.tensor_tensor(hatt[:, n], rows[:, :, 0:HF], att[:, n, :].unsqueeze(1).to_broadcast([P, NC, HF]), ALU.mult) \
                    .then_inc(vec, t.up())
            settle()
            v.tensor_reduce(rows[:, :, HF:ROW].rearrange("p j (s h) -> p s j h", s=2),
                            hatt.rearrange("p s j (h e) -> p s j h e", h=HEADS), AX.X, ALU.add).then_inc(rows_ready, 1)

        for m in range(SHOWS):
            dve.wait_ge(shown_copied, m + 1)
            for r in range(RPG):
                k = RPG * m + r
                v.max(coll[:, 8 * k:8 * k + 8], bcast[:, m % 4, SLOTS * r:SLOTS * (r + 1)]) \
                    .then_inc(*((vec, t.up()) if r < RPG - 1 else (keys_taken, 1)))
            if m % BANK_EVERY == 0 and EARLY + m // BANK_EVERY < NX + NCP + NPR:
                read_bank(EARLY + m // BANK_EVERY)
            if m == 1:
                compound_diagonals()
            elif m == AT_SUM:
                channel_sums()
            elif m == AT_CENTER:
                channel_center()
            elif m == AT_SUMSQ:
                channel_squares()
            elif m == AT_SCALE:
                channel_scale()
            elif m in AT_UPDATE:
                update(AT_UPDATE.index(m))
            elif m == AT_TOKENS:
                token_center()
            elif m in AT_TOKEN_SQUARES:
                token_squares(AT_TOKEN_SQUARES.index(m))
        settle()

        dve.wait_ge(keys_taken, SHOWS)

        def between_rounds(r):
            if r == AT_TOKEN_SCALE:
                token_scale()
            elif r == AT_ROWS:
                node_row_parts()

        compact(coll, cand2[:, :], CH2, NCH2, TAKE2, between=between_rounds)

        def local_index(a, b):
            settle()
            v.tensor_scalar(locali[:, 0, a:b], recv[:, a:b], -1.0, None, ALU.add).then_inc(vec, t.up())
            settle()
            v.tensor_single_scalar(locali[:, 2, a:b], locali[:, 0, a:b], NODES - 1, ALU.bitwise_and).then_inc(idx_ready, 1)

        def between_merges(r):
            if r == INDEX_FIRST // 8:
                local_index(0, INDEX_FIRST)

        merge(cand2, recv, between_merges)
        local_index(INDEX_FIRST, SLOTS)
        v.tensor_single_scalar(locali[:, 1], locali[:, 0], 12, ALU.arith_shift_right).then_inc(vec, t.up())
        v.tensor_scalar(local[:, :], locali[:, 0], 0.0, None, ALU.is_ge).then_inc(vec, t.up())
        settle()
        v.tensor_copy(tgt[:, :], locali[:, 1]).then_inc(vec, t.up())
        v.tensor_reduce(counts[:, 1:2], local[:, :], AX.X, ALU.add).then_inc(vec, t.up())
        settle()
        for n, slots in enumerate(SOMETIMES):
            v.tensor_scalar(more[:, n:n + 1], counts[:, 1:2], float(slots), None, ALU.is_gt) \
                .then_inc(*((more_ready, 1) if slots == SOMETIMES[-1] else (vec, t.up())))
        v.tensor_tensor(counts[:, 2:3], counts[:, 0:1], counts[:, 1:2], ALU.subtract).then_inc(vec, t.up())
        dve.wait_ge(keys_counted, 2)
        settle()
        v.tensor_tensor(counts[:, 2:3], counts[:, 2:3], counts[:, 3:4], ALU.add).then_inc(vec, t.up())
        every_j = tgt[:, :].unsqueeze(1).to_broadcast([P, NC, SLOTS])
        v.tensor_tensor(seg, every_j, wide(iota_j[:, :], SLOTS), ALU.is_ge).then_inc(vec, t.up())
        settle()
        v.tensor_reduce(cum[:, 0:NC], seg, AX.X, ALU.add).then_inc(vec, t.up())
        settle()
        v.tensor_tensor(present[:, :], cum[:, 0:NC], cum[:, 1:NC + 1], ALU.is_gt).then_inc(vec, t.up())
        v.tensor_scalar(tailf[:, :], cum[:, 0:NC], -1.0, 0.0, ALU.add, ALU.max).then_inc(vec, t.up())
        v.tensor_tensor(seg, every_j, wide(iota_j[:, :], SLOTS), ALU.is_equal).then_inc(seg_ready, 1)
        settle()
        v.tensor_scalar(taili[:, :], tailf[:, :], own[:, 0:1], None, ALU.add).then_inc(tails_ready, 1)
        dve.wait_ge(more_summed, 1)
        v.tensor_scalar(more_i[:, :], bank[5][:, 0:len(SOMETIMES)], 0.5, None, ALU.is_gt).then_inc(more_known, 1)
        v.memset(head[:, 0:1], 1.0).then_inc(head_started, 1)
        v.tensor_tensor(head[:, 1:SLOTS], tgt[:, 1:SLOTS], tgt[:, 0:SLOTS - 1], ALU.not_equal).then_inc(vec, t.up())
        settle()
        dve.wait_ge(head_started, 1)
        v.tensor_scalar(reset[:, :], head[:, :], NONE, None, ALU.mult).then_inc(vec, t.up())
        settle()
        v.tensor_scalar(head[:, :], head[:, :], -1.0, 1.0, ALU.mult, ALU.add).then_inc(vec, t.up())
        def between_sweeps(n):
            if n in DSLOT_AT:
                h = DSLOT_AT.index(n)
                dve.wait_ge(weighted, h + 1)
                v.tensor_reduce(dslot[:, h], segd[:, h % 2].rearrange("p j l -> p l j"), AX.X, ALU.add) \
                    .then_inc(dslot_done, 1)

        compact(clamped, ccand, CH3, NCH3, TAKE3, between=between_sweeps, rounds=range(1, TAKE3 // 8))
        v.tensor_scalar(cidx, ccand, -1.0, None, ALU.add).then_inc(vec, t.up())
        settle()
        for digit, (op, by) in ((hi16, (ALU.arith_shift_right, 6)), (lo16, (ALU.bitwise_and, 63))):
            v.tensor_single_scalar(cdigit, cidx, by, op).then_inc(vec, t.up())
            settle()
            v.tensor_copy(digit, cdigit).then_inc(vec, t.up())
            settle()
        between_sweeps(DSLOT_AT[-1])
        dve.wait_ge(dslot_done, HEADS)

        def onehots(b):
            if b >= 2:
                dve.wait_ge(hist_used, b - 1)
            for h, val in enumerate((hi16, lo16)):
                for k in range(64):
                    ins = v.tensor_scalar(onehot[:, b % 2, h, k, :], val[:, OHC * b:OHC * (b + 1)], float(k), None,
                                          ALU.is_equal)
            ins.then_inc(onehots_ready, 1)

        def scan_part(n):
            a, b = PARTS[n], PARTS[n + 1]
            length = b - a
            first = 1 if n == 0 else 0
            dve.wait_ge(gathered[n], 16 * (min(b, SOMETIMES[0]) - a))
            if b == SLOTS:
                dve.wait_ge(last_gathered, 1)
            e_, c_ = wgt[:, :, a:b], carry[:, :, a:b]
            rmax = gath[:, :, HF + HEADS:ROW].rearrange("p l h -> p h l")
            v.tensor_tensor(e_, gath[:, a:b, HF:HF + HEADS].rearrange("p l h -> p h l"), dslot[:, :, a:b], ALU.add) \
                .then_inc(vec, t.up())
            settle()
            v.scalar_tensor_tensor(e_, e_, 0.2, e_, ALU.mult, ALU.max).then_inc(vec, t.up())
            settle()
            for h in range(HEADS):
                v.tensor_tensor_scan(rmax[:, h, a:b], reset[:, a:b], e_[:, h], NONE if n == 0 else rmax[:, h, a - 1:a],
                                     ALU.add, ALU.max).then_inc(vec, t.up())
            if n == 0:
                v.memset(carry[:, :, 0:1], 0.0).then_inc(vec, t.up())
            settle()
            v.tensor_tensor(carry[:, :, a + first:b], rmax[:, :, a + first - 1:b - 1], rmax[:, :, a + first:b], ALU.subtract) \
                .then_inc(vec, t.up())
            v.tensor_tensor(e_, e_, rmax[:, :, a:b], ALU.subtract).then_inc(vec, t.up())
            settle()
            v.tensor_scalar(c_, c_, 0.0, None, ALU.min).then_inc(exps_wanted, 1)
            dve.wait_ge(exps_done, 2 * n + 2)
            v.tensor_tensor(c_, c_, head[:, a:b].unsqueeze(1).to_broadcast([P, HEADS, length]), ALU.mult) \
                .then_inc(vec, t.up())
            msg = gath[:, a:b, 0:HF].rearrange("p l (h e) -> p l h e", h=HEADS)
            v.tensor_tensor(msg, msg, e_.rearrange("p h l -> p l h").unsqueeze(3).to_broadcast([P, length, HEADS, EXPERTS]),
                            ALU.mult).then_inc(vec, t.up())
            settle()
            for f in range(HF + HEADS):
                h = f // EXPERTS if f < HF else f - HF
                terms = gath[:, a:b, f] if f < HF else e_[:, h]
                v.tensor_tensor_scan(gath[:, a:b, f], c_[:, h], terms, 0.0 if n == 0 else gath[:, a - 1:a, f],
                                     ALU.mult, ALU.add).then_inc(vec, t.up())
            settle()
            v.engine_nop().then_inc(slots_ready, 1)

        for b in range(OHB):
            for n, at in enumerate(SCAN_BEFORE):
                if at == b:
                    scan_part(n)
            onehots(b)
        dve.wait_ge(hist_used, OHB)
        v.tensor_copy(histo[:, :], bank[4][0:64, 0:64]).then_inc(hist_copied, 1)
        dve.wait_ge(hist_copied, 1)
        v.tensor_reduce(nstat[0:64, 0, 0:1], histo[:, :], AX.X, ALU.add).then_inc(vec, t.up())
        settle()
        v.tensor_scalar(counts[0:64, 4:5], nstat[0:64, 0, 0:1], -1.0, None, ALU.mult).then_inc(missing_ready, 1)
        dve.wait_ge(missing_summed, 1)
        v.tensor_scalar(flag[:, :], bank[5][:, 0:1], -1.0 if force_general else 0.5, None, ALU.is_gt).then_inc(flag_ready, 1)

        def own_scores(count):
            a_dst = rows[:, :, HF + HEADS:ROW]
            v.tensor_tensor(fin[:, 1], rows[:, :, HF:HF + HEADS], a_dst, ALU.add).then_inc(count.sem, count.up())
            v.tensor_tensor(fin[:, 2], a_dst, last_row[:, HF:HF + HEADS].unsqueeze(1).to_broadcast([P, NC, HEADS]), ALU.add) \
                .then_inc(count.sem, count.up())
            v.tensor_scalar(nstat[:, 4], nclamp[:, :], 0.5, NONE, ALU.is_lt, ALU.mult).then_inc(count.sem, count.up())
            v.tensor_scalar(nstat[:, 5], present[:, :], -1.0, -NONE, ALU.add, ALU.mult).then_inc(count.sem, count.up())
            dve.wait_ge(count.sem, count.n)
            v.scalar_tensor_tensor(fin[:, 1:3], fin[:, 1:3], 0.2, fin[:, 1:3], ALU.mult, ALU.max).then_inc(count.sem, count.up())
            dve.wait_ge(count.sem, count.n)
            v.tensor_tensor(fin[:, 2], fin[:, 2], wide(nstat[:, 4], HEADS), ALU.add).then_inc(count.sem, count.up())
            dve.wait_ge(count.sem, count.n)
            v.tensor_tensor(fin[:, 3], fin[:, 1], fin[:, 2], ALU.max).then_inc(count.sem, count.up())
            dve.wait_ge(count.sem, count.n)

        dve.wait_ge(late_in, 16 * len(late_loads))
        v.tensor_scalar(gat_aff[:, 1], gat_aff[:, 1], 1.0 / HEADS, None, ALU.mult).then_inc(vec, t.up())
        v.tensor_reduce(beta_mean[:, :], gat_aff[:, 2].rearrange("p (h e) -> p e h", h=HEADS), AX.X, ALU.add) \
            .then_inc(vec, t.up())
        settle()
        v.tensor_scalar(beta_mean[:, :], beta_mean[:, :], 1.0 / HEADS, None, ALU.mult).then_inc(vec, t.up())
        dve.wait_ge(last_in, 16)
        dve.wait_ge(clamped_in, 16)
        own_scores(t)
        dve.wait_ge(tails_in, 16 * NC)
        with dve.If(dve.value_load(flag[0:1, 0:1], min_val=0, max_val=1) > 0):
            n0 = Tally(gen_steps)
            v.memset(agg_in[:, :, 0:HF + HEADS], 0.0).then_inc(gen_steps, n0.up())
            v.memset(present[:, :], 1.0).then_inc(gen_steps, n0.up())
            dve.wait_ge(gen_steps, n0.n)
            v.memset(agg_in[:, :, HF + HEADS:ROW], NONE).then_inc(gen_blank, 1)
            dve.wait_ge(gen_edges, 32)
            v.tensor_scalar(gen_plain, gen_src, float(LAST), None, ALU.min).then_inc(gen_steps, n0.up())
            dve.wait_ge(gen_steps, n0.n)
            v.scalar_tensor_tensor(gen_keys, gen_dst, float(NODES), gen_plain, ALU.mult, ALU.add) \
                .then_inc(gen_steps, n0.up())
            dve.wait_ge(gen_steps, n0.n)
            v.tensor_scalar(gen_plain, gen_dst, float(NODES), None, ALU.is_lt).then_inc(gen_steps, n0.up())
            dve.wait_ge(gen_steps, n0.n)
            v.memset(nclamp[:, :], 0.0).then_inc(gen_steps, n0.up())
            v.scalar_tensor_tensor(gen_keys, gen_keys, 1.0, gen_plain, ALU.add, ALU.mult).then_inc(gen_steps, n0.up())
            dve.wait_ge(gen_steps, n0.n)
            dve.wait_ge(gen_mask, 1)
            base, per_step = n0.n, 22
            with dve.Fori(0, EC) as step:
                k = Tally(gen_steps)

                def settled():
                    dve.wait_ge(gen_steps, step * per_step + (base + k.n))

                v.tensor_copy(key1, gen_keys[:, bass.ds(step, 1)]).then_inc(gen_steps, k.up())
                settled()
                v.tensor_scalar(gi[:, 0:1], key1, -1.0, None, ALU.add).then_inc(gen_steps, k.up())
                v.tensor_scalar(valid1, key1, 0.0, None, ALU.is_gt).then_inc(gen_steps, k.up())
                settled()
                v.tensor_single_scalar(gi[:, 1:2], gi[:, 0:1], NODES - 1, ALU.bitwise_and).then_inc(gen_steps, k.up())
                v.tensor_scalar(gi[:, 2:3], gi[:, 0:1], 12, NODES - 1, ALU.arith_shift_right, ALU.bitwise_and) \
                    .then_inc(gen_steps, k.up())
                settled()
                v.scalar_tensor_tensor(dst1, gi[:, 2:3], 1.0, valid1, ALU.add, ALU.mult).then_inc(gen_steps, k.up())
                settled()
                v.tensor_scalar(dst1, dst1, -1.0, None, ALU.add).then_inc(gen_idx, 1)
                for n in range(3):
                    dve.wait_ge(gen_in[n], 16 * step + 16)
                v.tensor_tensor(escore, src_row[:, HF:HF + HEADS], dst_row[:, HF + HEADS:ROW], ALU.add) \
                    .then_inc(gen_steps, k.up())
                settled()
                v.scalar_tensor_tensor(escore, escore, 0.2, escore, ALU.mult, ALU.max).then_inc(gen_score, 1)
                dve.wait_ge(gen_same, step + 1)
                v.tensor_scalar(same, bank[0][:, 0:P], dst1, None, ALU.is_equal).then_inc(gen_steps, k.up())
                settled()
                v.tensor_scalar(notsame, same, -1.0, -NONE, ALU.add, ALU.mult).then_inc(gen_steps, k.up())
                v.tensor_tensor(first_of, same, earlier, ALU.mult).then_inc(gen_steps, k.up())
                dve.wait_ge(gen_others, step + 1)
                v.tensor_tensor(others, v3(bank[1][:, :], P), same.unsqueeze(1).to_broadcast([P, HEADS, P]), ALU.mult) \
                    .then_inc(gen_steps, k.up())
                settled()
                v.tensor_tensor(others, others, notsame.unsqueeze(1).to_broadcast([P, HEADS, P]), ALU.add) \
                    .then_inc(gen_steps, k.up())
                v.tensor_reduce(rank1, first_of, AX.X, ALU.add).then_inc(gen_steps, k.up())
                settled()
                v.tensor_reduce(emax, others, AX.X, ALU.max).then_inc(gen_steps, k.up())
                settled()
                v.tensor_tensor(new_row[:, HF + HEADS:ROW], emax, old_row[:, HF + HEADS:ROW], ALU.max).then_inc(gen_steps, k.up())
                settled()
                v.tensor_tensor(expo[:, 0], escore, new_row[:, HF + HEADS:ROW], ALU.subtract).then_inc(gen_steps, k.up())
                v.tensor_tensor(expo[:, 1], old_row[:, HF + HEADS:ROW], new_row[:, HF + HEADS:ROW], ALU.subtract) \
                    .then_inc(gen_exp, 1)
                v.scalar_tensor_tensor(write1, rank1, 0.5, valid1, ALU.is_lt, ALU.mult).then_inc(gen_steps, k.up())
                dve.wait_ge(gen_exped, step + 1)
                settled()
                v.tensor_scalar(payload[:, HF:], expo[:, 0], valid1, None, ALU.mult).then_inc(gen_steps, k.up())
                v.tensor_scalar(write1, write1, -2.0 * NODES, 2.0 * NODES, ALU.mult, ALU.add).then_inc(gen_steps, k.up())
                settled()
                v.tensor_tensor(payload[:, 0:HF].rearrange("p (h e) -> p h e", h=HEADS),
                                src_row[:, 0:HF].rearrange("p (h e) -> p h e", h=HEADS), wide(payload[:, HF:], EXPERTS),
                                ALU.mult).then_inc(gen_payload, 1)
                v.tensor_tensor(gi[:, 3:4], write1, gi[:, 2:3], ALU.add).then_inc(gen_steps, k.up())
                v.tensor_tensor(old_row[:, HF:HF + HEADS], old_row[:, HF:HF + HEADS], expo[:, 1], ALU.mult) \
                    .then_inc(gen_steps, k.up())
                old = old_row[:, 0:HF].rearrange("p (h e) -> p h e", h=HEADS)
                v.tensor_tensor(old, old, wide(expo[:, 1], EXPERTS), ALU.mult).then_inc(gen_steps, k.up())
                settled()
                dve.wait_ge(gen_summed, step + 1)
                v.tensor_tensor(new_row[:, 0:HF + HEADS], old_row[:, 0:HF + HEADS], bank[2][:, 0:HF + HEADS], ALU.add) \
                    .then_inc(gen_row, 1)
                dve.wait_ge(gen_written, 16 * step + 16)
                assert k.n == per_step, k.n
            dve.wait_ge(gen_back, 16)
            own_scores(Tally(gen_scores))
        v.tensor_tensor(fin[:, 0], agg_in[:, :, HF + HEADS:ROW], wide(present[:, :], HEADS), ALU.mult).then_inc(vec, t.up())
        settle()
        v.tensor_tensor(fin[:, 0], fin[:, 0], wide(nstat[:, 5], HEADS), ALU.add).then_inc(vec, t.up())
        settle()
        v.tensor_tensor(fin[:, 3], fin[:, 3], fin[:, 0], ALU.max).then_inc(vec, t.up())
        settle()
        v.tensor_tensor(fin[:, 0:3], fin[:, 0:3], fin[:, 3].unsqueeze(1).to_broadcast([P, 3, NC, HEADS]), ALU.subtract) \
            .then_inc(fin_wanted, 1)
        dve.wait_ge(fin_done, 1)
        v.tensor_tensor(fin[:, 2], fin[:, 2], wide(nclamp[:, :], HEADS), ALU.mult).then_inc(vec, t.up())
        v.tensor_tensor(fin[:, 4], agg_in[:, :, HF:HF + HEADS], fin[:, 0], ALU.mult).then_inc(vec, t.up())
        settle()
        v.tensor_tensor(fin[:, 5], fin[:, 1], fin[:, 2], ALU.add).then_inc(vec, t.up())
        settle()
        v.scalar_tensor_tensor(fin[:, 5], fin[:, 5], 1e-16, fin[:, 4], ALU.add, ALU.add).then_inc(vec, t.up())
        settle()
        v.reciprocal(fin[:, 6], fin[:, 5]).then_inc(vec, t.up())
        settle()
        v.tensor_tensor(fin[:, 0:3], fin[:, 0:3], fin[:, 6].unsqueeze(1).to_broadcast([P, 3, NC, HEADS]), ALU.mult) \
            .then_inc(vec, t.up())
        settle()

        def heads(ap):
            return ap.rearrange("p j (h e) -> p j h e", h=HEADS)

        def per_head(n):
            return fin[:, n].unsqueeze(3).to_broadcast([P, NC, HEADS, EXPERTS])

        msg_in = agg_in[:, :, 0:HF]
        v.tensor_tensor(heads(msg_in), heads(msg_in), per_head(0), ALU.mult).then_inc(vec, t.up())
        v.tensor_tensor(heads(hatt[:, 0]), heads(rows[:, :, 0:HF]), per_head(1), ALU.mult).then_inc(vec, t.up())
        v.tensor_tensor(heads(hatt[:, 1]), heads(last_row[:, 0:HF].unsqueeze(1).to_broadcast([P, NC, HF])), per_head(2),
                        ALU.mult).then_inc(vec, t.up())
        settle()
        agg = hatt[:, 0]

        def every_token(n):
            return gat_aff[:, n, :].unsqueeze(1).to_broadcast([P, NC, HF])

        for term in (msg_in, hatt[:, 1], every_token(0)):
            v.tensor_tensor(agg, agg, term, ALU.add).then_inc(vec, t.up())
            settle()
        v.tensor_reduce(nstat[:, 0], agg, AX.X, ALU.add).then_inc(vec, t.up())
        settle()
        v.scalar_tensor_tensor(agg, wide(nstat[:, 0], HF), -1.0 / HF, agg, ALU.mult, ALU.add).then_inc(vec, t.up())
        settle()
        v.tensor_tensor(hatt[:, 1], agg, agg, ALU.mult).then_inc(vec, t.up())
        settle()
        v.tensor_reduce(nstat[:, 1], hatt[:, 1], AX.X, ALU.add).then_inc(fin_wanted, 1)
        v.tensor_tensor(msg_in, agg, every_token(1), ALU.mult).then_inc(vec, t.up())
        settle()
        v.tensor_reduce(fin[:, 1], msg_in.rearrange("p j (h e) -> p j e h", h=HEADS), AX.X, ALU.add).then_inc(vec, t.up())
        dve.wait_ge(fin_done, 2)
        v.reciprocal(nstat[:, 3], nstat[:, 2]).then_inc(vec, t.up())
        settle()
        score, top, gate, sel = fin[:, 2], nstat[:, 0], fin[:, 3], fin[:, 5]
        v.tensor_tensor(score, fin[:, 1], wide(nstat[:, 3], EXPERTS), ALU.mult).then_inc(vec, t.up())
        settle()
        v.tensor_tensor(score, score, beta_mean[:, :].unsqueeze(1).to_broadcast([P, NC, EXPERTS]), ALU.add) \
            .then_inc(vec, t.up())
        settle()
        mine = score.unsqueeze(3).to_broadcast([P, NC, EXPERTS, EXPERTS])
        other = score.unsqueeze(2).to_broadcast([P, NC, EXPERTS, EXPERTS])
        larger, equal = heads(hatt[:, 0]), heads(hatt[:, 1])
        v.tensor_tensor(larger, other, mine, ALU.is_gt).then_inc(vec, t.up())
        v.tensor_tensor(equal, other, mine, ALU.is_equal).then_inc(vec, t.up())
        v.tensor_reduce(top, score, AX.X, ALU.max).then_inc(vec, t.up())
        settle()
        v.tensor_tensor(equal, equal, before[:, :, :].unsqueeze(1).to_broadcast([P, NC, EXPERTS, EXPERTS]), ALU.mult) \
            .then_inc(vec, t.up())
        v.tensor_tensor(gate, score, wide(top, EXPERTS), ALU.subtract).then_inc(fin_wanted, 1)
        settle()
        v.tensor_tensor(larger, larger, equal, ALU.add).then_inc(vec, t.up())
        settle()
        v.tensor_reduce(fin[:, 4], larger, AX.X, ALU.add).then_inc(vec, t.up())
        settle()
        v.tensor_scalar(sel, fin[:, 4], 1.5, None, ALU.is_lt).then_inc(vec, t.up())
        settle()
        dve.wait_ge(fin_done, 3)
        v.tensor_tensor(gate, gate, sel, ALU.mult).then_inc(vec, t.up())
        settle()
        v.tensor_reduce(nstat[:, 1], gate, AX.X, ALU.add).then_inc(vec, t.up())
        settle()
        v.reciprocal(nstat[:, 3], nstat[:, 1]).then_inc(vec, t.up())
        settle()
        v.tensor_tensor(gate, gate, wide(nstat[:, 3], EXPERTS), ALU.mult).then_inc(gate_ready, 1)
        dve.wait_ge(y_copied, 32)
        dve.wait_ge(gate_ready, 1)
        for a, b in zip(OUT_PARTS, OUT_PARTS[1:-1]):
            js = slice(a, b)
            for e in range(EXPERTS):
                v.tensor_tensor(yexp[:, e, js, :], yexp[:, e, js, :], wide(gate[:, js, e], E), ALU.mult) \
                    .then_inc(vec, t.up())
            for e in range(EXPERTS):
                dve.wait_ge(vec, t.n - (3 if e == 0 else 0))
                v.tensor_tensor(xin[:, js, :], xin[:, js, :], yexp[:, e, js, :], ALU.add) \
                    .then_inc(*((out_ready, 1) if e == 3 else (vec, t.up())))

    ctx.close()


NAMES = ["x", "L0_conv_protein_pair", "L0_conv_compound_pair", "L0_conv_z_mask", "L0_conv_ln_w", "L0_conv_ln_b",
         "L0_conv_lnc_w", "L0_conv_lnc_b", "L0_conv_g1_w", "L0_conv_g1_b", "L0_conv_g2_w", "L0_conv_g2_b",
         "L0_conv_l1_w", "L0_conv_l1_b", "L0_conv_l2_w", "L0_conv_l2_b", "L0_conv_eg_w", "L0_conv_eg_b",
         "L0_conv_las_w", "L0_conv_las_b", "L0_ffn_W_gat", "L0_ffn_att_src", "L0_ffn_att_dst", "L0_ffn_b_gat",
         "L0_ffn_ln_gamma", "L0_ffn_ln_beta", "L0_ffn_W1", "L0_ffn_b1", "L0_ffn_W2", "L0_ffn_b2",
         "L0_ffn_edge_index"]


def program(nc, shapes, **options):
    args = [nc.dram_tensor(f"in_{n}", s, d, kind="ExternalInput").ap() for n, (s, d) in zip(NAMES, shapes)]
    out = nc.dram_tensor("out_0", (1, P, NC, E), F32, kind="ExternalOutput").ap()
    build(nc, *args, out, **options)


def kernel(**inputs):
    import concourse.bacc as bacc
    import numpy as np
    from concourse.bass_utils import run_bass_kernel_spmd

    nc = bacc.Bacc("TRN2", target_bir_lowering=False, num_devices=1)
    arrays = {f"in_{n}": np.ascontiguousarray(inputs[n]) for n in NAMES}
    program(nc, [(a.shape, mybir.dt.from_np(a.dtype)) for a in arrays.values()])
    r = run_bass_kernel_spmd(nc, [arrays], core_ids=[0])
    return r.results[0]["out_0"]
```
